# Optimizing a Trainium2 kernel written in Bass

```python
import numpy as np
import jax
import jax.numpy as jnp

def _softmax(x, axis=-1):
    return jax.nn.softmax(x, axis=axis)

def _gelu(x):
    return jax.nn.gelu(x, approximate=True)

def _silu(x):
    return jax.nn.silu(x)

def _sigmoid(x):
    return jax.nn.sigmoid(x)

def _layernorm(x, axis=-1, eps=1e-05):
    m = jnp.mean(x, axis=axis, keepdims=True)
    v = jnp.var(x, axis=axis, keepdims=True)
    return (x - m) / jnp.sqrt(v + eps)

def _scatter_add(tgt, idx, src, axis=0):
    return tgt.at[idx].add(src)

def _segment_sum(src, seg, n):
    return jax.ops.segment_sum(src, seg, n)
kernel_name = 'mk_decoder_postln_d2_seqx_r8_886dbe'

def setup_inputs(seed: int=0):
    np.random.seed(seed)
    _w = jnp.asarray

    def _rec_inputs():
        import jax
        import jax.numpy as jnp
        _rk = jax.random.key(seed)
        x = -0.0002928 + 1 * jax.random.normal(jax.random.fold_in(_rk, 1), (32, 128, 128), jnp.float32)
        _lenS = 128 - jax.random.randint(jax.random.fold_in(_rk, 7), (32,), 0, max(1, 128 // 4) + 1, jnp.int32)
        _lenS2 = 128 - jax.random.randint(jax.random.fold_in(_rk, 8), (32,), 0, max(1, 128 // 4) + 1, jnp.int32)
        _ctx_1024P = jax.random.normal(jax.random.fold_in(_rk, 11), (32, 16, 128), jnp.float32)
        _ctx_1024c = jax.random.dirichlet(jax.random.fold_in(_rk, 511), 0.3 * jnp.ones((16,), jnp.float32), (32, 128))
        _ctx_1024t = jnp.einsum('bsk,bkd->bsd', _ctx_1024c, _ctx_1024P)
        _ctx_1024t = _ctx_1024t * jax.lax.rsqrt(jnp.mean(jnp.square(_ctx_1024t)) + 1e-12) * 0.953939
        ctx_1024 = 4.13588e-05 + 0.999923 * (_ctx_1024t + 0.3 * jax.random.normal(jax.random.fold_in(_rk, 611), (32, 128, 128), jnp.float32))
        _validS = jnp.arange(128)[None, :] < _lenS[:, None]
        _validS2 = jnp.arange(128)[None, :] < _lenS2[:, None]
        _causal = jnp.tril(jnp.ones((128, 128), dtype=bool))
        mask_BxSxS2_bf0 = jnp.logical_not(jnp.ones((32, 128, 128), dtype=bool))
        return (x, ctx_1024, mask_BxSxS2_bf0)
    x, ctx_1024, mask_BxSxS2_bf0 = _rec_inputs()

    def _L0_attn_setup():
        import jax, jax.numpy as jnp
        import numpy as np
        import math
        B, S, E = (2, 256, 128)
        H, DK, DV = (16, 64, 64)

        def _rope(q, k):
            D = q.shape[-1]
            theta = 10000.0 ** (jnp.arange(0, D, 2, dtype=jnp.float32) / D)
            pos = jnp.arange(q.shape[-2], dtype=jnp.float32)
            freqs = pos[:, None] * (1.0 / theta)[None, :]
            emb = jnp.concatenate([freqs, freqs], axis=-1)
            cos = jnp.cos(emb)[None, None]
            sin = jnp.sin(emb)[None, None]

            def rotate(x):
                x1 = x[..., ::2]
                x2 = x[..., 1::2]
                return jnp.stack([-x2, x1], axis=-1).reshape(x.shape)
            return (q * cos + rotate(q) * sin, k * cos + rotate(k) * sin)
        key = jax.random.key(seed)
        ks = jax.random.split(key, 9)
        sE = 1.0 / math.sqrt(E)
        sV = 1.0 / math.sqrt(H * DV)
        return {'x': jax.random.normal(ks[0], (B, S, E), dtype=jnp.float32), 'wq': jax.random.uniform(ks[1], (H * DK, E), jnp.float32, -sE, sE), 'bq': jax.random.uniform(ks[2], (H * DK,), jnp.float32, -sE, sE), 'wk': jax.random.uniform(ks[3], (H * DK, E), jnp.float32, -sE, sE), 'bk': jax.random.uniform(ks[4], (H * DK,), jnp.float32, -sE, sE), 'wv': jax.random.uniform(ks[5], (H * DV, E), jnp.float32, -sE, sE), 'bv': jax.random.uniform(ks[6], (H * DV,), jnp.float32, -sE, sE), 'wo': jax.random.uniform(ks[7], (E, H * DV), jnp.float32, -sV, sV), 'bo': jax.random.uniform(ks[8], (E,), jnp.float32, -sV, sV)}
    _L0_attn_all = _L0_attn_setup()
    _L0_attn_in = {k: v for k, v in _L0_attn_all.items() if k in ('wq', 'bq', 'wk', 'bk', 'wv', 'bv', 'wo', 'bo')}
    del _L0_attn_all

    def _L0_xattn_setup():
        import jax, jax.numpy as jnp
        import numpy as np
        HIDDEN = 128
        HEADS = 16
        D_K = HIDDEN // HEADS
        B, LQ, LKV = (4, 128, 256)
        NEG_INF = -1e+18
        key = jax.random.key(seed)
        ks = jax.random.split(key, 12)
        s = 1.0 / np.sqrt(HIDDEN)
        return {'tgt': jax.random.normal(ks[0], (B, LQ, HIDDEN), jnp.float32), 'memory': jax.random.normal(ks[1], (B, LKV, HIDDEN), jnp.float32), 'mask': jnp.zeros((B, LQ, LKV), dtype=bool), 'Wq': jax.random.normal(ks[2], (HIDDEN, HIDDEN), jnp.float32) * s, 'bq': jnp.zeros((HIDDEN,), jnp.float32), 'Wk': jax.random.normal(ks[3], (HIDDEN, HIDDEN), jnp.float32) * s, 'bk': jnp.zeros((HIDDEN,), jnp.float32), 'Wv': jax.random.normal(ks[4], (HIDDEN, HIDDEN), jnp.float32) * s, 'bv': jnp.zeros((HIDDEN,), jnp.float32), 'Wo': jax.random.normal(ks[5], (HIDDEN, HIDDEN), jnp.float32) * s, 'bo': jnp.zeros((HIDDEN,), jnp.float32)}
    _L0_xattn_all = _L0_xattn_setup()
    _L0_xattn_in = {k: v for k, v in _L0_xattn_all.items() if k in ('Wq', 'bq', 'Wk', 'bk', 'Wv', 'bv', 'Wo', 'bo')}
    del _L0_xattn_all

    def _L0_ffn_setup():
        import jax, jax.numpy as jnp
        import numpy as np
        B, S, H, F, E, K = (4, 512, 128, 512, 8, 2)
        LN_EPS = 1e-05
        key = jax.random.key(seed)
        kx, kr, k1, k2 = jax.random.split(key, 4)
        x = jax.random.normal(kx, (B, S, H), dtype=jnp.float32)
        gamma = jnp.ones((H,), jnp.float32)
        beta = jnp.zeros((H,), jnp.float32)
        Wr = jax.random.normal(kr, (H, E), jnp.float32) * 0.02
        br = jnp.zeros((E,), jnp.float32)
        W1 = jax.random.normal(k1, (E, H, F), jnp.float32) * (1.0 / np.sqrt(H))
        b1 = jnp.zeros((E, F), jnp.float32)
        W2 = jax.random.normal(k2, (E, F, H), jnp.float32) * (1.0 / np.sqrt(F))
        b2 = jnp.zeros((E, H), jnp.float32)
        return {'x': x, 'gamma': gamma, 'beta': beta, 'Wr': Wr, 'br': br, 'W1': W1, 'b1': b1, 'W2': W2, 'b2': b2}
    _L0_ffn_all = _L0_ffn_setup()
    _L0_ffn_in = {k: v for k, v in _L0_ffn_all.items() if k in ('gamma', 'beta', 'Wr', 'br', 'W1', 'b1', 'W2', 'b2')}
    del _L0_ffn_all

    def _L1_attn_setup():
        import jax, jax.numpy as jnp
        import numpy as np
        DIM = 128
        SQRT_DIM = float(np.sqrt(DIM))
        key = jax.random.key(seed)
        inputs = jax.random.normal(key, (512, 4, DIM), dtype=jnp.float32)
        return {'inputs': inputs}
    _L1_attn_all = _L1_attn_setup()
    _L1_attn_in = {k: v for k, v in _L1_attn_all.items() if k in ()}
    del _L1_attn_all

    def _L1_xattn_setup():
        import jax, jax.numpy as jnp
        import numpy as np
        D_MODEL = 128
        NUM_HEADS = 16
        D_K = D_MODEL // NUM_HEADS
        key = jax.random.key(seed)
        ks = jax.random.split(key, 11)
        B, S = (2, 256)
        scale = 1.0 / np.sqrt(D_MODEL)
        inp = {'q': jax.random.normal(ks[0], (B, S, D_MODEL), jnp.float32), 'k': jax.random.normal(ks[1], (B, S, D_MODEL), jnp.float32), 'v': jax.random.normal(ks[2], (B, S, D_MODEL), jnp.float32), 'wq': jax.random.normal(ks[3], (D_MODEL, D_MODEL), jnp.float32) * scale, 'bq': jax.random.normal(ks[4], (D_MODEL,), jnp.float32) * 0.01, 'wk': jax.random.normal(ks[5], (D_MODEL, D_MODEL), jnp.float32) * scale, 'bk': jax.random.normal(ks[6], (D_MODEL,), jnp.float32) * 0.01, 'wv': jax.random.normal(ks[7], (D_MODEL, D_MODEL), jnp.float32) * scale, 'bv': jax.random.normal(ks[8], (D_MODEL,), jnp.float32) * 0.01, 'wo': jax.random.normal(ks[9], (D_MODEL, D_MODEL), jnp.float32) * scale, 'bo': jax.random.normal(ks[10], (D_MODEL,), jnp.float32) * 0.01}
        return inp
    _L1_xattn_all = _L1_xattn_setup()
    _L1_xattn_in = {k: v for k, v in _L1_xattn_all.items() if k in ('wq', 'bq', 'wk', 'bk', 'wv', 'bv', 'wo', 'bo')}
    del _L1_xattn_all

    def _L1_ffn_setup():
        import jax, jax.numpy as jnp
        import numpy as np
        B, S, D, H, E = (8, 256, 128, 512, 16)
        key = jax.random.key(seed)
        ks = jax.random.split(key, 4)
        sd = 1.0 / np.sqrt(D).astype(np.float32)
        sh = 1.0 / np.sqrt(H).astype(np.float32)
        return {'x': jax.random.normal(ks[0], (B, S, D), jnp.float32), 'Wg': jax.random.normal(ks[1], (D, E), jnp.float32) * sd, 'bg': jnp.zeros((E,), jnp.float32), 'W1': jax.random.normal(ks[2], (E, D, H), jnp.float32) * sd, 'b1': jnp.zeros((E, H), jnp.float32), 'W2': jax.random.normal(ks[3], (E, H, D), jnp.float32) * sh, 'b2': jnp.zeros((E, D), jnp.float32)}
    _L1_ffn_all = _L1_ffn_setup()
    _L1_ffn_in = {k: v for k, v in _L1_ffn_all.items() if k in ('Wg', 'bg', 'W1', 'b1', 'W2', 'b2')}
    del _L1_ffn_all
    return {'x': x, 'ctx_1024': ctx_1024, 'mask_BxSxS2_bf0': mask_BxSxS2_bf0, 'L0_attn_wq': _L0_attn_in['wq'], 'L0_attn_bq': _L0_attn_in['bq'], 'L0_attn_wk': _L0_attn_in['wk'], 'L0_attn_bk': _L0_attn_in['bk'], 'L0_attn_wv': _L0_attn_in['wv'], 'L0_attn_bv': _L0_attn_in['bv'], 'L0_attn_wo': _L0_attn_in['wo'], 'L0_attn_bo': _L0_attn_in['bo'], 'L0_xattn_Wq': _L0_xattn_in['Wq'], 'L0_xattn_bq': _L0_xattn_in['bq'], 'L0_xattn_Wk': _L0_xattn_in['Wk'], 'L0_xattn_bk': _L0_xattn_in['bk'], 'L0_xattn_Wv': _L0_xattn_in['Wv'], 'L0_xattn_bv': _L0_xattn_in['bv'], 'L0_xattn_Wo': _L0_xattn_in['Wo'], 'L0_xattn_bo': _L0_xattn_in['bo'], 'L0_ffn_gamma': _L0_ffn_in['gamma'], 'L0_ffn_beta': _L0_ffn_in['beta'], 'L0_ffn_Wr': _L0_ffn_in['Wr'], 'L0_ffn_br': _L0_ffn_in['br'], 'L0_ffn_W1': _L0_ffn_in['W1'], 'L0_ffn_b1': _L0_ffn_in['b1'], 'L0_ffn_W2': _L0_ffn_in['W2'], 'L0_ffn_b2': _L0_ffn_in['b2'], 'L1_xattn_wq': _L1_xattn_in['wq'], 'L1_xattn_bq': _L1_xattn_in['bq'], 'L1_xattn_wk': _L1_xattn_in['wk'], 'L1_xattn_bk': _L1_xattn_in['bk'], 'L1_xattn_wv': _L1_xattn_in['wv'], 'L1_xattn_bv': _L1_xattn_in['bv'], 'L1_xattn_wo': _L1_xattn_in['wo'], 'L1_xattn_bo': _L1_xattn_in['bo'], 'L1_ffn_Wg': _L1_ffn_in['Wg'], 'L1_ffn_bg': _L1_ffn_in['bg'], 'L1_ffn_W1': _L1_ffn_in['W1'], 'L1_ffn_b1': _L1_ffn_in['b1'], 'L1_ffn_W2': _L1_ffn_in['W2'], 'L1_ffn_b2': _L1_ffn_in['b2']}

def reference(x, ctx_1024, mask_BxSxS2_bf0, L0_attn_wq, L0_attn_bq, L0_attn_wk, L0_attn_bk, L0_attn_wv, L0_attn_bv, L0_attn_wo, L0_attn_bo, L0_xattn_Wq, L0_xattn_bq, L0_xattn_Wk, L0_xattn_bk, L0_xattn_Wv, L0_xattn_bv, L0_xattn_Wo, L0_xattn_bo, L0_ffn_gamma, L0_ffn_beta, L0_ffn_Wr, L0_ffn_br, L0_ffn_W1, L0_ffn_b1, L0_ffn_W2, L0_ffn_b2, L1_xattn_wq, L1_xattn_bq, L1_xattn_wk, L1_xattn_bk, L1_xattn_wv, L1_xattn_bv, L1_xattn_wo, L1_xattn_bo, L1_ffn_Wg, L1_ffn_bg, L1_ffn_W1, L1_ffn_b1, L1_ffn_W2, L1_ffn_b2):
    import jax
    import jax.numpy as jnp

    def _L0_attn_ref(x, wq, bq, wk, bk, wv, bv, wo, bo):
        import jax, jax.numpy as jnp
        import numpy as np
        import math
        B, S, E = (2, 256, 128)
        H, DK, DV = (16, 64, 64)

        def _rope(q, k):
            D = q.shape[-1]
            theta = 10000.0 ** (jnp.arange(0, D, 2, dtype=jnp.float32) / D)
            pos = jnp.arange(q.shape[-2], dtype=jnp.float32)
            freqs = pos[:, None] * (1.0 / theta)[None, :]
            emb = jnp.concatenate([freqs, freqs], axis=-1)
            cos = jnp.cos(emb)[None, None]
            sin = jnp.sin(emb)[None, None]

            def rotate(x):
                x1 = x[..., ::2]
                x2 = x[..., 1::2]
                return jnp.stack([-x2, x1], axis=-1).reshape(x.shape)
            return (q * cos + rotate(q) * sin, k * cos + rotate(k) * sin)
        Bx, Sx, Ex = x.shape
        q = (x @ wq.T + bq).reshape(Bx, Sx, H, DK).transpose(0, 2, 1, 3)
        k = (x @ wk.T + bk).reshape(Bx, Sx, H, DK).transpose(0, 2, 1, 3)
        v = (x @ wv.T + bv).reshape(Bx, Sx, H, DV).transpose(0, 2, 1, 3)
        q, k = _rope(q, k)
        scores = jnp.einsum('bhqd,bhkd->bhqk', q, k)
        causal = jnp.triu(jnp.ones((Sx, Sx), dtype=bool), k=1)
        scores = jnp.where(causal[None, None], -jnp.inf, scores)
        attn = jax.nn.softmax(scores / math.sqrt(DK), axis=-1)
        out = jnp.einsum('bhqk,bhkd->bhqd', attn, v)
        out = out.transpose(0, 2, 1, 3).reshape(Bx, Sx, H * DV)
        return out @ wo.T + bo

    def _L0_xattn_ref(tgt, memory, mask, Wq, bq, Wk, bk, Wv, bv, Wo, bo):
        import jax, jax.numpy as jnp
        import numpy as np
        HIDDEN = 128
        HEADS = 16
        D_K = HIDDEN // HEADS
        B, LQ, LKV = (4, 128, 256)
        NEG_INF = -1e+18
        b = tgt.shape[0]

        def heads(x):
            return x.reshape(b, -1, HEADS, D_K).transpose(0, 2, 1, 3)
        q = heads(tgt @ Wq + bq) / jnp.sqrt(jnp.asarray(D_K, tgt.dtype))
        k = heads(memory @ Wk + bk)
        v = heads(memory @ Wv + bv)
        scores = jnp.einsum('bhqd,bhkd->bhqk', q, k)
        scores = jnp.where(mask[:, None, :, :], NEG_INF, scores)
        attn = jax.nn.softmax(scores, axis=-1)
        ctx = jnp.einsum('bhqk,bhkd->bhqd', attn, v)
        ctx = ctx.transpose(0, 2, 1, 3).reshape(b, -1, HIDDEN)
        return ctx @ Wo + bo

    def _L0_ffn_ref(x, gamma, beta, Wr, br, W1, b1, W2, b2):
        import jax, jax.numpy as jnp
        import numpy as np
        B, S, H, F, E, K = (4, 512, 128, 512, 8, 2)
        LN_EPS = 1e-05
        residual = x
        mu = jnp.mean(x, axis=-1, keepdims=True)
        var = jnp.var(x, axis=-1, keepdims=True)
        xn = (x - mu) * jax.lax.rsqrt(var + LN_EPS) * gamma + beta
        probs = jax.nn.softmax(xn @ Wr + br, axis=-1)
        scores, idx = jax.lax.top_k(probs, K)

        def expert_fn(w):
            W1_e, b1_e, W2_e, b2_e = w
            return jax.nn.relu(xn @ W1_e + b1_e) @ W2_e + b2_e
        full = jax.lax.map(expert_fn, (W1, b1, W2, b2))
        full = jnp.moveaxis(full, 0, 2)
        c = jnp.einsum('ef,efh->eh', jax.nn.relu(b1), W2) + b2
        c_total = c.sum(axis=0)
        sel_full = jnp.take_along_axis(full, idx[..., None], axis=2)
        c_sel = c[idx]
        output = jnp.sum(scores[..., None] * (sel_full - c_sel + c_total), axis=2)
        return residual + output

    def _L1_attn_ref(inputs):
        import jax, jax.numpy as jnp
        import numpy as np
        DIM = 128
        SQRT_DIM = float(np.sqrt(DIM))
        x = jnp.transpose(inputs, (1, 0, 2))
        scores = jnp.einsum('bsd,btd->bst', x, x) / SQRT_DIM
        attn = jax.nn.softmax(scores, axis=-1)
        out = jnp.einsum('bst,btd->bsd', attn, x)
        return jnp.transpose(out, (1, 0, 2))

    def _L1_xattn_ref(q, k, v, wq, bq, wk, bk, wv, bv, wo, bo):
        import jax, jax.numpy as jnp
        import numpy as np
        D_MODEL = 128
        NUM_HEADS = 16
        D_K = D_MODEL // NUM_HEADS
        B, S, _ = q.shape
        qh = (q @ wq.T + bq).reshape(B, S, NUM_HEADS, D_K).transpose(0, 2, 1, 3)
        kh = (k @ wk.T + bk).reshape(B, S, NUM_HEADS, D_K).transpose(0, 2, 1, 3)
        vh = (v @ wv.T + bv).reshape(B, S, NUM_HEADS, D_K).transpose(0, 2, 1, 3)
        scores = jnp.einsum('bhqd,bhkd->bhqk', qh, kh) / jnp.sqrt(jnp.asarray(D_K, qh.dtype))
        weights = jax.nn.softmax(scores, axis=-1)
        attn = jnp.einsum('bhqk,bhkd->bhqd', weights, vh)
        attn = attn.transpose(0, 2, 1, 3).reshape(B, S, D_MODEL)
        return attn @ wo.T + bo

    def _L1_ffn_ref(x, Wg, bg, W1, b1, W2, b2):
        import jax, jax.numpy as jnp
        import numpy as np
        B, S, D, H, E = (8, 256, 128, 512, 16)
        d = x.shape[-1]
        xf = x.reshape(-1, d)
        n_tok = xf.shape[0]
        n_exp = Wg.shape[1]
        cap = -(-n_tok // n_exp)
        score = jax.nn.softmax(xf @ Wg + bg, axis=-1)
        gate = jnp.max(score, axis=-1)
        idx = jnp.argmax(score, axis=-1)
        onehot = jax.nn.one_hot(idx, n_exp, dtype=jnp.int32)
        pos = jnp.sum((jnp.cumsum(onehot, axis=0) - 1) * onehot, axis=-1)
        keep = pos < cap
        safe_pos = jnp.where(keep, pos, cap - 1)
        buf = jnp.zeros((n_exp, cap, d), x.dtype).at[idx, safe_pos].add(jnp.where(keep[:, None], xf, 0.0))
        h = jax.nn.relu(jnp.einsum('ecd,edh->ech', buf, W1) + b1[:, None, :])
        y = jnp.einsum('ech,ehd->ecd', h, W2) + b2[:, None, :]
        out = y[idx, safe_pos] * gate[:, None]
        out = jnp.where(keep[:, None], out, 0.0)
        return out.reshape(x.shape)
    x = _layernorm(x + _L0_attn_ref(x, L0_attn_wq, L0_attn_bq, L0_attn_wk, L0_attn_bk, L0_attn_wv, L0_attn_bv, L0_attn_wo, L0_attn_bo), axis=-1)
    x = _layernorm(x + _L0_xattn_ref(x, ctx_1024, mask_BxSxS2_bf0, L0_xattn_Wq, L0_xattn_bq, L0_xattn_Wk, L0_xattn_bk, L0_xattn_Wv, L0_xattn_bv, L0_xattn_Wo, L0_xattn_bo), axis=-1)
    x = _layernorm(x + _L0_ffn_ref(x, L0_ffn_gamma, L0_ffn_beta, L0_ffn_Wr, L0_ffn_br, L0_ffn_W1, L0_ffn_b1, L0_ffn_W2, L0_ffn_b2), axis=-1)
    x = _layernorm(x + _L1_attn_ref(x), axis=-1)
    x = _layernorm(x + _L1_xattn_ref(x, ctx_1024, ctx_1024, L1_xattn_wq, L1_xattn_bq, L1_xattn_wk, L1_xattn_bk, L1_xattn_wv, L1_xattn_bv, L1_xattn_wo, L1_xattn_bo), axis=-1)
    x = _layernorm(x + _L1_ffn_ref(x, L1_ffn_Wg, L1_ffn_bg, L1_ffn_W1, L1_ffn_b1, L1_ffn_W2, L1_ffn_b2), axis=-1)
    return x

_drawn_inputs = setup_inputs


def setup_inputs(seed=0):
    import zlib

    import numpy as np

    out = dict(_drawn_inputs(seed))
    spreads = {'L0_xattn_bq': (0.0, 0.1),
     'L0_xattn_bk': (0.0, 2.0),
     'L0_xattn_bv': (0.0, 0.1),
     'L0_xattn_bo': (0.0, 0.1),
     'L0_ffn_gamma': (1.0, 0.2),
     'L0_ffn_beta': (0.0, 0.1),
     'L0_ffn_br': (0.0, 0.1),
     'L0_ffn_b1': (0.0, 0.1),
     'L0_ffn_b2': (0.0, 0.1),
     'L1_ffn_bg': (0.0, 0.1),
     'L1_ffn_b1': (0.0, 0.48),
     'L1_ffn_b2': (0.0, 0.335)}
    factors = {'L0_attn_bq': 7.297,
     'L0_attn_bk': 23.575,
     'L1_xattn_bq': 6.129,
     'L1_xattn_bk': 64.0,
     'L1_xattn_bo': 2.778}
    for name, (base, spread) in spreads.items():
        noise = np.random.default_rng([zlib.crc32(name.encode()), seed]).standard_normal(out[name].shape)
        drawn = base * np.exp(spread * noise) if base else spread * noise
        out[name] = jnp.asarray(drawn.astype(out[name].dtype))
    for name, factor in factors.items():
        out[name] = (out[name] * factor).astype(out[name].dtype)
    return out
```

```python
import concourse.bass as bass
from concourse import mybir
from contextlib import ExitStack

F32 = mybir.dt.float32
F16 = mybir.dt.float16
BF16 = mybir.dt.bfloat16
U32 = mybir.dt.uint32
I32 = mybir.dt.int32
U8 = mybir.dt.uint8
ALU = mybir.AluOpType
ACT = mybir.ActivationFunctionType
AX = mybir.AxisListType

P = 128
B = 32
S = 128
D = 128
H = 16
QUAD = 4
NQUAD = B // QUAD
UNITS = 4
HU = H // UNITS
LN_EPS = 1e-5
E0, E1 = 8, 16
F = 512
CAP1 = S * B // E1
REGION0 = S * B + P
TILES0 = 2 * S * B // P + E0
NSPLIT = 3


def hold(eng, s, value, held):
    eng.wait_ge(s, value)
    if not isinstance(value, int):
        eng.sem_inc(held, 1)


def release_semaphores(nc, sems):
    nc.clear_and_free_semaphores(sems)
    nc.all_engine_barrier()


def attention_pass(nc, tag, src, dst, w, k, ctx_src=None, mask_src=None, scale=1.0):
    own = ctx_src is None
    masked = own or mask_src is not None
    DH = 64 if own else 8
    DV = DH + 1
    NC = 8 if own else 4
    NP = 20 if own else 9
    NQK = 2 * NC

    sems = []
    with ExitStack() as ctx:
        def sb(name, shape, dt):
            return ctx.enter_context(nc.sbuf_tensor(f"{tag}_{name}", shape, dt))

        def sem(name):
            sems.append(nc.alloc_semaphore(f"{tag}_{name}"))
            return sems[-1]
        held = {e: sem(f"held_{e}") for e in ("sp", "pool", "dve")}

        ident = sb("ident", [P, P], F32)
        ident4 = sb("ident4", [P, QUAD * P], BF16)
        NSEL = 2 if own else 1
        sel = sb("sel", [P, NSEL, HU, P], BF16)
        if own:
            addmask = sb("addmask", [P, 1, QUAD * P], BF16)
            cos = sb("cos", [P, QUAD * S], F32)
            sin = sb("sin", [P, QUAD * S], F32)
        elif masked:
            rawmask = sb("rawmask", [P, QUAD, P], U8)
            addmask = [sb(f"addmask{i}", [P, QUAD, P], BF16) for i in range(2)]
        WN = {"q": NC * P, "k": NC * P, "v": H * DH, "o": (H * DH // P) * D}
        if own:
            WN |= {"qs": NC * P, "ks": NC * P}
        names = ["q", "qs", "k", "ks", "v", "o"] if own else ["q", "k", "v", "o"]
        wh = {n: sb(f"w{n}h", [P, WN[n]], F16) for n in names}
        wl = {n: sb(f"w{n}l", [P, WN[n]], F16) for n in names}
        stage = [sb(f"stage{i}", [P, max(WN.values())], F32) for i in range(2)]
        bias = sb("bias", [P, 4 if own else 2, NC], F32)
        if not own:
            low_rows = sb("low_rows", [P, 2], F32)
            low_bias = sb("low_bias", [P, 2, NC], F32)
        vbias = sb("vbias", [P, H * DH // P], F32)
        vbias_b = sb("vbias_b", [P, H * DH // P, P], F32)
        obias = sb("obias", [P, D], F32)
        obias4 = sb("obias4", [P, QUAD, D], F32)
        expo = sb("expo", [P, 2], F32)

        xin = [sb(f"xin{i}", [P, QUAD, D], F32) for i in range(2)]
        xres = [sb(f"xres{i}", [P, QUAD, D], F32) for i in range(2)]
        xout = [sb(f"xout{i}", [P, QUAD, D], F32) for i in range(2)]
        xh, xl = sb("xh", [P, QUAD * S], F16), sb("xl", [P, QUAD * S], F16)
        if own:
            ch, cl = xh, xl
            rot = [[sb(f"rot{i}{j}", [P, QUAD * S], F32) for j in range(2)] for i in range(2)]
            full = [sb(f"full{i}", [P, QUAD * S], F32) for i in range(2)]
            qkh = [[sb(f"qkh{i}{j}", [P, NC, QUAD * S], F16) for j in range(2)] for i in range(2)]
            qkl = [[sb(f"qkl{i}{j}", [P, NC, QUAD * S], F16) for j in range(2)] for i in range(2)]
        else:
            cin = [sb(f"cin{i}", [P, QUAD, D], F32) for i in range(2)]
            ch, cl = sb("ch", [P, QUAD * S], F16), sb("cl", [P, QUAD * S], F16)
            high = [sb(f"high{i}", [P, QUAD * S], F16) for i in range(2)]
            qks = [[sb(f"qks{i}{j}", [P, NC, QUAD * S], F16) for j in range(2)] for i in range(2)]
        vh = [sb(f"vh{i}", [P, QUAD, H, DV], F16) for i in range(2)]
        vl = [sb(f"vl{i}", [P, QUAD, H, DV], F16) for i in range(2)]
        negmax = [sb(f"negmax{i}", [P, H], F32) for i in range(2)]
        rest = [sb(f"rest{i}", [P, H], F32) for i in range(2)]
        max3 = [sb(f"max3{i}", [P, UNITS, 32], BF16) for i in range(2)]
        maxT = [sb(f"maxT{i}", [P, P], BF16) for i in range(2)]
        pf = [sb(f"pf{i}", [P, HU * P], F32) for i in range(2)]
        ph = [sb(f"ph{i}", [P, HU * P], F16) for i in range(2)]
        pl = [sb(f"pl{i}", [P, HU * P], F16) for i in range(2)]
        NA = HU if own else H
        recip = sb("recip", [P, NA], F32)
        att = [sb(f"att{i}", [P, NA, DH], F32) for i in range(2)]
        attTh = sb("attTh", [P, H * DH // P, P], F16)
        attTl = sb("attTl", [P, H * DH // P, P], F16)
        ysum = sb("ysum", [P, D], F32)
        stats, mv = sb("stats", [P, 6], F32), sb("mv", [P, 2], F32)
        veps, rstd = sb("veps", [P, 1], F32), sb("rstd", [P, 1], F32)

        def ps(name):
            return ctx.enter_context(nc.psum_tensor(f"{tag}_{name}", [P, 512], F32))
        scp = [ps("scores0"), ps("scores1")]
        stp = [ps("scoresT0"), ps("scoresT1")]
        prj = [ps("proj0"), ps("proj1")]
        avp = ps("attended")
        msc = ps("misc")

        s_const, s_stage, s_wh, s_wl = sem("const"), sem("stage"), sem("w_high"), sem("w_low")
        s_vb, s_obp, s_ready = sem("vbias_b"), sem("obias_ps"), sem("setup_done")
        s_xin, s_cin, s_min = sem("x_in"), sem("ctx_in"), sem("mask_in")
        s_misc, s_misc_hi, s_misc_free = sem("misc_ps"), sem("misc_high"), sem("misc_free")
        s_proj, s_proj_hi, s_proj_free = sem("proj_ps"), sem("proj_high"), sem("proj_free")
        s_full, s_qkhi, s_qklo = sem("rope_sum"), sem("qk_high"), sem("qk_low")
        s_scores, s_max, s_split = sem("scores_ps"), sem("max_done"), sem("max_split")
        s_link, s_maxT = sem("pool_link"), sem("max_T")
        s_scoresT, s_exp, s_plow = sem("scoresT_ps"), sem("exp_done"), sem("p_low")
        s_av, s_norm = sem("attended_ps"), sem("normed")
        s_dve, s_rec, s_st = sem("dve_link"), sem("reciprocal"), sem("stats")
        s_res, s_y, s_rstd, s_ln, s_out = (sem("residual"), sem("y_sum"), sem("rstd"),
                                           sem("ln_done"), sem("x_out"))
        s_mask = sem("mask_ready")

        def slots(first, last):
            npiece, per = NP, (2 if own else 1)
            for s in range(16):
                b, g = divmod(s, UNITS)
                if g == 0:
                    yield "maxT", b, 0
                if not (last and b == 3):
                    yield "scores", b + 1, g
                if not last and s == 0:
                    yield "xT", 0, 0
                    if not own:
                        yield "ctxT", 0, 0
                if not last and 1 <= s:
                    for p in range(per * (s - 1), min(per * s, npiece)):
                        yield "piece", 0, p
                yield "scoresT", b, g
                if not (first and s == 0):
                    yield "attend", (s - 1) // 4, (s - 1) % 4
                seen = not (first and b == 0)
                if own:
                    if g == 2 and seen:
                        yield "out", b - 1, 0
                    if not (first and s < 2):
                        yield "attT", (s - 2) // 4, (s - 2) % 4
                else:
                    if g == 1 and seen:
                        yield "attT", b - 1, 0
                    if g == 2 and seen:
                        yield "out", b - 1, 0
                if g == 3 and seen:
                    yield "norm", b - 1, 0
            if last:
                yield "attend", 3, 3
                if own:
                    yield "attT", 3, 2
                    yield "attT", 3, 3
                else:
                    yield "attT", 3, 0
                yield "out", 3, 0
                yield "norm", 3, 0

        def opening():
            yield "xT", 0, 0
            if not own:
                yield "ctxT", 0, 0
            for p in range(NP):
                yield "piece", 0, p
            for g in range(UNITS):
                yield "scores", 4, g

        MISC = ("maxT", "xT", "ctxT", "attT", "out")
        count = lambda events: sum(e[0] in MISC for e in events)
        M_OPEN, M_FIRST, M_STEP = count(opening()), count(slots(True, False)), count(slots(False, False))

        def numbered(n, events, base):
            m = base
            for what, b, g in events:
                yield what, b, g, m
                m += what in MISC

        def walk(eng, handle):
            for what, b, g, m in numbered(-1, opening(), 0):
                handle(what, -1, 1, b, g, m)
            for what, b, g, m in numbered(0, slots(True, False), M_OPEN):
                handle(what, 0, 0, b, g, m)
            with eng.Fori(0, (NQUAD - 2) // 2) as i:
                for half in range(2):
                    n = 2 * i + (1 + half)
                    base = M_OPEN + M_FIRST + M_STEP * half
                    for what, b, g, m in numbered(n, slots(False, False), base):
                        handle(what, n, 1 - half, b, g, i * (2 * M_STEP) + m)
            base = M_OPEN + M_FIRST + M_STEP * (NQUAD - 2)
            for what, b, g, m in numbered(NQUAD - 1, slots(False, True), base):
                handle(what, NQUAD - 1, 1, b, g, m)

        def wait(eng, s, value):
            if not (isinstance(value, int) and value <= 0):
                eng.wait_ge(s, value)

        def hold_late(eng, s, value, held):
            if not (isinstance(value, int) and value <= 0):
                hold(eng, s, value, held)

        def place(g, j):
            if own:
                return 64 * (g % 2), 64, 4 * (g // 2) + j
            return 32 * g, 32, j

        def seat(g):
            return 2 * (g % 2) + g // 2 if own else g

        block = ctx.enter_context(nc.Block())

        @block.sync
        def _(sp):
            consts = [(ident[:], k["ident"]), (ident4[:], k["ident4"]), (sel[:], k["sel"]),
                      (bias[:], w["bias"]), (vbias[:], w["vbias"]), (expo[:], k["expo"]),
                      (obias[:], w["obias"].partition_broadcast(P))]
            if own:
                consts += [(addmask[:, 0, :], k["causal4"]), (cos[:], k["cos"]), (sin[:], k["sin"])]
            else:
                consts += [(low_rows[:], k["low_rows"])]
            for n, (to, frm) in enumerate(consts):
                sp.dma_start(to, frm).then_inc(s_const, 16)
            wait(sp, s_const, 16 * len(consts))
            sp.dma_start(xin[0][:], src[0:QUAD].rearrange("b t d -> t b d")).then_inc(s_xin, 16)
            if not own:
                sp.dma_start(cin[0][:], ctx_src[0:QUAD].rearrange("b t d -> t b d")).then_inc(s_cin, 16)
            for n, name in enumerate(names):
                if n >= 2:
                    sp.wait_ge(s_wl, n - 1)
                sp.dma_start(stage[n % 2][:, 0:WN[name]], w[name]).then_inc(s_stage, 16)
                sp.wait_ge(s_stage, 16 * (n + 1))

            def load(n, par):
                if not (isinstance(n, int) and n < 2):
                    sp.wait_ge(s_res, n - 1)
                wait(sp, s_xin, 16 * n)
                sp.dma_start(xin[par][:], src[bass.ds(4 * n, QUAD)].rearrange("b t d -> t b d"))\
                  .then_inc(s_xin, 16)
                if not own:
                    wait(sp, s_cin, 16 * n)
                    sp.dma_start(cin[par][:], ctx_src[bass.ds(4 * n, QUAD)].rearrange("b t d -> t b d"))\
                      .then_inc(s_cin, 16)

            def load_mask(n):
                wait(sp, s_mask, n)
                sp.dma_start(rawmask[:], mask_src[bass.ds(4 * n, QUAD)].rearrange("b t d -> t b d"))\
                  .then_inc(s_min, 16)

            if masked and not own:
                load_mask(0)
            load(1, 1)

            def handle(what, n, par, b, g, m):
                if what == "norm":
                    row = 4 * n + b
                    hold(sp, s_ln, row + 1, held["sp"])
                    hold_late(sp, s_out, 16 * row, held["sp"])
                    q = par if b >= 0 else 1 - par
                    sp.dma_start(dst[bass.ds(row, 1)].rearrange("b t d -> t b d"),
                                 xout[q][:, b % 4:b % 4 + 1, :]).then_inc(s_out, 16)
                    if b == 0 and not (isinstance(n, int) and n >= NQUAD - 2):
                        load_next(n + 2, par)
                if what == "ctxT" and masked and not own and not (isinstance(n, int) and n < 0):
                    load_mask(n + 1)

            def load_next(n, par):
                load(n, par)

            for what, b, g, m in numbered(0, slots(True, False), 0):
                handle(what, 0, 0, b, g, m)
            with sp.Fori(0, (NQUAD - 2) // 2 - 1) as i:
                for half in range(2):
                    for what, b, g, m in numbered(0, slots(False, False), 0):
                        handle(what, 2 * i + (1 + half), 1 - half, b, g, m)
            for n in range(NQUAD - 3, NQUAD):
                for what, b, g, m in numbered(0, slots(False, n == NQUAD - 1), 0):
                    handle(what, n, n % 2, b, g, m)
            sp.wait_ge(s_out, 16 * B)

        @block.tensor
        def _(pe):
            pe.wait_ge(s_vb, 1)
            pe.wait_ge(s_stage, 16 * len(names))
            no = H * DH // P
            so = stage[(len(names) - 1) % 2]
            for c in range(no):
                mm = nc.tensor.matmul(msc[:, 0:D], vbias_b[:, c, :], so[:, c * D:(c + 1) * D],
                                      start=(c == 0), stop=(c == no - 1))
            mm.then_inc(s_obp, 1)
            pe.wait_ge(s_ready, 1)

            def three(out, lh, ll, rh, rl, start, stop):
                nc.tensor.matmul(out, lh, rl, start=start, stop=False)
                nc.tensor.matmul(out, ll, rh, start=False, stop=False)
                return nc.tensor.matmul(out, lh, rh, start=False, stop=stop)

            def handle(what, n, par, b, g, m):
                q = par if 0 <= b < 4 else 1 - par
                bb = b % 4
                unit = 16 * n + 4 * b + g
                row = 4 * n + b
                cols = slice(bb * S, (bb + 1) * S)
                if what in MISC:
                    wait(pe, s_misc_free, m)
                if what in ("xT", "ctxT"):
                    pe.wait_ge(s_xin if what == "xT" else s_cin, 16 * (n + 2))
                    t = xin[1 - par] if what == "xT" else cin[1 - par]
                    for j in range(QUAD):
                        mm = nc.tensor.transpose(msc[:, j * P:(j + 1) * P], t[:, j, :], ident[:])
                    mm.then_inc(s_misc, 1)
                elif what == "piece":
                    f = NP * (n + 1) + g
                    if g == 0:
                        wait(pe, s_misc_free, m)
                    wait(pe, s_proj_free, f if own or g == 0 else f - 1)
                    if own and g < NQK:
                        c = slice((g // 2) * P, (g // 2 + 1) * P)
                        for t, name in enumerate((("q", "qs"), ("k", "ks"))[g % 2]):
                            mm = three(prj[t][:], wh[name][:, c], wl[name][:, c], xh[:], xl[:], True, True)
                    elif own:
                        c = slice((g - NQK) * S, (g - NQK + 1) * S)
                        for t in range(2):
                            o = slice(t * 512, (t + 1) * 512)
                            mm = three(prj[t][:], xh[:, c], xl[:, c], wh["v"][:, o], wl["v"][:, o], True, True)
                    elif g < NQK:
                        name, a, l = (("q", xh, xl), ("k", ch, cl))[g % 2]
                        c = slice((g // 2) * P, (g // 2 + 1) * P)
                        mm = three(prj[g % 2][:], wh[name][:, c], wl[name][:, c], a[:], l[:], True, True)
                    else:
                        for j in range(QUAD):
                            c = slice(j * S, (j + 1) * S)
                            mm = three(prj[0][:, c], ch[:, c], cl[:, c], wh["v"][:], wl["v"][:], True, True)
                    mm.then_inc(s_proj, 1)
                elif what == "scores":
                    if g == 0 and bb == 0:
                        if own:
                            pe.wait_ge(s_qklo, NQK * (n + 2))
                        else:
                            pe.wait_ge(s_proj_free, NP * (n + 2))
                    if g == 0 and masked and not own and bb == 0:
                        pe.wait_ge(s_mask, n + 2)
                    wait(pe, s_max, unit - 1)
                    out = scp[g % 2]
                    if masked:
                        rhs = addmask[:, 0, :] if own else None
                        if own:
                            nc.tensor.matmul(out[:], ident4[:, 0:P], rhs, start=True, stop=False,
                                             skip_group_check=True)
                        else:
                            for j in range(HU):
                                nc.tensor.matmul(out[:, j * P:(j + 1) * P], ident4[:, 0:P],
                                                 addmask[q][:, bb, :], start=(j == 0), stop=False,
                                                 skip_group_check=True)
                    for j in range(HU):
                        r, nr, c = place(g, j)
                        o = out[:, j * P:(j + 1) * P]
                        if own:
                            qa, ql_, ka, kl_ = (t[q][r:r + nr, c, cols] for t in
                                                ([x[0] for x in qkh], [x[0] for x in qkl],
                                                 [x[1] for x in qkh], [x[1] for x in qkl]))
                            nc.tensor.matmul(o, qa, kl_, start=False, stop=False, skip_group_check=True)
                            nc.tensor.matmul(o, ql_, ka, start=False, stop=False, skip_group_check=True)
                            mm = nc.tensor.matmul(o, qa, ka, start=False, stop=True, skip_group_check=True)
                        else:
                            mm = nc.tensor.matmul(o, qks[q][0][r:r + nr, c, cols], qks[q][1][r:r + nr, c, cols],
                                                  start=not masked, stop=True, skip_group_check=True)
                    mm.then_inc(s_scores, 1)
                elif what == "maxT":
                    pe.wait_ge(s_split, row + 1)
                    t = max3[bb % 2]
                    nc.tensor.transpose(msc[:, 0:P // 2].bitcast(BF16), t[:].rearrange("p u r -> p (u r)"),
                                        ident4[:, 0:P])\
                      .then_inc(s_misc, 1)
                elif what == "scoresT":
                    wait(pe, s_exp, unit - 1)
                    if g == 0:
                        pe.wait_ge(s_maxT, row + 1)
                    out = stp[g % 2]
                    if masked:
                        msk = addmask[:, 0, 0:P] if own else addmask[q][:, bb, :]
                        nc.tensor.matmul(out[:], msk, ident4[:], start=True, stop=False, skip_group_check=True)
                    for j in range(HU):
                        r, nr, c = place(g, j)
                        o = out[:, j * P:(j + 1) * P]
                        if own:
                            qa, ql_, ka, kl_ = (t[q][r:r + nr, c, cols] for t in
                                                ([x[0] for x in qkh], [x[0] for x in qkl],
                                                 [x[1] for x in qkh], [x[1] for x in qkl]))
                            nc.tensor.matmul(o, kl_, qa, start=False, stop=False, skip_group_check=True)
                            nc.tensor.matmul(o, ka, ql_, start=False, stop=False, skip_group_check=True)
                            nc.tensor.matmul(o, ka, qa, start=False, stop=False, skip_group_check=True)
                        else:
                            nc.tensor.matmul(o, qks[q][1][r:r + nr, c, cols], qks[q][0][r:r + nr, c, cols],
                                             start=not masked, stop=False, skip_group_check=True)
                        mm = nc.tensor.matmul(o, sel[r:r + nr, g // 2 if own else 0, j, :],
                                              maxT[bb % 2][r:r + nr, :], start=False, stop=True,
                                              skip_group_check=True)
                    mm.then_inc(s_scoresT, 1)
                elif what == "attend":
                    pe.wait_ge(s_plow, unit + 1)
                    if own:
                        wait(pe, s_norm, unit)
                    elif g == 0:
                        wait(pe, s_norm, row)
                    for j in range(HU):
                        at = (j if own else 4 * g + j) * DV
                        o = avp[:, at:at + DV]
                        a, l = ph[g % 2][:, j * P:(j + 1) * P], pl[g % 2][:, j * P:(j + 1) * P]
                        hv, lv = vh[q][:, bb, 4 * g + j, :], vl[q][:, bb, 4 * g + j, :]
                        mm = three(o, a, l, hv, lv, True, True)
                    mm.then_inc(s_av, 1)
                elif what == "attT":
                    if own:
                        pe.wait_ge(s_norm, unit + 1)
                        t = att[g % 2]
                        for j in range(2):
                            mm = nc.tensor.transpose(msc[:, j * P:(j + 1) * P],
                                                     t[:, 2 * j:2 * j + 2, :].rearrange("p h d -> p (h d)"), ident[:])
                    else:
                        pe.wait_ge(s_norm, row + 1)
                        mm = nc.tensor.transpose(msc[:, 0:P], att[bb % 2][:].rearrange("p h d -> p (h d)"), ident[:])
                    mm.then_inc(s_misc, 1)
                elif what == "out":
                    for c in range(no):
                        mm = three(msc[:, 0:D], attTh[:, c, :], attTl[:, c, :], wh["o"][:, c * D:(c + 1) * D],
                                   wl["o"][:, c * D:(c + 1) * D], c == 0, c == no - 1)
                    mm.then_inc(s_misc, 1)

            walk(pe, handle)

        @block.scalar
        def _(act):
            for n, name in enumerate(names):
                act.wait_ge(s_stage, 16 * (n + 1))
                nc.scalar.copy(wh[name][:], stage[n % 2][:, 0:WN[name]]).then_inc(s_wh, 1)
            act.wait_ge(s_ready, 1)

            def handle(what, n, par, b, g, m):
                unit = 16 * n + 4 * b + g
                row = 4 * n + b
                bb = b % 4
                if what in ("xT", "ctxT"):
                    act.wait_ge(s_misc, m + 1)
                    nc.scalar.copy((xh if what == "xT" else ch)[:], msc[:]).then_inc(s_misc_hi, 1)
                elif what == "maxT":
                    act.wait_ge(s_misc, m + 1)
                    nc.scalar.copy(maxT[bb % 2][:], msc[:, 0:P // 2].bitcast(BF16))\
                      .then_inc(s_maxT, 1)
                elif what == "piece":
                    f = NP * (n + 1) + g
                    kk = NQK * (n + 1) + g
                    if own and 1 <= g <= NQK:
                        act.wait_ge(s_full, kk)
                        p = g - 1
                        nc.scalar.copy(qkh[1 - par][p % 2][:, p // 2, :], full[p % 2][:]).then_inc(s_qkhi, 1)
                    if own and g >= NQK:
                        act.wait_ge(s_proj, f + 1)
                        for t in range(2):
                            last = nc.scalar.copy(vh[1 - par][:, g - NQK, 8 * t:8 * t + 8, 0:DH],
                                                  prj[t][:].rearrange("p (h d) -> p h d", d=DH))
                        last.then_inc(s_proj_hi, 1)
                    if not own:
                        act.wait_ge(s_proj, f + 1)
                        if g < NQK:
                            wait(act, s_proj_free, f - 1)
                            nc.scalar.activation(high[g % 2][:], prj[g % 2][:], ACT.Identity,
                                                 bias=low_bias[:, g % 2, g // 2:g // 2 + 1],
                                                 scale=low_rows[:, g % 2:g % 2 + 1]).then_inc(s_proj_hi, 1)
                        else:
                            nc.scalar.copy(vh[1 - par][:, :, :, 0:DH],
                                           prj[0][:].rearrange("p (b h d) -> p b h d", b=QUAD, d=DH))\
                              .then_inc(s_proj_hi, 1)
                elif what == "scoresT":
                    act.wait_ge(s_scoresT, unit + 1)
                    wait(act, s_av, unit - 1)
                    wait(act, s_plow, unit - 1)
                    nc.scalar.activation(ph[g % 2][:], stp[g % 2][:], ACT.Exp, scale=scale)
                    nc.scalar.activation(pf[g % 2][:], stp[g % 2][:], ACT.Exp, scale=scale).then_inc(s_exp, 1)
                elif what == "attT":
                    act.wait_ge(s_misc, m + 1)
                    n_ = 2 if own else 1
                    c = 2 * g if own else 0
                    nc.scalar.copy(attTh[:, c:c + n_, :], msc[:, 0:n_ * P].rearrange("p (c t) -> p c t", c=n_))\
                      .then_inc(s_misc_hi, 1)

            walk(act, handle)

        HI = ("xT", "ctxT", "attT")
        count_hi = lambda events: sum(e[0] in HI for e in events)
        H_OPEN, H_FIRST, H_STEP = (count_hi(opening()), count_hi(slots(True, False)),
                                   count_hi(slots(False, False)))

        @block.gpsimd
        def _(pool):
            linked = [0]

            def link(ins):
                ins.then_inc(s_link, 1)

            for i in range(2):
                nc.gpsimd.memset(vh[i][:, :, :, DH:DV], 1.0)
                nc.gpsimd.memset(vl[i][:, :, :, DH:DV], 0.0).then_inc(s_link, 1)
            for i in range(2):
                nc.gpsimd.memset(max3[i][:], 0.0).then_inc(s_link, 1)
            LINKS = 3
            L0 = 4

            def split(row, bb):
                hold(pool, s_max, 4 * row + 4, held["pool"])
                if not (isinstance(row, int) and row < 2):
                    hold(pool, s_maxT, row - 1, held["pool"])
                at = L0 + LINKS * row
                x, r = (t[bb % 2][:].rearrange("p (u j) -> p u j", u=UNITS) for t in (negmax, rest))
                part = [max3[bb % 2][:, :, HU * t:HU * t + HU] for t in range(NSPLIT)]
                nc.gpsimd.tensor_copy(part[0], x).then_inc(s_link, 1)
                pool.wait_ge(s_link, at + 1)
                nc.gpsimd.tensor_tensor(r, x, part[0], ALU.subtract).then_inc(s_link, 1)
                hold(pool, s_link, at + 2, held["pool"])
                nc.gpsimd.tensor_copy(part[1], r).then_inc(s_link, 1)
                pool.wait_ge(s_link, at + 3)
                nc.gpsimd.tensor_tensor(part[2], r, part[1], ALU.subtract).then_inc(s_split, 1)

            def handle(what, n, par, b, g, m):
                row = 4 * n + b
                if what == "piece" and own:
                    f = NP * (n + 1) + g
                    kk = NQK * (n + 1) + g
                    if 2 <= g < NQK + 2:
                        p = g - 2
                        pool.wait_ge(s_qkhi, kk - 1)
                        nc.gpsimd.tensor_tensor(qkl[1 - par][p % 2][:, p // 2, :], full[p % 2][:],
                                                qkh[1 - par][p % 2][:, p // 2, :], ALU.subtract)\
                            .then_inc(s_qklo, 1)
                    if g < NQK:
                        pool.wait_ge(s_proj_free, f + 1)
                        if not (isinstance(n, int) and n < 0 and g < 2):
                            pool.wait_ge(s_qklo, kk - 1)
                        nc.gpsimd.tensor_tensor(full[g % 2][:], rot[g % 2][0][:], rot[g % 2][1][:], ALU.add)\
                            .then_inc(s_full, 1)
                if what == "piece" and g == NP - 3:
                    pool.wait_ge(s_xin, 16 * (n + 2))
                    pool.wait_ge(s_proj, NP * (n + 1) + g + 1)
                    wait(pool, s_y, 4 * n)
                    nc.gpsimd.tensor_tensor(xres[1 - par][:], xin[1 - par][:], obias4[:], ALU.add)\
                        .then_inc(s_res, 1)
                if what == "ctxT" and masked:
                    pool.wait_ge(s_min, 16 * (n + 2))
                    hold_late(pool, s_scoresT, 16 * n, held["pool"])
                    nc.gpsimd.tensor_scalar(addmask[1 - par][:], rawmask[:], -1e18, None, ALU.mult)\
                        .then_inc(s_mask, 1)
                if what == "scores" and g == 3:
                    split(row, b % 4)
                if what == "out":
                    hold(pool, s_y, row + 1, held["pool"])
                    nc.gpsimd.tensor_scalar(veps[:], mv[:, 1:2], LN_EPS, None, ALU.add).then_inc(s_rstd, 1)
                    pool.wait_ge(s_rstd, 2 * row + 1)
                    nc.gpsimd.tensor_tensor(rstd[:], veps[:], expo[:, 0:1], ALU.pow).then_inc(s_rstd, 1)

            pool.wait_ge(s_link, L0)
            pool.wait_ge(s_ready, 1)
            walk(pool, handle)

        @block.vector
        def _(dve):
            nconst = 7 + (3 if own else 1)
            dve.wait_ge(s_const, 16 * nconst)
            links = [0]

            def link(ins):
                links[0] += 1
                ins.then_inc(s_dve, 1)
                dve.wait_ge(s_dve, links[0])

            no = H * DH // P
            for c in range(no):
                ins = nc.vector.tensor_copy(vbias_b[:, c, :], vbias[:, c:c + 1].to_broadcast([P, P]))
            ins.then_inc(s_vb, 1)
            if not own:
                for t in range(2):
                    link(nc.vector.tensor_scalar(low_bias[:, t, :], bias[:, t, :], low_rows[:, t:t + 1], None,
                                                 ALU.mult))
            for n, name in enumerate(names):
                dve.wait_ge(s_wh, n + 1)
                nc.vector.tensor_tensor(wl[name][:], stage[n % 2][:, 0:WN[name]], wh[name][:],
                                        ALU.subtract).then_inc(s_wl, 1)
            dve.wait_ge(s_obp, 1)
            for j in range(QUAD):
                link(nc.vector.tensor_tensor(obias4[:, j, :], obias[:], msc[:, 0:D], ALU.add))
            dve.wait_ge(s_wl, len(names))
            dve.sem_inc(s_ready, 1)

            def lowp(n, par, b, g):
                unit = 16 * n + 4 * b + g
                dve.wait_ge(s_exp, unit + 1)
                wait(dve, s_av, unit - 1)
                nc.vector.tensor_tensor(pl[g % 2][:], pf[g % 2][:], ph[g % 2][:], ALU.subtract)\
                    .then_inc(s_plow, 1)

            def handle(what, n, par, b, g, m, hi):
                unit = 16 * n + 4 * b + g
                row = 4 * n + b
                bb = b % 4
                if what in ("xT", "ctxT"):
                    dve.wait_ge(s_misc_hi, hi + 1)
                    h, l = (xh, xl) if what == "xT" else (ch, cl)
                    nc.vector.tensor_tensor(l[:], msc[:], h[:], ALU.subtract).then_inc(s_misc_free, 1)
                elif what == "maxT":
                    dve.wait_ge(s_maxT, row + 1)
                    dve.sem_inc(s_misc_free, 1)
                elif what == "piece":
                    f = NP * (n + 1) + g
                    kk = NQK * (n + 1) + g
                    if own and g < NQK:
                        dve.wait_ge(s_proj, f + 1)
                        wait(dve, s_full, kk - 1)
                        for t, table in enumerate((cos, sin)):
                            ins = nc.vector.scalar_tensor_tensor(
                                out=rot[g % 2][t][:], in0=prj[t][:], scalar=bias[:, 2 * (g % 2) + t, g // 2:g // 2 + 1],
                                in1=table[:], op0=ALU.add, op1=ALU.mult)
                        ins.then_inc(s_proj_free, 1)
                    elif own:
                        dve.wait_ge(s_proj_hi, 4 * (n + 1) + g - NQK + 1)
                        for t in range(2):
                            ins = nc.vector.tensor_tensor(vl[1 - par][:, g - NQK, 8 * t:8 * t + 8, 0:DH],
                                                          prj[t][:].rearrange("p (h d) -> p h d", d=DH),
                                                          vh[1 - par][:, g - NQK, 8 * t:8 * t + 8, 0:DH], ALU.subtract)
                        ins.then_inc(s_proj_free, 1)
                    elif g < NQK:
                        dve.wait_ge(s_proj_hi, f + 1)
                        ins = nc.vector.scalar_tensor_tensor(
                            out=qks[1 - par][g % 2][:, g // 2, :], in0=prj[g % 2][:],
                            scalar=bias[:, g % 2, g // 2:g // 2 + 1], in1=high[g % 2][:],
                            op0=ALU.add, op1=ALU.subtract).then_inc(s_proj_free, 1)
                    else:
                        dve.wait_ge(s_proj_hi, f + 1)
                        nc.vector.tensor_tensor(vl[1 - par][:, :, :, 0:DH],
                                                prj[0][:].rearrange("p (b h d) -> p b h d", b=QUAD, d=DH),
                                                vh[1 - par][:, :, :, 0:DH], ALU.subtract).then_inc(s_proj_free, 1)
                elif what == "scores":
                    dve.wait_ge(s_scores, unit + 1)
                    if g == 0:
                        wait(dve, s_split, row - 1)
                    nc.vector.tensor_reduce(negmax[bb % 2][:, HU * seat(g):HU * seat(g) + HU],
                                            scp[g % 2][:].rearrange("p (h t) -> p h t", h=HU),
                                            AX.X, ALU.max, negate=True).then_inc(s_max, 1)
                elif what == "attend":
                    if own or g == 3:
                        dve.wait_ge(s_av, unit + 1)
                        v = avp[:, 0:NA * DV].rearrange("p (h d) -> p h d", d=DV)
                        nc.vector.reciprocal(recip[:], v[:, :, DH]).then_inc(s_rec, 1)
                        dve.wait_ge(s_rec, (unit if own else row) + 1)
                        i = g % 2 if own else bb % 2
                        nc.vector.tensor_tensor(att[i][:], v[:, :, 0:DH],
                                                recip[:].unsqueeze(2).to_broadcast([P, NA, DH]), ALU.mult)\
                            .then_inc(s_norm, 1)
                elif what == "attT":
                    dve.wait_ge(s_misc_hi, hi + 1)
                    n_ = 2 if own else 1
                    c = 2 * g if own else 0
                    nc.vector.tensor_tensor(attTl[:, c:c + n_, :], msc[:, 0:n_ * P].rearrange("p (c t) -> p c t", c=n_),
                                            attTh[:, c:c + n_, :], ALU.subtract).then_inc(s_misc_free, 1)
                elif what == "out":
                    dve.wait_ge(s_misc, m + 1)
                    dve.wait_ge(s_res, n + 1 if b >= 0 else n)
                    q = par if b >= 0 else 1 - par
                    nc.vector.tensor_tensor(ysum[:], msc[:, 0:D], xres[q][:, bb, :], ALU.add)\
                        .then_inc(s_misc_free, 1)
                    dve.wait_ge(s_misc_free, m + 1)
                    nc.vector.bn_stats(stats[:], ysum[:]).then_inc(s_st, 1)
                    hold(dve, s_st, row + 1, held["dve"])
                    nc.vector.bn_aggr(mv[:], stats[:]).then_inc(s_y, 1)
                elif what == "norm":
                    dve.wait_ge(s_rstd, 2 * row + 2)
                    if not (isinstance(row, int) and row < 3):
                        dve.wait_ge(s_out, 16 * (row - 2))
                    q = par if b >= 0 else 1 - par
                    nc.vector.tensor_scalar(xout[q][:, bb, :], ysum[:], mv[:, 0:1], rstd[:], ALU.subtract,
                                            ALU.mult).then_inc(s_ln, 1)

            def walk_hi():
                def run(n, par, events, mbase, hbase, i=None):
                    m, hi = 0, 0
                    for what, b, g in events:
                        mm = mbase + m if i is None else i * (2 * M_STEP) + (mbase + m)
                        hh = hbase + hi if i is None else i * (2 * H_STEP) + (hbase + hi)
                        if what == "attend":
                            lowp(n, par, b, g)
                        handle(what, n, par, b, g, mm, hh)
                        m += what in MISC
                        hi += what in HI
                run(-1, 1, opening(), 0, 0)
                run(0, 0, slots(True, False), M_OPEN, H_OPEN)
                with dve.Fori(0, (NQUAD - 2) // 2) as i:
                    for half in range(2):
                        run(2 * i + (1 + half), 1 - half, slots(False, False),
                            M_OPEN + M_FIRST + M_STEP * half, H_OPEN + H_FIRST + H_STEP * half, i)
                run(NQUAD - 1, 1, slots(False, True), M_OPEN + M_FIRST + M_STEP * (NQUAD - 2),
                    H_OPEN + H_FIRST + H_STEP * (NQUAD - 2))

            walk_hi()
    release_semaphores(nc, sems)


def route_pass(nc, tag, src, slots_dram, w, k, keep, experts, top, region, cap=None, norm=False, zeros=None):
    E = experts
    sems = []
    with ExitStack() as ctx:
        def sb(name, shape, dt):
            return ctx.enter_context(nc.sbuf_tensor(f"{tag}_{name}", shape, dt))

        def sem(name):
            sems.append(nc.alloc_semaphore(f"{tag}_{name}"))
            return sems[-1]
        held = {e: sem(f"held_{e}") for e in ("sp", "pool", "dve")}
        ident = sb("ident", [P, P], F32)
        below, ones = sb("below", [P, P], BF16), sb("ones", [P, P], BF16)
        iota = sb("iota", [P, 1, E], F32)
        wr, br = sb("wr", [P, E], F32), sb("br", [P, 1, E], F32)
        if norm:
            gamma, beta = sb("gamma", [P, 1, D], F32), sb("beta", [P, 1, D], F32)
            expo4 = sb("expo4", [P, QUAD], F32)
            stats, mv = sb("stats", [P, QUAD, 6], F32), sb("mv", [P, QUAD, 2], F32)
            veps, rstd = sb("veps", [P, QUAD], F32), sb("rstd", [P, QUAD], F32)
        x = [sb(f"x{i}", [P, QUAD, D], F32) for i in range(2)]
        rows = [sb(f"rows{i}", [P, QUAD, D], F32) for i in range(2)] if norm else x
        xT = sb("xT", [P, QUAD * S], F32)
        logit, top8, idx8 = sb("logit", [P, QUAD, E], F32), sb("top8", [P, QUAD, 8], F32), sb("idx8", [P, QUAD, 8], U32)
        peak, total = sb("peak", [P, QUAD], F32), sb("total", [P, QUAD], F32)
        prob = sb("prob", [P, QUAD, E], F32)
        hot = [sb(f"hot{i}", [P, QUAD, E], F32) for i in range(top)]
        both, seen = sb("both", [P, QUAD, E], BF16), sb("seen", [P, E], BF16)
        more = sb("more", [P, E], F32)
        ranks, work = sb("ranks", [P, QUAD, E], F32), sb("work", [P, QUAD, E], F32)
        place = sb("place", [P, QUAD], F32)
        kept = sb("kept", [P, QUAD], F32)
        slot = [sb(f"slot{i}", [P, QUAD, top], U32) for i in range(2)]
        ptr = ctx.enter_context(nc.psum_tensor(f"{tag}_ptr", [P, 512], F32))
        plg = ctx.enter_context(nc.psum_tensor(f"{tag}_plg", [P, 512], F32))
        prk = ctx.enter_context(nc.psum_tensor(f"{tag}_prk", [P, 512], F32))
        s_c, s_x, s_step, s_rows, s_rstd = sem("const"), sem("x_in"), sem("dve_step"), sem("rows_ready"), sem("rstd")
        s_T, s_Tsb, s_lg, s_peak, s_exp, s_hot, s_rank, s_slot = (
            sem("turned"), sem("turned_sb"), sem("logits_ps"), sem("less_peak"), sem("exp"), sem("hot"),
            sem("ranks_ps"), sem("slots"))
        s_sent = [sem(f"rows_sent{i}") for i in range(2)]
        s_mv, s_zero = sem("variance"), sem("zeros")
        block = ctx.enter_context(nc.Block())
        consts = [(ident[:], k["ident"]), (below[:], k["below"]), (ones[:], k["ones"]),
                  (iota[:, 0, :], k["iota"][:, 0:E]), (wr[:], w["wr"]), (br[:, 0, :], w["br"].partition_broadcast(P))]
        if norm:
            consts += [(gamma[:, 0, :], w["gamma"].partition_broadcast(P)), (beta[:, 0, :], w["beta"].partition_broadcast(P)),
                       (expo4[:], k["expo4"])]

        @block.sync
        def _(sp):
            for to, frm in consts:
                sp.dma_start(to, frm).then_inc(s_c, 16)
            sp.wait_ge(s_c, 16 * len(consts))

            def load(n, i):
                sp.dma_start(x[i][:], src[bass.ds(4 * n, QUAD)].rearrange("b t d -> t b d")).then_inc(s_x, 16)
                hold(sp, s_x, 16 * n + 16, held["sp"])
            load(0, 0)
            load(1, 1)
            if zeros is not None:
                sp.wait_ge(s_zero, 16 * 16)
            with sp.Fori(1, NQUAD // 2) as i:
                for h in range(2):
                    sp.wait_ge(s_sent[h], 16 * QUAD * top * i)
                    load(2 * i + h, h)

        @block.tensor
        def _(pe):
            pe.wait_ge(s_c, 16 * len(consts))
            with pe.Fori(0, NQUAD // 2) as i:
                for h in range(2):
                    n = 2 * i + h
                    pe.wait_ge(s_rows, n + 1)
                    for b in range(QUAD):
                        mm = nc.tensor.transpose(ptr[:, b * P:(b + 1) * P], rows[h][:, b, :], ident[:])
                    mm.then_inc(s_T, 1)
                    pe.wait_ge(s_Tsb, n + 1)
                    for b in range(QUAD):
                        mm = nc.tensor.matmul(plg[:, b * E:(b + 1) * E], xT[:, b * S:(b + 1) * S], wr[:],
                                              start=True, stop=True)
                    mm.then_inc(s_lg, 1)
                    pe.wait_ge(s_hot, n + 1)
                    for b in range(QUAD):
                        o = prk[:, b * E:(b + 1) * E]
                        nc.tensor.matmul(o, ones[:], seen[:], start=True, stop=False)
                        for a in range(b):
                            nc.tensor.matmul(o, ones[:], both[:, a, :], start=False, stop=False)
                        mm = nc.tensor.matmul(o, below[:], both[:, b, :], start=False, stop=True)
                    mm.then_inc(s_rank, 1)
            if cap is None:
                pe.wait_ge(s_slot, NQUAD)
                nc.tensor.matmul(prk[:, 0:E], ones[:], seen[:], start=True, stop=True).then_inc(s_rank, 1)

        @block.scalar
        def _(act):
            with act.Fori(0, NQUAD) as n:
                act.wait_ge(s_T, n + 1)
                nc.scalar.copy(xT[:], ptr[:]).then_inc(s_Tsb, 1)
                act.wait_ge(s_peak, n + 1)
                nc.scalar.activation(prob[:], logit[:], ACT.Exp).then_inc(s_exp, 1)

        @block.gpsimd
        def _(pool):
            if zeros is not None:
                pool.wait_ge(s_c, 16 * len(consts))
                nc.gpsimd.memset(zeros[0][:], 0.0).then_inc(s_rstd, 1)
                pool.wait_ge(s_rstd, 1)
                for i in range(16):
                    pool.dma_start(zeros[1][bass.ds(256 * i, 256), :].rearrange("(p a) d -> p (a d)", a=2),
                                   zeros[0][:]).then_inc(s_zero, 16)
                pool.wait_ge(s_zero, 256)
            with pool.Fori(0, NQUAD // 2) as i:
                for h in range(2):
                    n = 2 * i + h
                    if norm:
                        hold(pool, s_mv, n + 1, held["pool"])
                        nc.gpsimd.tensor_scalar(veps[:], mv[:, :, 1], LN_EPS, None, ALU.add).then_inc(s_rstd, 1)
                        pool.wait_ge(s_rstd, 2 * n + 1)
                        nc.gpsimd.tensor_tensor(rstd[:], veps[:], expo4[:], ALU.pow).then_inc(s_rstd, 1)
                    hold(pool, s_slot, n + 1, held["pool"])
                    for b in range(QUAD):
                        for t in range(top):
                            limit = E * cap - 1 if cap is not None else E * region - 1
                            pool.indirect_dma_start(slots_dram, bass.IndirectOffsetOnAxis(ap=slot[h][:, b, t:t + 1], axis=0),
                                                    rows[h][:, b, :], None, bounds_check=limit,
                                                    oob_is_err=False).then_inc(s_sent[h], 16)
            for h in range(2):
                pool.wait_ge(s_sent[h], 8 * B * top)

        @block.vector
        def _(dve):
            dve.wait_ge(s_c, 16 * len(consts))
            nc.vector.memset(seen[:], 0.0).then_inc(s_step, 1)
            dve.wait_ge(s_step, 1)

            def quad(n, h, steps):
                at = [0]

                def link(ins):
                    at[0] += 1
                    ins.then_inc(s_step, 1)
                    hold(dve, s_step, steps * n + 1 + at[0], held["dve"])

                dve.wait_ge(s_x, 16 * n + 16)
                if norm:
                    for b in range(QUAD):
                        ins = nc.vector.bn_stats(stats[:, b, :], x[h][:, b, :])
                    link(ins)
                    for b in range(QUAD):
                        ins = nc.vector.bn_aggr(mv[:, b, :], stats[:, b, :])
                    ins.then_inc(s_mv, 1)
                    dve.wait_ge(s_mv, n + 1)
                    dve.wait_ge(s_rstd, 2 * n + 2)
                    for b in range(QUAD):
                        ins = nc.vector.tensor_scalar(rows[h][:, b, :], x[h][:, b, :], mv[:, b, 0:1], rstd[:, b:b + 1],
                                                      ALU.subtract, ALU.mult)
                    link(ins)
                    link(nc.vector.tensor_tensor(rows[h][:], rows[h][:], gamma[:].to_broadcast([P, QUAD, D]), ALU.mult))
                    nc.vector.tensor_tensor(rows[h][:], rows[h][:], beta[:].to_broadcast([P, QUAD, D]),
                                            ALU.add).then_inc(s_rows, 1)
                else:
                    dve.sem_inc(s_rows, 1)
                dve.wait_ge(s_lg, n + 1)
                link(nc.vector.tensor_tensor(logit[:], plg[:, 0:QUAD * E].rearrange("p (b e) -> p b e", e=E),
                                             br[:].to_broadcast([P, QUAD, E]), ALU.add))
                link(nc.vector.tensor_reduce(peak[:], logit[:], AX.X, ALU.max))
                nc.vector.tensor_tensor(logit[:], logit[:], peak[:].unsqueeze(2).to_broadcast([P, QUAD, E]),
                                        ALU.subtract).then_inc(s_peak, 1)
                dve.wait_ge(s_exp, n + 1)
                link(nc.vector.tensor_reduce(total[:], prob[:], AX.X, ALU.add))
                link(nc.vector.reciprocal(total[:], total[:]))
                link(nc.vector.tensor_tensor(prob[:], prob[:], total[:].unsqueeze(2).to_broadcast([P, QUAD, E]), ALU.mult))
                for b in range(QUAD):
                    ins = nc.vector.max(top8[:, b, :], prob[:, b, :])
                link(ins)
                for b in range(QUAD):
                    ins = nc.vector.max_index(idx8[:, b, :], top8[:, b, :], prob[:, b, :])
                link(ins)
                four = bass.ds(4 * n, QUAD)
                nc.vector.tensor_copy(keep["gate"][:, four, :], top8[:, :, 0:top])
                link(nc.vector.tensor_copy(keep["index"][:, four, :], idx8[:, :, 0:top]))
                for t in range(top):
                    ins = nc.vector.tensor_tensor(hot[t][:], iota[:].to_broadcast([P, QUAD, E]),
                                                  keep["index"][:, four, t:t + 1].to_broadcast([P, QUAD, E]), ALU.is_equal)
                link(ins)
                if top == 2:
                    nc.vector.tensor_tensor(both[:], hot[0][:], hot[1][:], ALU.add).then_inc(s_hot, 1)
                else:
                    nc.vector.tensor_copy(both[:], hot[0][:]).then_inc(s_hot, 1)
                dve.wait_ge(s_rank, n + 1)
                link(nc.vector.tensor_copy(ranks[:], prk[:, 0:QUAD * E].rearrange("p (b e) -> p b e", e=E)))
                link(nc.vector.tensor_reduce(more[:], both[:].rearrange("p b e -> p e b"), AX.X, ALU.add))
                nc.vector.tensor_tensor(seen[:], seen[:], more[:], ALU.add)
                for t in range(top):
                    link(nc.vector.tensor_tensor(work[:], ranks[:], hot[t][:], ALU.mult))
                    link(nc.vector.tensor_reduce(keep["rank"][:, four, t:t + 1], work[:], AX.X, ALU.add))
                    link(nc.vector.scalar_tensor_tensor(out=place[:], in0=keep["index"][:, four, t], scalar=float(region),
                                                        in1=keep["rank"][:, four, t], op0=ALU.mult, op1=ALU.add))
                    if cap is None:
                        ins = nc.vector.tensor_copy(slot[h][:, :, t], place[:])
                        if t == top - 1:
                            ins.then_inc(s_slot, 1)
                        else:
                            link(ins)
                    else:
                        link(nc.vector.tensor_scalar(kept[:], keep["rank"][:, four, t], float(cap), None, ALU.is_lt))
                        link(nc.vector.tensor_tensor(keep["gate"][:, four, t], keep["gate"][:, four, t], kept[:], ALU.mult))
                        nc.vector.tensor_scalar(keep["slot"][:, four, t], place[:], float(E * cap - 1), None, ALU.min)
                        link(nc.vector.tensor_scalar(kept[:], kept[:], -1.0e6, 1.0e6, ALU.mult, ALU.add))
                        nc.vector.tensor_tensor(slot[h][:, :, t], place[:], kept[:], ALU.add).then_inc(s_slot, 1)
                return at[0]

            n_links = count_links(norm, top, cap)
            with dve.Fori(0, NQUAD // 2) as i:
                for h in range(2):
                    got = quad(2 * i + h, h, n_links)
                    assert got == n_links, (got, n_links)
            if cap is None:
                dve.wait_ge(s_rank, NQUAD + 1)
                nc.vector.tensor_copy(keep["count"][:], prk[:, 0:E]).then_inc(s_hot, 1)
                dve.wait_ge(s_hot, NQUAD + 1)
    release_semaphores(nc, sems)


def count_links(norm, top, cap):
    return (3 if norm else 0) + 2 + 3 + 2 + 1 + 1 + 2 + 3 * top + (top - 1 if cap is None else 3 * top)


def ffn_pass(nc, tag, src, dst, w, k, experts, tiles, width, tables=None, shared=False):
    E, F, NF, NT, W = experts, 512, 4, tiles, width
    NW = W // P
    sems = []
    with ExitStack() as ctx:
        def sb(name, shape, dt):
            return ctx.enter_context(nc.sbuf_tensor(f"{tag}_{name}", shape, dt))

        def sem(name):
            sems.append(nc.alloc_semaphore(f"{tag}_{name}"))
            return sems[-1]
        held = {e: sem(f"held_{e}") for e in ("sp", "pool", "dve")}

        def ps(name):
            return ctx.enter_context(nc.psum_tensor(f"{tag}_{name}", [P, 512], F32))
        ident = sb("ident", [P, P], F32)
        w1h, w1l = sb("w1h", [P, E * F], F16), sb("w1l", [P, E * F], F16)
        w2h, w2l = sb("w2h", [P, E * NF * D], F16), sb("w2l", [P, E * NF * D], F16)
        b1p = sb("b1p", [P, E * F], F16)
        ones = sb("ones", [P, W], F16)
        const = sb("const", [P, E * D], F32)
        stage = [sb(f"stage{i}", [P, F], F32) for i in range(4)]
        b1s = sb("b1s", [33, E * F], F32)
        b1t = sb("b1t", [33, E * F], F16)
        if shared:
            b1c, b1ch, b1cl = sb("b1c", [P, E * NF], F32), sb("b1ch", [P, E * NF], F16), sb("b1cl", [P, E * NF], F16)
            b2r, crow, ctot = sb("b2r", [1, E * D], F32), sb("crow", [1, E, D], F32), sb("ctot", [1, 1, D], F32)
            onesf = sb("onesf", [1, P], F32)
        NX = 4
        xg = [sb(f"xg{i}", [P, NW, D], F32) for i in range(NX)]
        xh, xl = [[sb(f"x{a}{i}", [P, W], F16) for i in range(2)] for a in "hl"]
        hh, hl = [[sb(f"h{a}{i}", [P, NF * W], F16) for i in range(2)] for a in "hl"]
        yo = [sb(f"yo{i}", [P, NW, D], F32) for i in range(2)]
        NH = NF * W // 512
        pT = ps("pT")
        pH = [[ps(f"pH{i}{j}") for j in range(NH)] for i in range(2)]
        pY = [ps(f"pY{i}") for i in range(2)]
        pC = pH[0][0], pH[1][0]
        s_c, s_st, s_wh, s_wl, s_b1, s_m, s_ready, s_k = (sem("const"), sem("stage"), sem("w_high"), sem("w_low"),
                                                         sem("b1"), sem("setup_mm"), sem("ready"), sem("setup"))
        s_x, s_T, s_xh, s_xl, s_H, s_hh, s_hl, s_Y, s_y, s_o = (
            sem("x_in"), sem("turned"), sem("x_high"), sem("x_low"), sem("hidden_ps"), sem("hidden_high"),
            sem("hidden_low"), sem("out_ps"), sem("out_sb"), sem("stored"))
        NS = 2 * E
        block = ctx.enter_context(nc.Block())

        def piece(n):
            e, second = divmod(n, 2)
            if second:
                return w["w2"][:, e * F:(e + 1) * F], w2h[:, e * F:(e + 1) * F], w2l[:, e * F:(e + 1) * F]
            return w["w1"][:, e * F:(e + 1) * F], w1h[:, e * F:(e + 1) * F], w1l[:, e * F:(e + 1) * F]

        nconst = 6 if shared else 4

        @block.sync
        def _(sp):
            sp.dma_start(ident[:], k["ident"]).then_inc(s_c, 16)
            for r in (0, 32):
                sp.dma_start(b1s[r:r + 1, :], w["b1"]).then_inc(s_c, 16)
            if shared:
                sp.dma_start(b1c[:], w["b1c"]).then_inc(s_c, 16)
                sp.dma_start(b2r[:], w["b2"]).then_inc(s_c, 16)
                sp.dma_start(onesf[:], k["onesf"]).then_inc(s_c, 16)
            else:
                sp.dma_start(const[:], w["b2"][0, :].partition_broadcast(P)).then_inc(s_c, 16)
            sp.wait_ge(s_c, 16 * nconst)
            for n in range(NS):
                if n >= 4:
                    sp.wait_ge(s_wl, n - 3)
                if n:
                    sp.wait_ge(s_st, 16 * n)
                sp.dma_start(stage[n % 4][:], piece(n)[0]).then_inc(s_st, 16)

            def load(j, i):
                if not (isinstance(j, int) and j < NX):
                    sp.wait_ge(s_T, j - NX + 1)
                if tables is None:
                    row = j * W
                else:
                    row = sp.value_load(tables["row"][0:1, bass.ds(j, 1)], min_val=0, max_val=src.shape[0] - W)
                if not (isinstance(j, int) and j == 0):
                    sp.wait_ge(s_x, 16 * j)
                sp.dma_start(xg[i][:], src[bass.ds(row, W), :].rearrange("(a p) d -> p a d", p=P)).then_inc(s_x, 16)

            def store(j, i):
                hold(sp, s_y, j + 1, held["sp"])
                if not (isinstance(j, int) and j == 0):
                    sp.wait_ge(s_o, 16 * j)
                sp.dma_start(dst[bass.ds(j * W, W), :].rearrange("(a p) d -> p a d", p=P), yo[i][:]).then_inc(s_o, 16)

            for j in range(NX):
                load(j, j)
            for j in range(4):
                store(j, j % 2)
                load(j + NX, j)
            with sp.Fori(1, (NT - NX) // 4) as i:
                for h in range(4):
                    store(4 * i + h, h % 2)
                    load(4 * i + (h + NX), h)
            for j in range(NT - NX, NT):
                store(j, j % 2)
            sp.wait_ge(s_o, 16 * NT)

        @block.gpsimd
        def _(pool):
            nc.gpsimd.memset(ones[:], 1.0).then_inc(s_k, 1)
            nc.gpsimd.memset(b1p[:], 0.0).then_inc(s_k, 1)

        @block.tensor
        def _(pe):
            pe.wait_ge(s_ready, 1)
            if shared:
                for e in range(E):
                    o = pC[e // 4][0:1, (e % 4) * D:(e % 4 + 1) * D]
                    for c in range(NF):
                        a = slice(e * NF + c, e * NF + c + 1)
                        v = slice((e * NF + c) * D, (e * NF + c + 1) * D)
                        nc.tensor.matmul(o, b1ch[:, a], w2l[:, v], start=(c == 0), stop=False)
                        nc.tensor.matmul(o, b1cl[:, a], w2h[:, v], start=False, stop=False)
                        mm = nc.tensor.matmul(o, b1ch[:, a], w2h[:, v], start=False, stop=(c == NF - 1))
                mm.then_inc(s_m, 1)
                pe.wait_ge(s_ready, 2)
                for t in range(2):
                    mm = nc.tensor.matmul(pC[t][:], onesf[:], crow[:, 4 * t:4 * t + 4, :].rearrange("p e d -> p (e d)"),
                                          start=True, stop=True)
                mm.then_inc(s_m, 1)
                pe.wait_ge(s_ready, 3)

            def turn(j, i):
                pe.wait_ge(s_x, 16 * j + 16)
                if not (isinstance(j, int) and j == 0):
                    pe.wait_ge(s_xl, j)
                for a in range(NW):
                    mm = nc.tensor.transpose(pT[:, a * P:(a + 1) * P], xg[i % NX][:, a, :], ident[:])
                mm.then_inc(s_T, 1)

            def expert(j):
                if tables is None:
                    return j
                return pe.value_load(tables["expert"][0:1, bass.ds(j, 1)], min_val=0, max_val=E - 1)

            def up(j, i):
                e = expert(j)
                pe.wait_ge(s_xl, j + 1)
                if not (isinstance(j, int) and j < 2):
                    pe.wait_ge(s_hl, j - 1)
                for c in range(NF):
                    at = c * W
                    o = pH[i][at // 512][:, at % 512:at % 512 + W]
                    v = bass.ds(e * F + c * P, P)
                    nc.tensor.matmul(o, b1p[:, v], ones[:], start=True, stop=False)
                    nc.tensor.matmul(o, w1l[:, v], xh[i][:], start=False, stop=False)
                    nc.tensor.matmul(o, w1h[:, v], xl[i][:], start=False, stop=False)
                    mm = nc.tensor.matmul(o, w1h[:, v], xh[i][:], start=False, stop=True)
                mm.then_inc(s_H, 1)
                return e

            def down(j, i, e=None):
                e = expert(j)
                pe.wait_ge(s_hl, j + 1)
                if not (isinstance(j, int) and j < 2):
                    pe.wait_ge(s_y, j - 1)
                for a in range(NW):
                    o = pY[i][:, a * D:(a + 1) * D]
                    for c in range(NF):
                        r = slice(c * W + a * P, c * W + a * P + P)
                        v = bass.ds((e * NF + c) * D, D)
                        nc.tensor.matmul(o, hh[i][:, r], w2l[:, v], start=(c == 0), stop=False)
                        nc.tensor.matmul(o, hl[i][:, r], w2h[:, v], start=False, stop=False)
                        mm = nc.tensor.matmul(o, hh[i][:, r], w2h[:, v], start=False, stop=(c == NF - 1))
                mm.then_inc(s_Y, 1)

            turn(0, 0)
            turn(1, 1)
            up(0, 0)
            for j in range(4):
                turn(j + 2, (j + 2) % 4)
                up(j + 1, (j + 1) % 2)
                down(j, j % 2)
            with pe.Fori(1, (NT - 4) // 4) as i:
                for h in range(4):
                    turn(4 * i + (h + 2), (h + 2) % 4)
                    up(4 * i + (h + 1), (h + 1) % 2)
                    down(4 * i + h, h % 2)
            for j in range(NT - 4, NT):
                if j + 2 < NT:
                    turn(j + 2, (j + 2) % 4)
                if j + 1 < NT:
                    up(j + 1, (j + 1) % 2)
                down(j, j % 2)

        @block.scalar
        def _(act):
            act.wait_ge(s_c, 16 * nconst)
            if shared:
                nc.scalar.activation(b1ch[:], b1c[:], ACT.Relu).then_inc(s_b1, 1)
            act.wait_ge(s_k, 2)
            nc.scalar.copy(b1p[0:1, :], b1s[0:1, :])
            nc.scalar.copy(b1t[32:33, :], b1s[32:33, :]).then_inc(s_b1, 1)
            for n in range(NS):
                act.wait_ge(s_st, 16 * n + 16)
                nc.scalar.copy(piece(n)[1], stage[n % 4][:]).then_inc(s_wh, 1)

            def tile(j, i):
                act.wait_ge(s_T, j + 1)
                if not (isinstance(j, int) and j < 2):
                    act.wait_ge(s_H, j - 1)
                nc.scalar.copy(xh[i][:], pT[:, 0:W]).then_inc(s_xh, 1)

            def hidden(j, i):
                act.wait_ge(s_H, j + 1)
                if not (isinstance(j, int) and j < 2):
                    act.wait_ge(s_Y, j - 1)
                for t in range(NH):
                    ins = nc.scalar.activation(hh[i][:, t * 512:(t + 1) * 512], pH[i][t][:], ACT.Relu)
                ins.then_inc(s_hh, 1)
            act.wait_ge(s_ready, 3 if shared else 1)
            tile(0, 0)
            tile(1, 1)
            hidden(0, 0)
            for j in range(2):
                tile(j + 2, j)
                hidden(j + 1, (j + 1) % 2)
            with act.Fori(1, (NT - 2) // 2) as i:
                for h in range(2):
                    tile(2 * i + (h + 2), h)
                    hidden(2 * i + (h + 1), (h + 1) % 2)
            hidden(NT - 1, (NT - 1) % 2)

        @block.vector
        def _(dve):
            dve.wait_ge(s_c, 16 * nconst)
            at = [0]

            def link(ins):
                at[0] += 1
                ins.then_inc(s_wl, 1)
                dve.wait_ge(s_wl, NS + at[0])
            dve.wait_ge(s_k, 2)
            for n in range(NS):
                dve.wait_ge(s_wh, n + 1)
                nc.vector.tensor_tensor(piece(n)[2], stage[n % 4][:], piece(n)[1], ALU.subtract).then_inc(s_wl, 1)
            dve.wait_ge(s_b1, 2 if shared else 1)
            link(nc.vector.tensor_tensor(b1p[32:33, :], b1s[32:33, :], b1t[32:33, :], ALU.subtract))
            if shared:
                link(nc.vector.scalar_tensor_tensor(out=b1cl[:], in0=b1c[:], scalar=0.0, in1=b1ch[:], op0=ALU.max,
                                                    op1=ALU.subtract))
            dve.sem_inc(s_ready, 1)
            if shared:
                dve.wait_ge(s_m, 1)
                b2v = b2r[:].rearrange("p (e d) -> p e d", e=E)
                for t in range(2):
                    link(nc.vector.tensor_tensor(crow[:, 4 * t:4 * t + 4, :],
                                                 pC[t][0:1, :].rearrange("p (e d) -> p e d", d=D),
                                                 b2v[:, 4 * t:4 * t + 4, :], ALU.add))
                link(nc.vector.tensor_reduce(ctot[:, 0, :], crow[:].rearrange("p e d -> p d e"), AX.X, ALU.add))
                link(nc.vector.tensor_tensor(crow[:], b2v, crow[:], ALU.subtract))
                link(nc.vector.tensor_tensor(crow[:], crow[:], ctot[:].to_broadcast([1, E, D]), ALU.add))
                dve.sem_inc(s_ready, 1)
                dve.wait_ge(s_m, 2)
                for t in range(2):
                    link(nc.vector.tensor_copy(const[:, 512 * t:512 * t + 512], pC[t][:]))
                dve.sem_inc(s_ready, 1)

            def tile(j, i):
                dve.wait_ge(s_xh, j + 1)
                nc.vector.tensor_tensor(xl[i][:], pT[:, 0:W], xh[i][:], ALU.subtract).then_inc(s_xl, 1)

            def hidden(j, i):
                dve.wait_ge(s_hh, j + 1)
                for t in range(NH):
                    c = slice(t * 512, (t + 1) * 512)
                    ins = nc.vector.scalar_tensor_tensor(out=hl[i][:, c], in0=pH[i][t][:], scalar=0.0, in1=hh[i][:, c],
                                                         op0=ALU.max, op1=ALU.subtract)
                ins.then_inc(s_hl, 1)

            def out(j, i):
                if tables is None:
                    e = j
                else:
                    e = dve.value_load(tables["expert"][0:1, bass.ds(j, 1)], min_val=0, max_val=E - 1)
                dve.wait_ge(s_Y, j + 1)
                if not (isinstance(j, int) and j < 2):
                    dve.wait_ge(s_o, 16 * (j - 1))
                for a in range(NW):
                    ins = nc.vector.tensor_tensor(yo[i][:, a, :], pY[i][:, a * D:(a + 1) * D], const[:, bass.ds(e * D, D)],
                                                  ALU.add)
                ins.then_inc(s_y, 1)
            tile(0, 0)
            tile(1, 1)
            hidden(0, 0)
            for j in range(2):
                tile(j + 2, j)
                hidden(j + 1, (j + 1) % 2)
                out(j, j)
            with dve.Fori(1, (NT - 2) // 2) as i:
                for h in range(2):
                    tile(2 * i + (h + 2), h)
                    hidden(2 * i + (h + 1), (h + 1) % 2)
                    out(2 * i + h, h)
            hidden(NT - 1, (NT - 1) % 2)
            out(NT - 2, 0)
            out(NT - 1, 1)
    release_semaphores(nc, sems)


def plan_pass(nc, tag, slots_dram, k, keep, experts, region, tiles):
    E, NT, NI = experts, tiles, S * B // P
    sems = []
    with ExitStack() as ctx:
        def sb(name, shape, dt):
            return ctx.enter_context(nc.sbuf_tensor(f"{tag}_{name}", shape, dt))

        def sem(name):
            sems.append(nc.alloc_semaphore(f"{tag}_{name}"))
            return sems[-1]
        held = {e: sem(f"held_{e}") for e in ("sp", "pool", "dve")}
        iota, steps = sb("iota", [P, 1, 1, E], F32), sb("steps", [P, 1, NI], F32)
        tile_no = sb("tile_no", [P, NT], F32)
        more = sb("more", [P, E, NI], F32)
        need, end, one = sb("need", [P, E], F32), sb("end", [P, E], F32), sb("one", [P, E], F32)
        past, used = sb("past", [P, NT, E], F32), sb("used", [P, NT, E], F32)
        te, tb = sb("te", [P, NT], F32), sb("tb", [P, NT], F32)
        pads, padi = sb("pads", [P, E], F32), sb("padi", [P, E], I32)
        hot = sb("hot", [P, B, 2, E], F32)
        base, zero = sb("base", [P, B, 2], F32), sb("zero", [P, 9, D], F32)
        s_c, s_k, s_pad, s_z = sem("const"), sem("step"), sem("padded"), sem("zeroed")
        block = ctx.enter_context(nc.Block())

        @block.sync
        def _(sp):
            for to, frm in ((iota[:, 0, 0, :], k["iota"][:, 0:E]), (steps[:, 0, :], k["steps"]), (tile_no[:], k["tile_no"])):
                sp.dma_start(to, frm).then_inc(s_c, 16)
            sp.wait_ge(s_z, 1)
            sp.dma_start(slots_dram[E * region:E * region + 9 * P, :].rearrange("(a p) d -> p a d", p=P),
                         zero[:]).then_inc(s_pad, 16)
            sp.wait_ge(s_z, 2)
            for e in range(E):
                row = sp.value_load(padi[0:1, e:e + 1], min_val=0, max_val=E * region - P)
                sp.dma_start(slots_dram[bass.ds(row, P), :], zero[:, 0, :]).then_inc(s_pad, 16)
            sp.wait_ge(s_pad, 16 * (E + 1))

        @block.vector
        def _(dve):
            at = [0]

            def link(ins):
                at[0] += 1
                ins.then_inc(s_k, 1)
                dve.wait_ge(s_k, at[0])
            nc.vector.memset(zero[:], 0.0).then_inc(s_z, 1)
            link(nc.vector.memset(one[:], 1.0))
            dve.wait_ge(s_c, 48)
            count = keep["count"]
            link(nc.vector.tensor_tensor(more[:], count[:].unsqueeze(2).to_broadcast([P, E, NI]),
                                         steps[:].to_broadcast([P, E, NI]), ALU.is_gt))
            link(nc.vector.tensor_reduce(need[:], more[:], AX.X, ALU.add))
            link(nc.vector.tensor_tensor_scan(end[:], one[:], need[:], 0.0, ALU.mult, ALU.add))
            link(nc.vector.tensor_tensor(past[:], tile_no[:].unsqueeze(2).to_broadcast([P, NT, E]),
                                         end[:].unsqueeze(1).to_broadcast([P, NT, E]), ALU.is_ge))
            link(nc.vector.tensor_tensor(used[:], past[:], need[:].unsqueeze(1).to_broadcast([P, NT, E]), ALU.mult))
            link(nc.vector.tensor_reduce(te[:], past[:], AX.X, ALU.add))
            link(nc.vector.tensor_reduce(tb[:], used[:], AX.X, ALU.add))
            link(nc.vector.tensor_tensor(tb[:], tile_no[:], tb[:], ALU.subtract))
            link(nc.vector.tensor_scalar(tb[:], tb[:], float(P), None, ALU.mult))
            link(nc.vector.scalar_tensor_tensor(out=tb[:], in0=te[:], scalar=float(region), in1=tb[:], op0=ALU.mult,
                                                op1=ALU.add))
            nc.vector.tensor_copy(keep["tile_row"][:], tb[:])
            nc.vector.tensor_scalar(keep["tile_expert"][:], te[:], float(E - 1), None, ALU.min)
            link(nc.vector.scalar_tensor_tensor(out=pads[:], in0=iota[:, 0, 0, :], scalar=float(region), in1=count[:],
                                                op0=ALU.mult, op1=ALU.add))
            nc.vector.tensor_copy(padi[:], pads[:]).then_inc(s_z, 1)
            link(nc.vector.tensor_tensor(end[:], end[:], need[:], ALU.subtract))
            link(nc.vector.tensor_scalar(end[:], end[:], float(P), None, ALU.mult))
            link(nc.vector.tensor_tensor(hot[:], keep["index"][:].unsqueeze(3).to_broadcast([P, B, 2, E]),
                                         iota[:].to_broadcast([P, B, 2, E]), ALU.is_equal))
            for t in range(2):
                ins = nc.vector.tensor_tensor(hot[:, :, t, :], hot[:, :, t, :], end[:].unsqueeze(1).to_broadcast([P, B, E]),
                                              ALU.mult)
            link(ins)
            link(nc.vector.tensor_reduce(base[:], hot[:], AX.X, ALU.add))
            nc.vector.tensor_tensor(keep["slot"][:], base[:], keep["rank"][:], ALU.add).then_inc(s_k, 1)
    release_semaphores(nc, sems)


def combine_pass(nc, tag, src, results, dst, k, keep, top, twice=False):
    sems = []
    with ExitStack() as ctx:
        def sb(name, shape, dt):
            return ctx.enter_context(nc.sbuf_tensor(f"{tag}_{name}", shape, dt))

        def sem(name):
            sems.append(nc.alloc_semaphore(f"{tag}_{name}"))
            return sems[-1]
        held = {e: sem(f"held_{e}") for e in ("sp", "pool", "dve")}
        x = [sb(f"x{i}", [P, QUAD, D], F32) for i in range(2)]
        got = [sb(f"got{i}", [P, QUAD, top, D], F32) for i in range(2)]
        out = [sb(f"out{i}", [P, QUAD, D], F32) for i in range(2)]
        expo4 = sb("expo4", [P, QUAD], F32)
        stats, mv = sb("stats", [P, QUAD, 6], F32), sb("mv", [P, QUAD, 2], F32)
        veps, rstd = sb("veps", [P, QUAD], F32), sb("rstd", [P, QUAD], F32)
        s_c, s_x, s_got, s_mv, s_r, s_k, s_out, s_st = (sem("const"), sem("x_in"), sem("gathered"), sem("variance"),
                                                  sem("rstd"), sem("step"), sem("normed"), sem("stored"))
        block = ctx.enter_context(nc.Block())

        @block.sync
        def _(sp):
            sp.dma_start(expo4[:], k["expo4"]).then_inc(s_c, 16)

            def load(n, i):
                sp.dma_start(x[i][:], src[bass.ds(4 * n, QUAD)].rearrange("b t d -> t b d")).then_inc(s_x, 16)
                hold(sp, s_x, 16 * n + 16, held["sp"])
            load(0, 0)
            load(1, 1)

            def store(n, i):
                sp.wait_ge(s_out, n + 1)
                sp.dma_start(dst[bass.ds(4 * n, QUAD)].rearrange("b t d -> t b d"), out[i][:]).then_inc(s_st, 16)
                sp.wait_ge(s_st, 16 * n + 16)
            with sp.Fori(0, NQUAD // 2 - 1) as i:
                for h in range(2):
                    store(2 * i + h, h)
                    load(2 * i + (h + 2), h)
            for h in range(2):
                store(NQUAD - 2 + h, h)

        @block.gpsimd
        def _(pool):
            def gather(n, i):
                for b in range(QUAD):
                    for t in range(top):
                        pool.indirect_dma_start(got[i][:, b, t, :], None, results,
                                                bass.IndirectOffsetOnAxis(ap=keep["slot"][:, 4 * n + b, t:t + 1], axis=0))\
                            .then_inc(s_got, 16)
            pool.wait_ge(s_c, 16)
            for n in range(NQUAD):
                if n >= 2:
                    pool.wait_ge(s_out, n - 1)
                gather(n, n % 2)
                pool.wait_ge(s_mv, n + 1)
                nc.gpsimd.tensor_scalar(veps[:], mv[:, :, 1], LN_EPS, None, ALU.add).then_inc(s_r, 1)
                pool.wait_ge(s_r, 2 * n + 1)
                nc.gpsimd.tensor_tensor(rstd[:], veps[:], expo4[:], ALU.pow).then_inc(s_r, 1)

        @block.vector
        def _(dve):
            links = top + 1 + (1 if twice else 0)

            def quad(n, i):
                at = [0]

                def link(ins):
                    at[0] += 1
                    ins.then_inc(s_k, 1)
                    hold(dve, s_k, links * n + at[0], held["dve"])
                dve.wait_ge(s_x, 16 * n + 16)
                dve.wait_ge(s_got, 16 * QUAD * top * (n + 1))
                for t in range(top):
                    for b in range(QUAD):
                        gate = keep["gate"][:, bass.ds(4 * n + b, 1), t]
                        sofar = x[i][:, b, :] if t == 0 else got[i][:, b, 0, :]
                        to = got[i][:, b, 0, :] if t < top - 1 or twice else x[i][:, b, :]
                        ins = nc.vector.scalar_tensor_tensor(out=to, in0=got[i][:, b, t, :], scalar=gate, in1=sofar,
                                                             op0=ALU.mult, op1=ALU.add)
                    link(ins)
                if twice:
                    link(nc.vector.tensor_tensor(x[i][:], x[i][:], got[i][:, :, 0, :], ALU.add))
                for b in range(QUAD):
                    ins = nc.vector.bn_stats(stats[:, b, :], x[i][:, b, :])
                link(ins)
                for b in range(QUAD):
                    ins = nc.vector.bn_aggr(mv[:, b, :], stats[:, b, :])
                ins.then_inc(s_mv, 1)
                dve.wait_ge(s_mv, n + 1)
                dve.wait_ge(s_r, 2 * n + 2)
                if not (isinstance(n, int) and n < 2):
                    dve.wait_ge(s_st, 16 * (n - 1))
                for b in range(QUAD):
                    ins = nc.vector.tensor_scalar(out[i][:, b, :], x[i][:, b, :], mv[:, b, 0:1], rstd[:, b:b + 1],
                                                  ALU.subtract, ALU.mult)
                ins.then_inc(s_out, 1)
            quad(0, 0)
            quad(1, 1)
            with dve.Fori(1, NQUAD // 2) as i:
                for h in range(2):
                    quad(2 * i + h, h)
    release_semaphores(nc, sems)


def position_attention_pass(nc, tag, src, dst, k):
    NT = S // QUAD
    scale = float(D) ** -0.5
    sems = []
    with ExitStack() as ctx:
        def sb(name, shape, dt):
            return ctx.enter_context(nc.sbuf_tensor(f"{tag}_{name}", shape, dt))

        def sem(name):
            sems.append(nc.alloc_semaphore(f"{tag}_{name}"))
            return sems[-1]
        held = {e: sem(f"held_{e}") for e in ("sp", "pool", "dve")}
        ident, identb, blocks = sb("ident", [P, P], F32), sb("identb", [P, P], BF16), sb("blocks", [P, P], BF16)
        expo = sb("expo", [P, 2], F32)
        x = [sb(f"x{i}", [P, D], F32) for i in range(4)]
        xT = [sb(f"xT{i}", [P, P], F32) for i in range(2)]
        top, bias = [sb(f"top{i}", [P, 1], F32) for i in range(2)], [sb(f"bias{i}", [P, 1], F32) for i in range(2)]
        total, recip = [sb(f"total{i}", [P, 1], F32) for i in range(2)], [sb(f"recip{i}", [P, 1], F32) for i in range(2)]
        p, pT = [sb(f"p{i}", [P, P], F32) for i in range(2)], [sb(f"pt{i}", [P, P], F32) for i in range(2)]
        y = [sb(f"y{i}", [P, D], F32) for i in range(2)]
        out = [sb(f"out{i}", [P, D], F32) for i in range(2)]
        stats, mv = [sb(f"stats{i}", [P, 6], F32) for i in range(2)], [sb(f"mv{i}", [P, 2], F32) for i in range(2)]
        veps, rstd = [sb(f"veps{i}", [P, 1], F32) for i in range(2)], [sb(f"rstd{i}", [P, 1], F32) for i in range(2)]
        b_ = [[ctx.enter_context(nc.psum_tensor(f"{tag}_{n}{i}", [P, 512], F32)) for i in range(2)]
              for n in ("xTp", "sc", "pTp", "yp")]
        xTp, sc, pTp, yp = b_
        s_c, s_x, s_T, s_Ts, s_S, s_b, s_e, s_P, s_Ps, s_Y, s_y, s_mv, s_r, s_o, s_st, s_k, s_q = (
            sem(n) for n in ("const", "x_in", "turned", "turned_sb", "scores", "bias", "exp", "p_turned", "p_turned_sb",
                             "out_ps", "summed", "variance", "rstd", "normed", "stored", "step", "sum_step"))
        block = ctx.enter_context(nc.Block())

        sem_held = held

        def late(eng, s, j, back, inc=1, held=None):
            if not (isinstance(j, int) and j < back):
                if held:
                    hold(eng, s, inc * (j - (back - 1)), sem_held[held])
                else:
                    eng.wait_ge(s, inc * (j - (back - 1)))

        @block.sync
        def _(sp):
            for to, frm in ((ident[:], k["ident"]), (identb[:], k["ident4"][:, 0:P]), (blocks[:], k["blocks"]), (expo[:], k["expo"])):
                sp.dma_start(to, frm).then_inc(s_c, 16)

            by_pos = src.rearrange("b t d -> t b d")
            to_pos = dst.rearrange("b t d -> t b d")

            def load(j, q):
                late(sp, s_y, j, 4)
                if not (isinstance(j, int) and j == 0):
                    sp.wait_ge(s_x, 64 * j)
                for a in range(QUAD):
                    sp.dma_start(x[q][32 * a:32 * a + 32, :], by_pos[bass.ds(4 * j + a, 1)].rearrange("t b d -> (t b) d"))\
                      .then_inc(s_x, 16)

            def store(j, i):
                hold(sp, s_o, j + 1, held["sp"])
                if not (isinstance(j, int) and j == 0):
                    sp.wait_ge(s_st, 64 * j)
                for a in range(QUAD):
                    sp.dma_start(to_pos[bass.ds(4 * j + a, 1)].rearrange("t b d -> (t b) d"), out[i][32 * a:32 * a + 32, :])\
                      .then_inc(s_st, 16)
            for j in range(4):
                load(j, j)
            for j in range(4):
                load(j + 4, j)
                store(j, j % 2)
            with sp.Fori(1, NT // 4 - 1) as i:
                for h in range(4):
                    load(4 * i + (h + 4), h)
                    store(4 * i + h, h % 2)
            for j in range(NT - 4, NT):
                store(j, j % 2)
            sp.wait_ge(s_st, 64 * NT)

        def skewed4(eng, stages):
            deep = max(lag for lag, _ in stages)
            for j in range(8):
                for lag, f in stages:
                    if j - lag >= 0:
                        f(j - lag, (j - lag) % 4)
            with eng.Fori(1, NT // 4 - 1) as i:
                for h in range(4):
                    for lag, f in stages:
                        f(4 * i + (4 + h - lag), (4 + h - lag) % 4)
            for j in range(NT, NT + deep):
                for lag, f in stages:
                    if j - lag < NT:
                        f(j - lag, (j - lag) % 4)

        @block.tensor
        def _(pe):
            pe.wait_ge(s_c, 64)

            def turn(j, q):
                i = q % 2
                pe.wait_ge(s_x, 64 * j + 64)
                late(pe, s_Ts, j, 2)
                nc.tensor.transpose(xTp[i][:, 0:P], x[q][:], ident[:]).then_inc(s_T, 1)

            def score(j, q):
                i = q % 2
                pe.wait_ge(s_Ts, j + 1)
                late(pe, s_e, j, 2)
                nc.tensor.matmul(sc[i][:, 0:P], identb[:], blocks[:], start=True, stop=False)
                nc.tensor.matmul(sc[i][:, 0:P], xT[i][:], xT[i][:], start=False, stop=True).then_inc(s_S, 1)

            def turn_p(j, q):
                i = q % 2
                pe.wait_ge(s_e, j + 1)
                late(pe, s_Ps, j, 2)
                nc.tensor.transpose(pTp[i][:, 0:P], p[i][:], ident[:]).then_inc(s_P, 1)

            def attend(j, q):
                i = q % 2
                pe.wait_ge(s_Ps, j + 1)
                late(pe, s_y, j, 2)
                nc.tensor.matmul(yp[i][:, 0:D], pT[i][:], x[q][:], start=True, stop=True).then_inc(s_Y, 1)
            skewed4(pe, [(0, turn), (1, score), (2, turn_p), (3, attend)])

        @block.scalar
        def _(act):
            def turned(j, q):
                i = q % 2
                act.wait_ge(s_T, j + 1)
                late(act, s_S, j, 2)
                nc.scalar.copy(xT[i][:], xTp[i][:, 0:P]).then_inc(s_Ts, 1)

            def exp(j, q):
                i = q % 2
                act.wait_ge(s_b, j + 1)
                late(act, s_P, j, 2)
                late(act, s_y, j, 2)
                nc.scalar.activation(p[i][:], sc[i][:, 0:P], ACT.Exp, scale=scale, bias=bias[i][:],
                                     accum_out=total[i][:]).then_inc(s_e, 1)

            def p_turned(j, q):
                i = q % 2
                act.wait_ge(s_P, j + 1)
                late(act, s_Y, j, 2)
                nc.scalar.copy(pT[i][:], pTp[i][:, 0:P]).then_inc(s_Ps, 1)
            skewed4(act, [(0, turned), (1, exp), (2, p_turned)])

        @block.gpsimd
        def _(pool):
            pool.wait_ge(s_c, 64)

            def root(j, q):
                i = q % 2
                hold(pool, s_mv, j + 1, held["pool"])
                late(pool, s_o, j, 2, held="pool")
                nc.gpsimd.tensor_scalar(veps[i][:], mv[i][:, 1:2], LN_EPS, None, ALU.add).then_inc(s_r, 1)
                pool.wait_ge(s_r, 2 * j + 1)
                nc.gpsimd.tensor_tensor(rstd[i][:], veps[i][:], expo[:, 0:1], ALU.pow).then_inc(s_r, 1)
            skewed4(pool, [(0, root)])

        @block.vector
        def _(dve):
            def peak(j, q):
                i = q % 2
                dve.wait_ge(s_S, j + 1)
                nc.vector.tensor_reduce(top[i][:], sc[i][:, 0:P], AX.X, ALU.max, negate=True).then_inc(s_k, 1)
                dve.wait_ge(s_k, j + 1)
                late(dve, s_e, j, 2)
                nc.vector.tensor_scalar(bias[i][:], top[i][:], scale, None, ALU.mult).then_inc(s_b, 1)

            def add(j, q):
                i = q % 2
                dve.wait_ge(s_Y, j + 1)
                nc.vector.reciprocal(recip[i][:], total[i][:]).then_inc(s_q, 1)
                dve.wait_ge(s_q, 2 * j + 1)
                late(dve, s_o, j, 2)
                nc.vector.scalar_tensor_tensor(out=y[i][:], in0=yp[i][:, 0:D], scalar=recip[i][:], in1=x[q][:],
                                               op0=ALU.mult, op1=ALU.add).then_inc(s_y, 1)
                dve.wait_ge(s_y, j + 1)
                nc.vector.bn_stats(stats[i][:], y[i][:]).then_inc(s_q, 1)
                hold(dve, s_q, 2 * j + 2, held["dve"])
                nc.vector.bn_aggr(mv[i][:], stats[i][:]).then_inc(s_mv, 1)

            def norm(j, q):
                i = q % 2
                dve.wait_ge(s_r, 2 * j + 2)
                late(dve, s_st, j, 2, 64)
                nc.vector.tensor_scalar(out[i][:], y[i][:], mv[i][:, 0:1], rstd[i][:], ALU.subtract,
                                        ALU.mult).then_inc(s_o, 1)
            skewed4(dve, [(0, peak), (2, add), (3, norm)])
    release_semaphores(nc, sems)


def decoder_kernel(nc, out, **a):
    k = {n[2:]: v for n, v in a.items() if n.startswith("c_")}

    def group(tag):
        return {n[len(tag):]: v for n, v in a.items() if n.startswith(tag)}

    def rows(name, shape=(B, S, D)):
        return nc.dram_tensor(name, shape, F32, kind="Internal").ap()
    x1, x2, x3, x4, x5 = (rows(f"after{i}") for i in range(1, 6))
    slots0, results0 = rows("slots0", (E0 * REGION0 + 9 * P, D)), rows("results0", (TILES0 * P, D))
    slots1, results1 = rows("slots1", (E1 * CAP1, D)), rows("results1", (E1 * CAP1, D))
    cross = float(8) ** -0.5

    attention_pass(nc, "own", a["x"], x1, group("own_"), k | {"sel": k["sel_own"]}, scale=0.125)
    attention_pass(nc, "cross0", x1, x2, group("cross0_"), k | {"sel": k["sel_cross"]}, ctx_src=a["ctx"],
                   mask_src=a["mask"], scale=cross)
    with ExitStack() as ctx:
        def sb(name, shape, dt):
            return ctx.enter_context(nc.sbuf_tensor(f"keep0_{name}", shape, dt))
        keep = {"gate": sb("gate", [P, B, 2], F32), "index": sb("index", [P, B, 2], F32),
                "rank": sb("rank", [P, B, 2], F32), "slot": sb("slot", [P, B, 2], U32), "count": sb("count", [P, E0], F32),
                "tile_row": sb("tile_row", [P, TILES0], I32), "tile_expert": sb("tile_expert", [P, TILES0], I32)}
        route_pass(nc, "route0", x2, slots0, group("route0_"), k, keep, E0, 2, REGION0, norm=True)
        plan_pass(nc, "plan0", slots0, k, keep, E0, REGION0, TILES0)
        ffn_pass(nc, "ffn0", slots0, results0, group("ffn0_"), k, E0, TILES0, P,
                 tables={"row": keep["tile_row"], "expert": keep["tile_expert"]}, shared=True)
        combine_pass(nc, "combine0", x2, results0, x3, k, keep, 2, twice=True)
    position_attention_pass(nc, "position", x3, x4, k)
    attention_pass(nc, "cross1", x4, x5, group("cross1_"), k | {"sel": k["sel_cross"]}, ctx_src=a["ctx"], scale=cross)
    with ExitStack() as ctx:
        def sb(name, shape, dt):
            return ctx.enter_context(nc.sbuf_tensor(f"keep1_{name}", shape, dt))
        keep = {"gate": sb("gate", [P, B, 1], F32), "index": sb("index", [P, B, 1], F32),
                "rank": sb("rank", [P, B, 1], F32), "slot": sb("slot", [P, B, 1], U32)}
        blank = sb("blank", [P, 2 * D], F32)
        route_pass(nc, "route1", x5, slots1, group("route1_"), k, keep, E1, 1, CAP1, cap=CAP1, zeros=(blank, slots1))
        ffn_pass(nc, "ffn1", slots1, results1, group("ffn1_"), k, E1, E1, CAP1)
        combine_pass(nc, "combine1", x5, results1, out, k, keep, 1)



def constants():
    import numpy as np
    bf = mybir.dt.np(BF16)
    c = {"ident": np.eye(P, dtype=np.float32), "ident4": np.tile(np.eye(P, dtype=bf), (1, QUAD))}
    c["causal4"] = np.tile(np.triu(np.full((P, P), -1e30, np.float32), 1), (1, QUAD)).astype(bf)
    dh = 64
    theta = np.float32(10000.0) ** (np.arange(0, dh, 2, dtype=np.float32) / np.float32(dh))
    freqs = np.arange(S, dtype=np.float32)[:, None] * (np.float32(1.0) / theta)[None, :]
    emb = np.concatenate([freqs, freqs], axis=-1)
    sign = np.where(np.arange(dh) % 2 == 0, np.float32(-1), np.float32(1))
    c["cos"] = np.ascontiguousarray(np.tile(np.cos(emb).T.astype(np.float32), (2, QUAD)))
    c["sin"] = np.ascontiguousarray(np.tile((np.sin(emb) * sign).T.astype(np.float32), (2, QUAD)))
    own = np.zeros((P, 2, HU, P), np.float32)
    cross = np.zeros((P, 1, HU, P), np.float32)
    for u in range(UNITS):
        for part in range(NSPLIT):
            for j in range(HU):
                own[32 * u + HU * part + j, u % 2, j, :] = 1
                cross[32 * u + HU * part + j, 0, j, :] = 1
    c["sel_own"], c["sel_cross"] = own.astype(bf), cross.astype(bf)
    low = np.zeros((P, 2), np.float32)
    for u in range(UNITS):
        low[32 * u + 16:32 * u + 24, 0] = 1
        low[32 * u + 8:32 * u + 16, 1] = 1
    c["low_rows"] = low
    c["expo"] = np.full((P, 2), -0.5, np.float32)
    c["expo4"] = np.full((P, QUAD), -0.5, np.float32)
    c["below"] = np.triu(np.ones((P, P), np.float32), 1).astype(bf)
    c["ones"] = np.ones((P, P), bf)
    c["onesf"] = np.ones((1, P), np.float32)
    c["iota"] = np.tile(np.arange(16, dtype=np.float32), (P, 1))
    c["steps"] = np.tile(np.arange(B, dtype=np.float32) * P, (P, 1))
    c["tile_no"] = np.tile(np.arange(TILES0, dtype=np.float32), (P, 1))
    at = np.arange(P) // B
    c["blocks"] = np.where(at[:, None] == at[None, :], np.float32(0), np.float32(-1e30)).astype(bf)
    return c


def rows_own(t):
    import numpy as np
    out = np.zeros((P, 8) + t.shape[1:], t.dtype)
    for h in range(H):
        g, j = divmod(h, HU)
        out[64 * (g % 2):64 * (g % 2) + 64, 4 * (g // 2) + j] = t[64 * h:64 * h + 64]
    return out


def rows_cross(t):
    import numpy as np
    out = np.zeros((P, 4) + t.shape[1:], t.dtype)
    for h in range(H):
        g, j = divmod(h, HU)
        for r in range(3):
            out[32 * g + 8 * r:32 * g + 8 * r + 8, j] = t[8 * h:8 * h + 8]
    return out


def swap_pairs(t):
    import numpy as np
    return np.ascontiguousarray(t.reshape((-1, 2) + t.shape[1:])[:, ::-1].reshape(t.shape))


def attention_layout(own, wq, bq, wk, bk, wv, bv, wo, bo):
    import numpy as np
    rows = rows_own if own else rows_cross
    cols = lambda t: np.ascontiguousarray(rows(t).transpose(2, 1, 0).reshape(P, -1))
    no = wo.shape[1] // P
    r = {"q": cols(wq), "k": cols(wk), "v": np.ascontiguousarray(wv.T),
         "o": np.ascontiguousarray(wo.T.reshape(no, P, D).transpose(1, 0, 2).reshape(P, no * D)),
         "vbias": np.ascontiguousarray(bv.reshape(no, P).T), "obias": bo}
    b = [rows(t) for t in ((bq, swap_pairs(bq), bk, swap_pairs(bk)) if own else (bq, bk))]
    r["bias"] = np.ascontiguousarray(np.stack(b, axis=1))
    if own:
        r["qs"], r["ks"] = cols(swap_pairs(wq)), cols(swap_pairs(wk))
    return r


def ffn_layout(w1, b1, w2, b2):
    import numpy as np
    e = w1.shape[0]
    return {"w1": np.ascontiguousarray(w1.transpose(1, 0, 2).reshape(P, e * F)),
            "w2": np.ascontiguousarray(w2.reshape(e, F // P, P, D).transpose(2, 0, 1, 3).reshape(P, -1)),
            "b1": np.ascontiguousarray(b1.reshape(1, -1)), "b2": np.ascontiguousarray(b2.reshape(1, -1)),
            "b1c": np.ascontiguousarray(b1.reshape(e, F // P, P).transpose(2, 0, 1).reshape(P, -1))}


def lay_out(inputs):
    import numpy as np
    f = {n: np.asarray(v) for n, v in inputs.items()}
    t = lambda v: np.ascontiguousarray(v.T)
    get = lambda tag, names: [f[f"{tag}_{n}"] for n in names]
    own = attention_layout(True, *get("L0_attn", ("wq", "bq", "wk", "bk", "wv", "bv", "wo", "bo")))
    cross0 = attention_layout(False, *[t(v) if v.ndim == 2 else v for v in
                                       get("L0_xattn", ("Wq", "bq", "Wk", "bk", "Wv", "bv", "Wo", "bo"))])
    cross1 = attention_layout(False, *get("L1_xattn", ("wq", "bq", "wk", "bk", "wv", "bv", "wo", "bo")))
    ffn0 = ffn_layout(*get("L0_ffn", ("W1", "b1", "W2", "b2")))
    ffn1 = ffn_layout(*get("L1_ffn", ("W1", "b1", "W2", "b2")))
    del ffn1["b1c"]
    route0 = {"wr": f["L0_ffn_Wr"], "br": f["L0_ffn_br"], "gamma": f["L0_ffn_gamma"], "beta": f["L0_ffn_beta"]}
    route1 = {"wr": f["L1_ffn_Wg"], "br": f["L1_ffn_bg"]}
    arrays = {"x": f["x"], "ctx": f["ctx_1024"], "mask": f["mask_BxSxS2_bf0"]}
    for tag, group in (("own", own), ("cross0", cross0), ("cross1", cross1), ("ffn0", ffn0), ("ffn1", ffn1),
                       ("route0", route0), ("route1", route1), ("c", constants())):
        arrays |= {f"{tag}_{n}": np.ascontiguousarray(v) for n, v in group.items()}
    return arrays


def kernel(**inputs):
    import numpy as np
    import concourse.bacc as bacc
    from concourse.bass_utils import run_bass_kernel_spmd

    nc = bacc.Bacc("TRN2", target_bir_lowering=False, num_devices=1)
    arrays = lay_out(inputs)
    args = {n: nc.dram_tensor(f"in_{n}", v.shape, mybir.dt.from_np(v.dtype), kind="ExternalInput").ap()
            for n, v in arrays.items()}
    out = nc.dram_tensor("out_0", (B, S, D), F32, kind="ExternalOutput").ap()
    decoder_kernel(nc, out, **args)
    r = run_bass_kernel_spmd(nc, [{f"in_{n}": v for n, v in arrays.items()}], core_ids=[0])
    return r.results[0]["out_0"]
```

```python
import concourse.bass as bass
from concourse import mybir
from contextlib import ExitStack

F32 = mybir.dt.float32
F16 = mybir.dt.float16
BF16 = mybir.dt.bfloat16
U32 = mybir.dt.uint32
I32 = mybir.dt.int32
U8 = mybir.dt.uint8
ALU = mybir.AluOpType
ACT = mybir.ActivationFunctionType
AX = mybir.AxisListType

P = 128
B = 32
S = 128
D = 128
H = 16
QUAD = 4
NQUAD = B // QUAD
UNITS = 4
HU = H // UNITS
LN_EPS = 1e-5
E0, E1 = 8, 16
F = 512
CAP1 = S * B // E1
REGION0 = S * B + P
TILES0 = 2 * S * B // P + E0
NSPLIT = 3


def hold(eng, s, value, held):
    eng.wait_ge(s, value)
    if not isinstance(value, int):
        eng.sem_inc(held, 1)


def release_semaphores(nc, sems):
    nc.clear_and_free_semaphores(sems)
    nc.all_engine_barrier()


def attention_pass(nc, tag, src, dst, w, k, ctx_src=None, mask_src=None, scale=1.0):
    own = ctx_src is None
    masked = own or mask_src is not None
    DH = 64 if own else 8
    DV = DH + 1
    NC = 8 if own else 4
    NP = 20 if own else 9
    NQK = 2 * NC
    NST = 3

    sems = []
    with ExitStack() as ctx:
        def sb(name, shape, dt):
            return ctx.enter_context(nc.sbuf_tensor(f"{tag}_{name}", shape, dt))

        def sem(name):
            sems.append(nc.alloc_semaphore(f"{tag}_{name}"))
            return sems[-1]
        held = {e: sem(f"held_{e}") for e in ("sp", "pool", "dve")}

        ident = sb("ident", [P, P], F32)
        ident4 = sb("ident4", [P, QUAD * P], BF16)
        NSEL = 2 if own else 1
        sel = sb("sel", [P, NSEL, HU, P], BF16)
        if own:
            addmask = sb("addmask", [P, 1, QUAD * P], BF16)
            cos = sb("cos", [P, QUAD * S], F32)
            sin = sb("sin", [P, QUAD * S], F32)
        elif masked:
            rawmask = sb("rawmask", [P, QUAD, P], U8)
            addmask = [sb(f"addmask{i}", [P, QUAD, P], BF16) for i in range(2)]
        WN = {"q": NC * P, "k": NC * P, "v": H * DH, "o": (H * DH // P) * D}
        if own:
            WN |= {"qs": NC * P, "ks": NC * P}
        names = ["q", "qs", "k", "ks", "v", "o"] if own else ["q", "k", "v", "o"]
        wh = {n: sb(f"w{n}h", [P, WN[n]], F16) for n in names}
        wl = {n: sb(f"w{n}l", [P, WN[n]], F16) for n in names}
        stage = [sb(f"stage{i}", [P, max(WN.values())], F32) for i in range(NST)]
        bias = sb("bias", [P, 4 if own else 2, NC], F32)
        if not own:
            low_rows = sb("low_rows", [P, 2], F32)
            low_bias = sb("low_bias", [P, 2, NC], F32)
        vbias = sb("vbias", [P, H * DH // P], F32)
        vbias_b = sb("vbias_b", [P, H * DH // P, P], F32)
        obias = sb("obias", [P, D], F32)
        obias4 = sb("obias4", [P, QUAD, D], F32)
        expo = sb("expo", [P, 2], F32)

        xin = [sb(f"xin{i}", [P, QUAD, D], F32) for i in range(2)]
        xres = [sb(f"xres{i}", [P, QUAD, D], F32) for i in range(2)]
        xout = [sb(f"xout{i}", [P, QUAD, D], F32) for i in range(2)]
        xh, xl = sb("xh", [P, QUAD * S], F16), sb("xl", [P, QUAD * S], F16)
        if own:
            ch, cl = xh, xl
            rot = [[sb(f"rot{i}{j}", [P, QUAD * S], F32) for j in range(2)] for i in range(2)]
            full = [sb(f"full{i}", [P, QUAD * S], F32) for i in range(2)]
            qkh = [[sb(f"qkh{i}{j}", [P, NC, QUAD * S], F16) for j in range(2)] for i in range(2)]
            qkl = [[sb(f"qkl{i}{j}", [P, NC, QUAD * S], F16) for j in range(2)] for i in range(2)]
        else:
            cin = [sb(f"cin{i}", [P, QUAD, D], F32) for i in range(2)]
            ch, cl = sb("ch", [P, QUAD * S], F16), sb("cl", [P, QUAD * S], F16)
            high = [sb(f"high{i}", [P, QUAD * S], F16) for i in range(2)]
            qks = [[sb(f"qks{i}{j}", [P, NC, QUAD * S], F16) for j in range(2)] for i in range(2)]
        vh = [sb(f"vh{i}", [P, QUAD, H, DV], F16) for i in range(2)]
        vl = [sb(f"vl{i}", [P, QUAD, H, DV], F16) for i in range(2)]
        negmax = [sb(f"negmax{i}", [P, H], F32) for i in range(2)]
        rest = [sb(f"rest{i}", [P, H], F32) for i in range(2)]
        max3 = [sb(f"max3{i}", [P, UNITS, 32], BF16) for i in range(2)]
        maxT = [sb(f"maxT{i}", [P, P], BF16) for i in range(2)]
        pf = [sb(f"pf{i}", [P, HU * P], F32) for i in range(2)]
        ph = [sb(f"ph{i}", [P, HU * P], F16) for i in range(UNITS)]
        pl = [sb(f"pl{i}", [P, HU * P], F16) for i in range(UNITS)]
        NA = HU if own else H
        recip = sb("recip", [P, NA], F32)
        att = [sb(f"att{i}", [P, NA, DH], F32) for i in range(2)]
        attTh = sb("attTh", [P, H * DH // P, P], F16)
        attTl = sb("attTl", [P, H * DH // P, P], F16)
        ysum = sb("ysum", [P, D], F32)
        stats, mv = sb("stats", [P, 6], F32), sb("mv", [P, 2], F32)
        veps, rstd = sb("veps", [P, 1], F32), sb("rstd", [P, 1], F32)

        def ps(name):
            return ctx.enter_context(nc.psum_tensor(f"{tag}_{name}", [P, 512], F32))
        scp = [ps("scores0"), ps("scores1")]
        stp = [ps("scoresT0"), ps("scoresT1")]
        prj = [ps("proj0"), ps("proj1")]
        avp = ps("attended")
        msc = ps("misc")

        s_const, s_wh, s_wl = sem("const"), sem("w_high"), sem("w_low")
        s_stage = [sem(f"stage{i}") for i in range(NST)]
        s_vb, s_obp, s_ready = sem("vbias_b"), sem("obias_ps"), sem("setup_done")
        s_xin, s_cin, s_min = sem("x_in"), sem("ctx_in"), sem("mask_in")
        s_misc, s_misc_hi, s_misc_free = sem("misc_ps"), sem("misc_high"), sem("misc_free")
        s_proj, s_proj_hi, s_proj_free = sem("proj_ps"), sem("proj_high"), sem("proj_free")
        s_full, s_qkhi, s_qklo = sem("rope_sum"), sem("qk_high"), sem("qk_low")
        s_scores, s_max, s_split = sem("scores_ps"), sem("max_done"), sem("max_split")
        s_link, s_maxT = sem("pool_link"), sem("max_T")
        s_scoresT, s_exp, s_plow = sem("scoresT_ps"), sem("exp_done"), sem("p_low")
        s_av, s_norm = sem("attended_ps"), sem("normed")
        s_dve, s_rec, s_st = sem("dve_link"), sem("reciprocal"), sem("stats")
        s_res, s_y, s_rstd, s_ln, s_out = (sem("residual"), sem("y_sum"), sem("rstd"),
                                           sem("ln_done"), sem("x_out"))
        s_mask = sem("mask_ready")

        PIECE_SLOT = (1, 1, 2, 3, 3, 4, 4, 5, 6, 6, 7, 7, 8, 9, 9, 10, 11, 11, 13, 14) if own else (1, 2, 3, 4, 5, 6, 7, 8, 9)

        def slots(first, last):
            unit = lambda u: divmod(u, UNITS)
            there = lambda u: u >= 0 or not first
            for s in range(16):
                b, g = unit(s)
                pieces = () if last else [p for p, at in enumerate(PIECE_SLOT) if at == s]
                if there(s - 1):
                    yield "low", *unit(s - 1)
                if g == 0 and there(s - 8):
                    yield "root", b - 2, 0
                if not (last and b == 3):
                    yield "scores", b + 1, g
                if g == 0:
                    yield "maxT", b, 0
                if not last and s == 0:
                    yield "xT", 0, 0
                    if not own:
                        yield "ctxT", 0, 0
                for p in pieces[:1]:
                    yield "piece", 0, p
                yield "scoresT", b, g
                if there(s - 2):
                    yield "attend", *unit(s - 2)
                for p in pieces[1:]:
                    yield "piece", 0, p
                if g == 3 and there(s - 7):
                    yield "out", b - 1, 0
                if own and there(s - 3):
                    yield "attT", *unit(s - 3)
                if not own and g == 2 and there(s - 6):
                    yield "attT", b - 1, 0
                if g == 0 and there(s - 8):
                    yield "norm", b - 2, 0
            if last:
                yield "root", 2, 0
                yield "low", 3, 3
                yield "attend", 3, 2
                yield "norm", 2, 0
                if own:
                    yield "attT", 3, 1
                yield "attend", 3, 3
                for g in ((2, 3) if own else (0,)):
                    yield "attT", 3, g
                yield "out", 3, 0
                yield "root", 3, 0
                yield "norm", 3, 0

        def opening():
            yield "xT", 0, 0
            if not own:
                yield "ctxT", 0, 0
            for p in range(NP):
                yield "piece", 0, p
            for g in range(UNITS):
                yield "scores", 4, g

        MISC = ("maxT", "xT", "ctxT", "attT", "out")
        count = lambda events: sum(e[0] in MISC for e in events)
        M_OPEN, M_FIRST, M_STEP = count(opening()), count(slots(True, False)), count(slots(False, False))

        def numbered(n, events, base):
            m = base
            for what, b, g in events:
                yield what, b, g, m
                m += what in MISC

        def walk(eng, handle):
            for what, b, g, m in numbered(-1, opening(), 0):
                handle(what, -1, 1, b, g, m)
            for what, b, g, m in numbered(0, slots(True, False), M_OPEN):
                handle(what, 0, 0, b, g, m)
            with eng.Fori(0, (NQUAD - 2) // 2) as i:
                for half in range(2):
                    n = 2 * i + (1 + half)
                    base = M_OPEN + M_FIRST + M_STEP * half
                    for what, b, g, m in numbered(n, slots(False, False), base):
                        handle(what, n, 1 - half, b, g, i * (2 * M_STEP) + m)
            base = M_OPEN + M_FIRST + M_STEP * (NQUAD - 2)
            for what, b, g, m in numbered(NQUAD - 1, slots(False, True), base):
                handle(what, NQUAD - 1, 1, b, g, m)

        def wait(eng, s, value):
            if not (isinstance(value, int) and value <= 0):
                eng.wait_ge(s, value)

        def hold_late(eng, s, value, held):
            if not (isinstance(value, int) and value <= 0):
                hold(eng, s, value, held)

        def place(g, j):
            if own:
                return 64 * (g % 2), 64, 4 * (g // 2) + j
            return 32 * g, 32, j

        def seat(g):
            return 2 * (g % 2) + g // 2 if own else g

        block = ctx.enter_context(nc.Block())

        @block.sync
        def _(sp):
            consts = [(ident[:], k["ident"]), (ident4[:], k["ident4"]), (sel[:], k["sel"]),
                      (bias[:], w["bias"]), (vbias[:], w["vbias"]), (expo[:], k["expo"]),
                      (obias[:], w["obias"].partition_broadcast(P))]
            if own:
                consts += [(addmask[:, 0, :], k["causal4"]), (cos[:], k["cos"]), (sin[:], k["sin"])]
            else:
                consts += [(low_rows[:], k["low_rows"])]
            def load_weights(n):
                name = names[n]
                if n >= NST:
                    sp.wait_ge(s_wl, n - NST + 1)
                sp.dma_start(stage[n % NST][:, 0:WN[name]], w[name]).then_inc(s_stage[n % NST], 16)
            load_weights(0)
            for to, frm in consts:
                sp.dma_start(to, frm).then_inc(s_const, 16)
            sp.dma_start(xin[0][:], src[0:QUAD].rearrange("b t d -> t b d")).then_inc(s_xin, 16)
            if not own:
                sp.dma_start(cin[0][:], ctx_src[0:QUAD].rearrange("b t d -> t b d")).then_inc(s_cin, 16)
            for n in range(1, len(names)):
                load_weights(n)

            def load(n, par):
                if not (isinstance(n, int) and n < 2):
                    sp.wait_ge(s_res, n - 1)
                wait(sp, s_xin, 16 * n)
                sp.dma_start(xin[par][:], src[bass.ds(4 * n, QUAD)].rearrange("b t d -> t b d"))\
                  .then_inc(s_xin, 16)
                if not own:
                    wait(sp, s_cin, 16 * n)
                    sp.dma_start(cin[par][:], ctx_src[bass.ds(4 * n, QUAD)].rearrange("b t d -> t b d"))\
                      .then_inc(s_cin, 16)

            def load_mask(n):
                wait(sp, s_mask, n)
                sp.dma_start(rawmask[:], mask_src[bass.ds(4 * n, QUAD)].rearrange("b t d -> t b d"))\
                  .then_inc(s_min, 16)

            if masked and not own:
                load_mask(0)
            load(1, 1)

            def handle(what, n, par, b, g, m):
                if what == "norm":
                    row = 4 * n + b
                    hold(sp, s_ln, row + 1, held["sp"])
                    hold_late(sp, s_out, 16 * row, held["sp"])
                    q = par if b >= 0 else 1 - par
                    sp.dma_start(dst[bass.ds(row, 1)].rearrange("b t d -> t b d"),
                                 xout[q][:, b % 4:b % 4 + 1, :]).then_inc(s_out, 16)
                    if b == 0 and not (isinstance(n, int) and n >= NQUAD - 2):
                        load_next(n + 2, par)
                if what == "ctxT" and masked and not own and not (isinstance(n, int) and n < 0):
                    load_mask(n + 1)

            def load_next(n, par):
                load(n, par)

            for what, b, g, m in numbered(0, slots(True, False), 0):
                handle(what, 0, 0, b, g, m)
            with sp.Fori(0, (NQUAD - 2) // 2 - 1) as i:
                for half in range(2):
                    for what, b, g, m in numbered(0, slots(False, False), 0):
                        handle(what, 2 * i + (1 + half), 1 - half, b, g, m)
            for n in range(NQUAD - 3, NQUAD):
                for what, b, g, m in numbered(0, slots(False, n == NQUAD - 1), 0):
                    handle(what, n, n % 2, b, g, m)
            sp.wait_ge(s_out, 16 * B)

        @block.tensor
        def _(pe):
            pe.wait_ge(s_vb, 1)
            last = len(names) - 1
            pe.wait_ge(s_stage[last % NST], 16 * (last // NST + 1))
            no = H * DH // P
            so = stage[last % NST]
            for c in range(no):
                mm = nc.tensor.matmul(msc[:, 0:D], vbias_b[:, c, :], so[:, c * D:(c + 1) * D],
                                      start=(c == 0), stop=(c == no - 1))
            mm.then_inc(s_obp, 1)
            pe.wait_ge(s_ready, 1)

            def three(out, lh, ll, rh, rl, start, stop):
                nc.tensor.matmul(out, lh, rl, start=start, stop=False)
                nc.tensor.matmul(out, ll, rh, start=False, stop=False)
                return nc.tensor.matmul(out, lh, rh, start=False, stop=stop)

            def handle(what, n, par, b, g, m):
                q = par if 0 <= b < 4 else 1 - par
                bb = b % 4
                unit = 16 * n + 4 * b + g
                row = 4 * n + b
                cols = slice(bb * S, (bb + 1) * S)
                if what in MISC:
                    wait(pe, s_misc_free, m)
                if what in ("xT", "ctxT"):
                    pe.wait_ge(s_xin if what == "xT" else s_cin, 16 * (n + 2))
                    t = xin[1 - par] if what == "xT" else cin[1 - par]
                    for j in range(QUAD):
                        mm = nc.tensor.transpose(msc[:, j * P:(j + 1) * P], t[:, j, :], ident[:])
                    mm.then_inc(s_misc, 1)
                elif what == "piece":
                    f = NP * (n + 1) + g
                    if g == 0:
                        wait(pe, s_misc_free, m)
                    wait(pe, s_proj_free, f if own or g == 0 else f - 1)
                    if own and g < NQK:
                        c = slice((g // 2) * P, (g // 2 + 1) * P)
                        for t, name in enumerate((("q", "qs"), ("k", "ks"))[g % 2]):
                            mm = three(prj[t][:], wh[name][:, c], wl[name][:, c], xh[:], xl[:], True, True)
                    elif own:
                        c = slice((g - NQK) * S, (g - NQK + 1) * S)
                        for t in range(2):
                            o = slice(t * 512, (t + 1) * 512)
                            mm = three(prj[t][:], xh[:, c], xl[:, c], wh["v"][:, o], wl["v"][:, o], True, True)
                    elif g < NQK:
                        name, a, l = (("q", xh, xl), ("k", ch, cl))[g % 2]
                        c = slice((g // 2) * P, (g // 2 + 1) * P)
                        mm = three(prj[g % 2][:], wh[name][:, c], wl[name][:, c], a[:], l[:], True, True)
                    else:
                        for j in range(QUAD):
                            c = slice(j * S, (j + 1) * S)
                            mm = three(prj[0][:, c], ch[:, c], cl[:, c], wh["v"][:], wl["v"][:], True, True)
                    mm.then_inc(s_proj, 1)
                elif what == "scores":
                    if g == 0 and bb == 0:
                        if own:
                            pe.wait_ge(s_qklo, NQK * (n + 2))
                        else:
                            pe.wait_ge(s_proj_free, NP * (n + 1) + NQK)
                    if g == 0 and masked and not own and bb == 0:
                        pe.wait_ge(s_mask, n + 2)
                    wait(pe, s_max, unit - 1)
                    out = scp[g % 2]
                    if masked:
                        rhs = addmask[:, 0, :] if own else None
                        if own:
                            nc.tensor.matmul(out[:], ident4[:, 0:P], rhs, start=True, stop=False,
                                             skip_group_check=True)
                        else:
                            for j in range(HU):
                                nc.tensor.matmul(out[:, j * P:(j + 1) * P], ident4[:, 0:P],
                                                 addmask[q][:, bb, :], start=(j == 0), stop=False,
                                                 skip_group_check=True)
                    for j in range(HU):
                        r, nr, c = place(g, j)
                        o = out[:, j * P:(j + 1) * P]
                        if own:
                            qa, ql_, ka, kl_ = (t[q][r:r + nr, c, cols] for t in
                                                ([x[0] for x in qkh], [x[0] for x in qkl],
                                                 [x[1] for x in qkh], [x[1] for x in qkl]))
                            nc.tensor.matmul(o, qa, kl_, start=False, stop=False, skip_group_check=True)
                            nc.tensor.matmul(o, ql_, ka, start=False, stop=False, skip_group_check=True)
                            mm = nc.tensor.matmul(o, qa, ka, start=False, stop=True, skip_group_check=True)
                        else:
                            mm = nc.tensor.matmul(o, qks[q][0][r:r + nr, c, cols], qks[q][1][r:r + nr, c, cols],
                                                  start=not masked, stop=True, skip_group_check=True)
                    mm.then_inc(s_scores, 1)
                elif what == "maxT":
                    pe.wait_ge(s_split, row + 1)
                    t = max3[bb % 2]
                    nc.tensor.transpose(msc[:, 0:P // 2].bitcast(BF16), t[:].rearrange("p u r -> p (u r)"),
                                        ident4[:, 0:P])\
                      .then_inc(s_misc, 1)
                elif what == "scoresT":
                    wait(pe, s_exp, unit - 1)
                    if g == 0:
                        pe.wait_ge(s_maxT, row + 1)
                    out = stp[g % 2]
                    if masked:
                        msk = addmask[:, 0, 0:P] if own else addmask[q][:, bb, :]
                        nc.tensor.matmul(out[:], msk, ident4[:], start=True, stop=False, skip_group_check=True)
                    for j in range(HU):
                        r, nr, c = place(g, j)
                        o = out[:, j * P:(j + 1) * P]
                        if own:
                            qa, ql_, ka, kl_ = (t[q][r:r + nr, c, cols] for t in
                                                ([x[0] for x in qkh], [x[0] for x in qkl],
                                                 [x[1] for x in qkh], [x[1] for x in qkl]))
                            nc.tensor.matmul(o, kl_, qa, start=False, stop=False, skip_group_check=True)
                            nc.tensor.matmul(o, ka, ql_, start=False, stop=False, skip_group_check=True)
                            nc.tensor.matmul(o, ka, qa, start=False, stop=False, skip_group_check=True)
                        else:
                            nc.tensor.matmul(o, qks[q][1][r:r + nr, c, cols], qks[q][0][r:r + nr, c, cols],
                                             start=not masked, stop=False, skip_group_check=True)
                        mm = nc.tensor.matmul(o, sel[r:r + nr, g // 2 if own else 0, j, :],
                                              maxT[bb % 2][r:r + nr, :], start=False, stop=True,
                                              skip_group_check=True)
                    mm.then_inc(s_scoresT, 1)
                elif what == "attend":
                    pe.wait_ge(s_plow, unit + 1)
                    if own:
                        wait(pe, s_norm, unit)
                    elif g == 0:
                        wait(pe, s_norm, row)
                    for j in range(HU):
                        at = (j if own else 4 * g + j) * DV
                        o = avp[:, at:at + DV]
                        a, l = ph[g][:, j * P:(j + 1) * P], pl[g][:, j * P:(j + 1) * P]
                        hv, lv = vh[q][:, bb, 4 * g + j, :], vl[q][:, bb, 4 * g + j, :]
                        mm = three(o, a, l, hv, lv, True, True)
                    mm.then_inc(s_av, 1)
                elif what == "attT":
                    if own:
                        pe.wait_ge(s_norm, unit + 1)
                        t = att[g % 2]
                        for j in range(2):
                            mm = nc.tensor.transpose(msc[:, j * P:(j + 1) * P],
                                                     t[:, 2 * j:2 * j + 2, :].rearrange("p h d -> p (h d)"), ident[:])
                    else:
                        pe.wait_ge(s_norm, row + 1)
                        mm = nc.tensor.transpose(msc[:, 0:P], att[bb % 2][:].rearrange("p h d -> p (h d)"), ident[:])
                    mm.then_inc(s_misc, 1)
                elif what == "out":
                    for c in range(no):
                        mm = three(msc[:, 0:D], attTh[:, c, :], attTl[:, c, :], wh["o"][:, c * D:(c + 1) * D],
                                   wl["o"][:, c * D:(c + 1) * D], c == 0, c == no - 1)
                    mm.then_inc(s_misc, 1)

            walk(pe, handle)

        @block.scalar
        def _(act):
            for n, name in enumerate(names):
                act.wait_ge(s_stage[n % NST], 16 * (n // NST + 1))
                nc.scalar.copy(wh[name][:], stage[n % NST][:, 0:WN[name]]).then_inc(s_wh, 1)
            act.wait_ge(s_ready, 1)

            def handle(what, n, par, b, g, m):
                unit = 16 * n + 4 * b + g
                row = 4 * n + b
                bb = b % 4
                if what in ("xT", "ctxT"):
                    act.wait_ge(s_misc, m + 1)
                    nc.scalar.copy((xh if what == "xT" else ch)[:], msc[:]).then_inc(s_misc_hi, 1)
                elif what == "maxT":
                    act.wait_ge(s_misc, m + 1)
                    nc.scalar.copy(maxT[bb % 2][:], msc[:, 0:P // 2].bitcast(BF16))\
                      .then_inc(s_maxT, 1)
                    act.wait_ge(s_maxT, row + 1)
                    act.sem_inc(s_misc_free, 1)
                elif what == "piece":
                    f = NP * (n + 1) + g
                    kk = NQK * (n + 1) + g
                    if own and 1 <= g <= NQK:
                        act.wait_ge(s_full, kk)
                        p = g - 1
                        nc.scalar.copy(qkh[1 - par][p % 2][:, p // 2, :], full[p % 2][:]).then_inc(s_qkhi, 1)
                    if own and g >= NQK:
                        act.wait_ge(s_proj, f + 1)
                        for t in range(2):
                            last = nc.scalar.copy(vh[1 - par][:, g - NQK, 8 * t:8 * t + 8, 0:DH],
                                                  prj[t][:].rearrange("p (h d) -> p h d", d=DH))
                        last.then_inc(s_proj_hi, 1)
                    if not own:
                        act.wait_ge(s_proj, f + 1)
                        if g < NQK:
                            wait(act, s_proj_free, f - 1)
                            nc.scalar.activation(high[g % 2][:], prj[g % 2][:], ACT.Identity,
                                                 bias=low_bias[:, g % 2, g // 2:g // 2 + 1],
                                                 scale=low_rows[:, g % 2:g % 2 + 1]).then_inc(s_proj_hi, 1)
                        else:
                            nc.scalar.copy(vh[1 - par][:, :, :, 0:DH],
                                           prj[0][:].rearrange("p (b h d) -> p b h d", b=QUAD, d=DH))\
                              .then_inc(s_proj_hi, 1)
                elif what == "scoresT":
                    act.wait_ge(s_scoresT, unit + 1)
                    wait(act, s_av, unit - 3)
                    wait(act, s_plow, unit - 1)
                    nc.scalar.activation(ph[g][:], stp[g % 2][:], ACT.Exp, scale=scale)
                    nc.scalar.activation(pf[g % 2][:], stp[g % 2][:], ACT.Exp, scale=scale).then_inc(s_exp, 1)
                elif what == "attT":
                    act.wait_ge(s_misc, m + 1)
                    n_ = 2 if own else 1
                    c = 2 * g if own else 0
                    nc.scalar.copy(attTh[:, c:c + n_, :], msc[:, 0:n_ * P].rearrange("p (c t) -> p c t", c=n_))\
                      .then_inc(s_misc_hi, 1)

            walk(act, handle)

        HI = ("xT", "ctxT", "attT")
        count_hi = lambda events: sum(e[0] in HI for e in events)
        H_OPEN, H_FIRST, H_STEP = (count_hi(opening()), count_hi(slots(True, False)),
                                   count_hi(slots(False, False)))

        @block.gpsimd
        def _(pool):
            linked = [0]

            def link(ins):
                ins.then_inc(s_link, 1)

            for i in range(2):
                nc.gpsimd.memset(vh[i][:, :, :, DH:DV], 1.0)
                nc.gpsimd.memset(vl[i][:, :, :, DH:DV], 0.0).then_inc(s_link, 1)
            for i in range(2):
                nc.gpsimd.memset(max3[i][:], 0.0).then_inc(s_link, 1)
            LINKS = 3
            L0 = 4

            def split(row, bb):
                hold(pool, s_max, 4 * row + 4, held["pool"])
                if not (isinstance(row, int) and row < 2):
                    hold(pool, s_maxT, row - 1, held["pool"])
                at = L0 + LINKS * row
                x, r = (t[bb % 2][:].rearrange("p (u j) -> p u j", u=UNITS) for t in (negmax, rest))
                part = [max3[bb % 2][:, :, HU * t:HU * t + HU] for t in range(NSPLIT)]
                nc.gpsimd.tensor_copy(part[0], x).then_inc(s_link, 1)
                pool.wait_ge(s_link, at + 1)
                nc.gpsimd.tensor_tensor(r, x, part[0], ALU.subtract).then_inc(s_link, 1)
                hold(pool, s_link, at + 2, held["pool"])
                nc.gpsimd.tensor_copy(part[1], r).then_inc(s_link, 1)
                pool.wait_ge(s_link, at + 3)
                nc.gpsimd.tensor_tensor(part[2], r, part[1], ALU.subtract).then_inc(s_split, 1)

            def handle(what, n, par, b, g, m):
                row = 4 * n + b
                if what == "piece" and own:
                    f = NP * (n + 1) + g
                    kk = NQK * (n + 1) + g
                    if 2 <= g < NQK + 2:
                        p = g - 2
                        pool.wait_ge(s_qkhi, kk - 1)
                        nc.gpsimd.tensor_tensor(qkl[1 - par][p % 2][:, p // 2, :], full[p % 2][:],
                                                qkh[1 - par][p % 2][:, p // 2, :], ALU.subtract)\
                            .then_inc(s_qklo, 1)
                    if g < NQK:
                        pool.wait_ge(s_proj_free, f + 1)
                        if not (isinstance(n, int) and n < 0 and g < 2):
                            pool.wait_ge(s_qklo, kk - 1)
                        nc.gpsimd.tensor_tensor(full[g % 2][:], rot[g % 2][0][:], rot[g % 2][1][:], ALU.add)\
                            .then_inc(s_full, 1)
                if what == "piece" and g == NP - 3:
                    pool.wait_ge(s_xin, 16 * (n + 2))
                    pool.wait_ge(s_proj, NP * (n + 1) + g + 1)
                    wait(pool, s_y, 4 * n)
                    nc.gpsimd.tensor_tensor(xres[1 - par][:], xin[1 - par][:], obias4[:], ALU.add)\
                        .then_inc(s_res, 1)
                if what == "ctxT" and masked:
                    pool.wait_ge(s_min, 16 * (n + 2))
                    hold_late(pool, s_scoresT, 16 * n, held["pool"])
                    nc.gpsimd.tensor_scalar(addmask[1 - par][:], rawmask[:], -1e18, None, ALU.mult)\
                        .then_inc(s_mask, 1)
                if what == "scores" and g == 3:
                    split(row, b % 4)
                if what == "root":
                    hold(pool, s_y, row + 1, held["pool"])
                    nc.gpsimd.tensor_scalar(veps[:], mv[:, 1:2], LN_EPS, None, ALU.add).then_inc(s_rstd, 1)
                    pool.wait_ge(s_rstd, 2 * row + 1)
                    nc.gpsimd.tensor_tensor(rstd[:], veps[:], expo[:, 0:1], ALU.pow).then_inc(s_rstd, 1)

            pool.wait_ge(s_link, L0)
            pool.wait_ge(s_ready, 1)
            walk(pool, handle)

        @block.vector
        def _(dve):
            nconst = 7 + (3 if own else 1)
            dve.wait_ge(s_const, 16 * nconst)
            links = [0]

            def link(ins):
                links[0] += 1
                ins.then_inc(s_dve, 1)
                dve.wait_ge(s_dve, links[0])

            no = H * DH // P
            for c in range(no):
                ins = nc.vector.tensor_copy(vbias_b[:, c, :], vbias[:, c:c + 1].to_broadcast([P, P]))
            ins.then_inc(s_vb, 1)
            if not own:
                for t in range(2):
                    link(nc.vector.tensor_scalar(low_bias[:, t, :], bias[:, t, :], low_rows[:, t:t + 1], None,
                                                 ALU.mult))
            for n, name in enumerate(names):
                dve.wait_ge(s_wh, n + 1)
                nc.vector.tensor_tensor(wl[name][:], stage[n % NST][:, 0:WN[name]], wh[name][:],
                                        ALU.subtract).then_inc(s_wl, 1)
            dve.wait_ge(s_obp, 1)
            for j in range(QUAD):
                link(nc.vector.tensor_tensor(obias4[:, j, :], obias[:], msc[:, 0:D], ALU.add))
            dve.wait_ge(s_wl, len(names))
            dve.sem_inc(s_ready, 1)

            def lowp(n, par, b, g):
                unit = 16 * n + 4 * b + g
                dve.wait_ge(s_exp, unit + 1)
                wait(dve, s_av, unit - 3)
                nc.vector.tensor_tensor(pl[g][:], pf[g % 2][:], ph[g][:], ALU.subtract)\
                    .then_inc(s_plow, 1)

            def handle(what, n, par, b, g, m, hi):
                unit = 16 * n + 4 * b + g
                row = 4 * n + b
                bb = b % 4
                if what in ("xT", "ctxT"):
                    dve.wait_ge(s_misc_hi, hi + 1)
                    h, l = (xh, xl) if what == "xT" else (ch, cl)
                    nc.vector.tensor_tensor(l[:], msc[:], h[:], ALU.subtract).then_inc(s_misc_free, 1)
                elif what == "piece":
                    f = NP * (n + 1) + g
                    kk = NQK * (n + 1) + g
                    if own and g < NQK:
                        dve.wait_ge(s_proj, f + 1)
                        wait(dve, s_full, kk - 1)
                        for t, table in enumerate((cos, sin)):
                            ins = nc.vector.scalar_tensor_tensor(
                                out=rot[g % 2][t][:], in0=prj[t][:], scalar=bias[:, 2 * (g % 2) + t, g // 2:g // 2 + 1],
                                in1=table[:], op0=ALU.add, op1=ALU.mult)
                        ins.then_inc(s_proj_free, 1)
                    elif own:
                        dve.wait_ge(s_proj_hi, 4 * (n + 1) + g - NQK + 1)
                        for t in range(2):
                            ins = nc.vector.tensor_tensor(vl[1 - par][:, g - NQK, 8 * t:8 * t + 8, 0:DH],
                                                          prj[t][:].rearrange("p (h d) -> p h d", d=DH),
                                                          vh[1 - par][:, g - NQK, 8 * t:8 * t + 8, 0:DH], ALU.subtract)
                        ins.then_inc(s_proj_free, 1)
                    elif g < NQK:
                        dve.wait_ge(s_proj_hi, f + 1)
                        ins = nc.vector.scalar_tensor_tensor(
                            out=qks[1 - par][g % 2][:, g // 2, :], in0=prj[g % 2][:],
                            scalar=bias[:, g % 2, g // 2:g // 2 + 1], in1=high[g % 2][:],
                            op0=ALU.add, op1=ALU.subtract).then_inc(s_proj_free, 1)
                    else:
                        dve.wait_ge(s_proj_hi, f + 1)
                        nc.vector.tensor_tensor(vl[1 - par][:, :, :, 0:DH],
                                                prj[0][:].rearrange("p (b h d) -> p b h d", b=QUAD, d=DH),
                                                vh[1 - par][:, :, :, 0:DH], ALU.subtract).then_inc(s_proj_free, 1)
                elif what == "scores":
                    dve.wait_ge(s_scores, unit + 1)
                    if g == 0:
                        wait(dve, s_split, row - 1)
                    nc.vector.tensor_reduce(negmax[bb % 2][:, HU * seat(g):HU * seat(g) + HU],
                                            scp[g % 2][:].rearrange("p (h t) -> p h t", h=HU),
                                            AX.X, ALU.max, negate=True).then_inc(s_max, 1)
                elif what == "attend":
                    if own or g == 3:
                        dve.wait_ge(s_av, unit + 1)
                        v = avp[:, 0:NA * DV].rearrange("p (h d) -> p h d", d=DV)
                        nc.vector.reciprocal(recip[:], v[:, :, DH]).then_inc(s_rec, 1)
                        dve.wait_ge(s_rec, (unit if own else row) + 1)
                        i = g % 2 if own else bb % 2
                        nc.vector.tensor_tensor(att[i][:], v[:, :, 0:DH],
                                                recip[:].unsqueeze(2).to_broadcast([P, NA, DH]), ALU.mult)\
                            .then_inc(s_norm, 1)
                elif what == "attT":
                    dve.wait_ge(s_misc_hi, hi + 1)
                    n_ = 2 if own else 1
                    c = 2 * g if own else 0
                    nc.vector.tensor_tensor(attTl[:, c:c + n_, :], msc[:, 0:n_ * P].rearrange("p (c t) -> p c t", c=n_),
                                            attTh[:, c:c + n_, :], ALU.subtract).then_inc(s_misc_free, 1)
                elif what == "out":
                    dve.wait_ge(s_misc, m + 1)
                    dve.wait_ge(s_res, n + 1 if b >= 0 else n)
                    q = par if b >= 0 else 1 - par
                    nc.vector.tensor_tensor(ysum[:], msc[:, 0:D], xres[q][:, bb, :], ALU.add)\
                        .then_inc(s_misc_free, 1)
                    dve.wait_ge(s_misc_free, m + 1)
                    nc.vector.bn_stats(stats[:], ysum[:]).then_inc(s_st, 1)
                    hold(dve, s_st, row + 1, held["dve"])
                    nc.vector.bn_aggr(mv[:], stats[:]).then_inc(s_y, 1)
                elif what == "norm":
                    dve.wait_ge(s_rstd, 2 * row + 2)
                    if not (isinstance(row, int) and row < 2):
                        dve.wait_ge(s_out, 16 * (row - 1))
                    q = par if b >= 0 else 1 - par
                    nc.vector.tensor_scalar(xout[q][:, bb, :], ysum[:], mv[:, 0:1], rstd[:], ALU.subtract,
                                            ALU.mult).then_inc(s_ln, 1)

            def walk_hi():
                def run(n, par, events, mbase, hbase, i=None):
                    m, hi = 0, 0
                    for what, b, g in events:
                        mm = mbase + m if i is None else i * (2 * M_STEP) + (mbase + m)
                        hh = hbase + hi if i is None else i * (2 * H_STEP) + (hbase + hi)
                        if what == "low":
                            lowp(n, par, b, g)
                        handle(what, n, par, b, g, mm, hh)
                        m += what in MISC
                        hi += what in HI
                run(-1, 1, opening(), 0, 0)
                run(0, 0, slots(True, False), M_OPEN, H_OPEN)
                with dve.Fori(0, (NQUAD - 2) // 2) as i:
                    for half in range(2):
                        run(2 * i + (1 + half), 1 - half, slots(False, False),
                            M_OPEN + M_FIRST + M_STEP * half, H_OPEN + H_FIRST + H_STEP * half, i)
                run(NQUAD - 1, 1, slots(False, True), M_OPEN + M_FIRST + M_STEP * (NQUAD - 2),
                    H_OPEN + H_FIRST + H_STEP * (NQUAD - 2))

            walk_hi()
    release_semaphores(nc, sems)


def mixture_pass(nc, tag, src, dst, w, k, slots, results, experts, top, tiles, width, normed=False, cap=None):
    E, NF, NT, W = experts, F // P, tiles, width
    NW = W // P
    planned = cap is None
    NI = S * B // P
    NS = 2 * E
    NX = 4
    NST = 6
    sems = []
    with ExitStack() as ctx:
        def sb(name, shape, dt):
            return ctx.enter_context(nc.sbuf_tensor(f"{tag}_{name}", shape, dt))

        def sem(name):
            sems.append(nc.alloc_semaphore(f"{tag}_{name}"))
            return sems[-1]

        def two(name, shape, dt=F32):
            return [sb(f"{name}{i}", shape, dt) for i in range(2)]

        def ps(name):
            return ctx.enter_context(nc.psum_tensor(f"{tag}_{name}", [P, 512], F32))
        held = {e: sem(f"held_{e}") for e in ("sp", "pool", "dve")}

        ident = sb("ident", [P, P], F32)
        below, ones = sb("below", [P, P], BF16), sb("ones", [P, P], BF16)
        iota, expo4 = sb("iota", [P, 1, E], F32), sb("expo4", [P, QUAD], F32)
        wr, br = sb("wr", [P, E], F32), sb("br", [P, 1, E], F32)
        x = sb("x", [P, B, D], F32)
        rows = sb("rows", [P, B, D], F32) if normed else x
        if normed:
            gamma, beta = sb("gamma", [P, 1, D], F32), sb("beta", [P, 1, D], F32)
        xT = two("xT", [P, QUAD * S])
        stats, mv = two("stats", [P, QUAD, 6]), two("mv", [P, QUAD, 2])
        veps, rstd = two("veps", [P, QUAD]), two("rstd", [P, QUAD])
        prob = sb("prob", [P, B, E], F32)
        peak, total = sb("peak", [P, B], F32), sb("total", [P, B], F32)
        top8, idx8 = sb("top8", [P, B, 8], F32), sb("idx8", [P, B, 8], U32)
        index, gate = sb("index", [P, B, top], F32), sb("gate", [P, B, top], F32)
        hot = [sb(f"hot{t}", [P, B, E], F32) for t in range(top)]
        both, ranks = sb("both", [P, B, E], BF16), sb("ranks", [P, B, E], F32)
        one, seen, before = (sb(n, [P, E, B], F32) for n in ("one", "seen", "before"))
        count, start = sb("count", [P, E], F32), sb("start", [P, E], F32)
        place, kept = sb("place", [P, B, top], F32), sb("kept", [P, B, top], F32)
        send, fetch = sb("send", [P, B, top], U32), sb("fetch", [P, B, top], U32)
        blank = sb("blank", [P, 1, D], F32)
        if planned:
            steps, tile_no = sb("steps", [P, 1, NI], F32), sb("tile_no", [P, NT], F32)
            more, past = sb("more", [P, E, NI], F32), sb("past", [P, NT, E], F32)
            need, end, one_e = sb("need", [P, E], F32), sb("end", [P, E], F32), sb("one_e", [P, E], F32)
            tile_of, tile_expert = sb("tile_of", [P, NT], F32), sb("tile_expert", [P, NT], I32)

        w1h, w1l = sb("w1h", [P, E * F], F16), sb("w1l", [P, E * F], F16)
        w2h, w2l = sb("w2h", [P, E * F], F16), sb("w2l", [P, E * F], F16)
        b1, b1h, b1l = sb("b1", [P, E * F // P], F32), sb("b1h", [P, E * F // P], F16), sb("b1l", [P, E * F // P], F16)
        b1p = sb("b1p", [P, E * F], F16)
        ones_w = sb("ones_w", [P, W], F16)
        const = sb("const", [P, E * D], F32)
        stage = [sb(f"stage{i}", [P, F], F32) for i in range(NST)]
        if normed:
            b1c, b1ch, b1cl = (sb(n, [P, E * NF], t) for n, t in (("b1c", F32), ("b1ch", F16), ("b1cl", F16)))
            b2r, crow, ctot = sb("b2r", [1, E, D], F32), sb("crow", [1, E, D], F32), sb("ctot", [1, 1, D], F32)
            onesf = sb("onesf", [1, P], F32)
        xg = [sb(f"xg{i}", [P, NW, D], F32) for i in range(NX)]
        xh, xl = two("xh", [P, W], F16), two("xl", [P, W], F16)
        hh, hl = two("hh", [P, NF * W], F16), two("hl", [P, NF * W], F16)
        yo = two("yo", [P, NW, D])

        got, out = two("got", [P, QUAD, top, D]), two("out", [P, QUAD, D])

        NH = NF * W // 512
        pT = ps("pT")
        pH = [[ps(f"pH{i}{j}") for j in range(NH)] for i in range(2)]
        pY = [ps(f"pY{i}") for i in range(2)]
        pX, pLogit, pBelow, pCount = (pH[0][0], pH[1][0]), pT, pY[0], pY[1]
        pC = pH[0][0], pH[1][0]

        s_const, s_k, s_ready = sem("const"), sem("dve_step"), sem("ready")
        s_x = [sem(f"x_in{n}") for n in range(NQUAD)]
        s_mv, s_r, s_norm, s_rows = sem("variance"), sem("rstd"), sem("normed"), sem("rows_ready")
        s_T, s_Tsb, s_logit, s_less, s_exp = sem("turned"), sem("turned_sb"), sem("logits"), sem("less_peak"), sem("exp")
        s_hot, s_rank, s_slot, s_blank, s_zero, s_sent = (sem("hot"), sem("ranks_ps"), sem("slots"), sem("blank"),
                                                         sem("zeroed"), sem("rows_sent"))
        s_stage, s_wh, s_wl, s_b1h, s_b1l, s_b1p, s_fill, s_c = (
            [sem(f"stage{i}") for i in range(NST)], sem("w_high"), sem("w_low"), sem("b1_high"), sem("b1_low"), sem("b1_rows"), sem("filled"),
            sem("const_rows"))
        s_in, s_turn, s_xh, s_xl, s_H, s_hh, s_hl, s_Y, s_y, s_o = (
            [sem(f"slots_in{i}") for i in range(NX)], sem("slots_turned"), sem("x_high"), sem("x_low"), sem("hidden_ps"), sem("hidden_high"),
            sem("hidden_low"), sem("out_ps"), sem("out_sb"), [sem(f"results_out{i}") for i in range(2)])
        s_got, s_mv2, s_r2, s_add, s_out, s_st = (
            [sem(f"fetched{i}") for i in range(2)], sem("sum_variance"), sem("sum_rstd"), sem("sum_step"),
            sem("sum_normed"), sem("stored"))
        block = ctx.enter_context(nc.Block())

        def piece(n):
            e, second = divmod(n, 2)
            c = slice(e * F, (e + 1) * F)
            return (w["w2"][:, c], w2h[:, c], w2l[:, c]) if second else (w["w1"][:, c], w1h[:, c], w1l[:, c])

        def late(eng, s, j, back, inc=1):
            if not (isinstance(j, int) and j < back):
                eng.wait_ge(s, inc * (j - (back - 1)))

        consts = [(ident[:], k["ident"]), (expo4[:], k["expo4"]), (wr[:], w["wr"]),
                  (br[:, 0, :], w["br"].partition_broadcast(P)), (below[:], k["below"]), (ones[:], k["ones"]),
                  (iota[:, 0, :], k["iota"][:, 0:E]), (b1[:], w["b1"])]
        if normed:
            consts += [(gamma[:, 0, :], w["gamma"].partition_broadcast(P)), (beta[:, 0, :], w["beta"].partition_broadcast(P)),
                       (b1c[:], w["b1c"]), (b2r[:].rearrange("p e d -> p (e d)"), w["b2"]), (onesf[:], k["onesf"])]
        else:
            consts += [(const[:], w["b2"][0, :].partition_broadcast(P))]
        if planned:
            consts += [(steps[:, 0, :], k["steps"]), (tile_no[:], k["tile_no"])]
        NC = 16 * len(consts)
        ZR = 8 * P

        @block.sync
        def _(sp):
            def load_x(n):
                sp.dma_start(x[:, 4 * n:4 * n + 4, :], src[4 * n:4 * n + 4].rearrange("b t d -> t b d")).then_inc(s_x[n], 16)
            load_x(0)
            for to, frm in consts:
                sp.dma_start(to, frm).then_inc(s_const, 16)
            for n in range(1, NQUAD):
                load_x(n)
            sp.wait_ge(s_blank, 1)
            for r in range(0, NT * W, ZR):
                sp.dma_start(slots[r:r + ZR, :].rearrange("(a p) d -> p a d", p=P),
                             blank[:].to_broadcast([P, 8, D])).then_inc(s_zero, 16)
            for n in range(NS):
                late(sp, s_wl, n, NST)
                sp.dma_start(stage[n % NST][:], piece(n)[0]).then_inc(s_stage[n % NST], 16)
            sp.wait_ge(s_fill, 2)
            sp.wait_ge(s_b1h, 1)
            sp.dma_start(b1p[0:1, :].rearrange("q (p c) -> q p c", p=P), b1h[:]).then_inc(s_b1p, 16)
            sp.wait_ge(s_b1l, 1)
            sp.dma_start(b1p[32:33, :].rearrange("q (p c) -> q p c", p=P), b1l[:]).then_inc(s_b1p, 16)

            def load(j, i):
                late(sp, s_turn, j, NX)
                sp.dma_start(xg[i][:], slots[bass.ds(j * W, W), :].rearrange("(a p) d -> p a d", p=P))\
                  .then_inc(s_in[i], 16)

            def store(j, i):
                hold(sp, s_y, j + 1, held["sp"])
                sp.dma_start(results[bass.ds(j * W, W), :].rearrange("(a p) d -> p a d", p=P), yo[i][:])\
                  .then_inc(s_o[i], 16)
            sp.wait_ge(s_sent, 16 * B * top)
            for j in range(NX):
                load(j, j)
            for j in range(4):
                store(j, j % 2)
                load(j + NX, j)
            with sp.Fori(1, (NT - NX) // 4) as i:
                for h in range(4):
                    store(4 * i + h, h % 2)
                    load(4 * i + (h + NX), h)
            for j in range(NT - NX, NT):
                store(j, j % 2)
            for i in range(2):
                sp.wait_ge(s_o[i], 8 * NT)
            for n in range(NQUAD):
                sp.wait_ge(s_out, n + 1)
                sp.dma_start(dst[4 * n:4 * n + 4].rearrange("b t d -> t b d"), out[n % 2][:]).then_inc(s_st, 16)
                sp.wait_ge(s_st, 16 * n + 16)

        @block.tensor
        def _(pe):
            pe.wait_ge(s_const, NC)

            def turn_rows(n):
                if normed:
                    pe.wait_ge(s_rows, n + 1)
                else:
                    pe.wait_ge(s_x[n], 16)
                late(pe, s_Tsb, n, 2)
                for b in range(QUAD):
                    mm = nc.tensor.transpose(pX[n % 2][:, b * P:(b + 1) * P], rows[:, 4 * n + b, :], ident[:])
                mm.then_inc(s_T, 1)

            def logits(n):
                pe.wait_ge(s_Tsb, n + 1)
                for b in range(QUAD):
                    o = pLogit[:, (4 * n + b) * E:(4 * n + b + 1) * E]
                    mm = nc.tensor.matmul(o, xT[n % 2][:, b * S:(b + 1) * S], wr[:], start=True, stop=True)
                mm.then_inc(s_logit, 1)
            for n in range(NQUAD + 1):
                if n < NQUAD:
                    turn_rows(n)
                if n:
                    logits(n - 1)
            pe.wait_ge(s_hot, 1)
            hots = both[:].rearrange("p b e -> p (b e)")
            nc.tensor.matmul(pBelow[:, 0:B * E], below[:], hots, start=True, stop=True)
            nc.tensor.matmul(pCount[:, 0:B * E], ones[:], hots, start=True, stop=True).then_inc(s_rank, 1)

            pe.wait_ge(s_ready, 1)
            if normed:
                for e in range(E):
                    o = pC[e // 4][0:1, (e % 4) * D:(e % 4 + 1) * D]
                    for c in range(NF):
                        a = slice(e * NF + c, e * NF + c + 1)
                        v = slice((e * NF + c) * D, (e * NF + c + 1) * D)
                        nc.tensor.matmul(o, b1ch[:, a], w2l[:, v], start=(c == 0), stop=False)
                        nc.tensor.matmul(o, b1cl[:, a], w2h[:, v], start=False, stop=False)
                        mm = nc.tensor.matmul(o, b1ch[:, a], w2h[:, v], start=False, stop=(c == NF - 1))
                mm.then_inc(s_c, 1)
                pe.wait_ge(s_ready, 2)
                for t in range(2):
                    mm = nc.tensor.matmul(pC[t][:], onesf[:], crow[:, 4 * t:4 * t + 4, :].rearrange("p e d -> p (e d)"),
                                          start=True, stop=True)
                mm.then_inc(s_c, 1)
                pe.wait_ge(s_ready, 3)

            def turn(j, i, nth):
                pe.wait_ge(s_in[i], 16 * nth + 16)
                late(pe, s_xl, j, 1)
                for a in range(NW):
                    mm = nc.tensor.transpose(pT[:, a * P:(a + 1) * P], xg[i][:, a, :], ident[:])
                mm.then_inc(s_turn, 1)

            def up(j, i, e):
                pe.wait_ge(s_xl, j + 1)
                late(pe, s_hl, j, 2)
                for c in range(NF):
                    at = c * W
                    o = pH[i][at // 512][:, at % 512:at % 512 + W]
                    v = bass.ds(e * F + c * P, P)
                    nc.tensor.matmul(o, b1p[:, v], ones_w[:], start=True, stop=False)
                    nc.tensor.matmul(o, w1l[:, v], xh[i][:], start=False, stop=False)
                    nc.tensor.matmul(o, w1h[:, v], xl[i][:], start=False, stop=False)
                    mm = nc.tensor.matmul(o, w1h[:, v], xh[i][:], start=False, stop=True)
                mm.then_inc(s_H, 1)

            def down(j, i, e):
                pe.wait_ge(s_hl, j + 1)
                late(pe, s_y, j, 2)
                for a in range(NW):
                    o = pY[i][:, a * D:(a + 1) * D]
                    for c in range(NF):
                        r = slice(c * W + a * P, c * W + a * P + P)
                        v = bass.ds((e * NF + c) * D, D)
                        nc.tensor.matmul(o, hh[i][:, r], w2l[:, v], start=(c == 0), stop=False)
                        nc.tensor.matmul(o, hl[i][:, r], w2h[:, v], start=False, stop=False)
                        mm = nc.tensor.matmul(o, hh[i][:, r], w2h[:, v], start=False, stop=(c == NF - 1))
                mm.then_inc(s_Y, 1)

            def experts_of(j, n):
                if not planned:
                    return [j + t for t in range(n)]
                return nc.values_load_multi_w_load_instructions(tile_expert[0:1, bass.ds(j, n)],
                                                                engines=(mybir.EngineType.PE,),
                                                                min_val=0, max_val=E - 1)[1]
            pe.wait_ge(s_slot, 1)
            turn(0, 0, 0)
            turn(1, 1, 0)
            e = experts_of(0, 5)
            up(0, 0, e[0])
            for j in range(4):
                turn(j + 2, (j + 2) % 4, (j + 2) // 4)
                up(j + 1, (j + 1) % 2, e[j + 1])
                down(j, j % 2, e[j])
            with pe.Fori(0, (NT - 8) // 8) as i:
                e = experts_of(8 * i + 4, 9)
                for h in range(8):
                    turn(8 * i + (h + 6), (h + 2) % 4, 2 * i + (h + 6) // 4)
                    up(8 * i + (h + 5), (h + 1) % 2, e[h + 1])
                    down(8 * i + (h + 4), h % 2, e[h])
            e = experts_of(NT - 4, 4)
            for h in range(4):
                j = NT - 4 + h
                if j + 2 < NT:
                    turn(j + 2, (j + 2) % 4, (j + 2) // 4)
                if j + 1 < NT:
                    up(j + 1, (j + 1) % 2, e[h + 1])
                down(j, j % 2, e[h])

        @block.scalar
        def _(act):
            for n in range(NQUAD):
                act.wait_ge(s_T, n + 1)
                late(act, s_logit, n, 2)
                nc.scalar.copy(xT[n % 2][:], pX[n % 2][:]).then_inc(s_Tsb, 1)
            act.wait_ge(s_less, 1)
            nc.scalar.activation(prob[:], prob[:], ACT.Exp).then_inc(s_exp, 1)
            nc.scalar.copy(b1h[:], b1[:]).then_inc(s_b1h, 1)
            if normed:
                nc.scalar.activation(b1ch[:], b1c[:], ACT.Relu).then_inc(s_b1h, 1)
            for n in range(NS):
                act.wait_ge(s_stage[n % NST], 16 * (n // NST) + 16)
                nc.scalar.copy(piece(n)[1], stage[n % NST][:]).then_inc(s_wh, 1)

            def tile(j, i):
                act.wait_ge(s_turn, j + 1)
                late(act, s_H, j, 2)
                nc.scalar.copy(xh[i][:], pT[:, 0:W]).then_inc(s_xh, 1)

            def hidden(j, i):
                act.wait_ge(s_H, j + 1)
                late(act, s_Y, j, 2)
                for t in range(NH):
                    ins = nc.scalar.activation(hh[i][:, t * 512:(t + 1) * 512], pH[i][t][:], ACT.Relu)
                ins.then_inc(s_hh, 1)
            tile(0, 0)
            tile(1, 1)
            hidden(0, 0)
            for j in range(6):
                tile(j + 2, j % 2)
                hidden(j + 1, (j + 1) % 2)
            with act.Fori(0, (NT - 8) // 4) as i:
                for h in range(4):
                    tile(4 * i + (h + 8), h % 2)
                    hidden(4 * i + (h + 7), (h + 1) % 2)
            hidden(NT - 1, (NT - 1) % 2)

        @block.gpsimd
        def _(pool):
            nc.gpsimd.memset(blank[:], 0.0).then_inc(s_blank, 1)
            nc.gpsimd.memset(ones_w[:], 1.0).then_inc(s_fill, 1)
            nc.gpsimd.memset(b1p[:], 0.0).then_inc(s_fill, 1)
            pool.wait_ge(s_const, NC)
            if normed:
                for n in range(NQUAD + 1):
                    if n < NQUAD:
                        i = n % 2
                        pool.wait_ge(s_mv, n + 1)
                        late(pool, s_norm, n, 2)
                        nc.gpsimd.tensor_scalar(veps[i][:], mv[i][:, :, 1], LN_EPS, None, ALU.add).then_inc(s_r, 1)
                        pool.wait_ge(s_r, 2 * n + 1)
                        nc.gpsimd.tensor_tensor(rstd[i][:], veps[i][:], expo4[:], ALU.pow).then_inc(s_r, 1)
                    if n:
                        pool.wait_ge(s_norm, n)
                        r = rows[:, 4 * n - 4:4 * n, :]
                        nc.gpsimd.tensor_tensor(r, r, beta[:].to_broadcast([P, QUAD, D]), ALU.add).then_inc(s_rows, 1)
                pool.wait_ge(s_rows, NQUAD)
            else:
                for n in range(NQUAD):
                    pool.wait_ge(s_x[n], 16)
            pool.wait_ge(s_slot, 1)
            pool.wait_ge(s_zero, 16 * (NT * W // ZR))
            for b in range(B):
                for t in range(top):
                    pool.indirect_dma_start(slots, bass.IndirectOffsetOnAxis(ap=send[:, b, t:t + 1], axis=0),
                                            rows[:, b, :], None, bounds_check=NT * W - 1,
                                            oob_is_err=False).then_inc(s_sent, 16)
            pool.wait_ge(s_slot, 2)
            for i in range(2):
                pool.wait_ge(s_o[i], 8 * NT)
            for n in range(NQUAD + 1):
                i = n % 2
                if n < NQUAD:
                    late(pool, s_mv2, n, 2)
                    for b in range(QUAD):
                        for t in range(top):
                            pool.indirect_dma_start(got[i][:, b, t, :], None, results,
                                                    bass.IndirectOffsetOnAxis(ap=fetch[:, 4 * n + b, t:t + 1], axis=0))\
                                .then_inc(s_got[i], 16)
                if n:
                    j = 1 - i
                    pool.wait_ge(s_mv2, n)
                    late(pool, s_out, n - 1, 2)
                    nc.gpsimd.tensor_scalar(veps[j][:], mv[j][:, :, 1], LN_EPS, None, ALU.add).then_inc(s_r2, 1)
                    pool.wait_ge(s_r2, 2 * n - 1)
                    nc.gpsimd.tensor_tensor(rstd[j][:], veps[j][:], expo4[:], ALU.pow).then_inc(s_r2, 1)

        @block.vector
        def _(dve):
            steps_done = [0]

            def link(ins):
                steps_done[0] += 1
                ins.then_inc(s_k, 1)
                dve.wait_ge(s_k, steps_done[0])

            be = lambda t: t.to_broadcast([P, B, E])
            nc.vector.memset(one[:], 1.0)
            if planned:
                nc.vector.memset(one_e[:], 1.0)
            dve.wait_ge(s_const, NC)
            if normed:
                def moments(n):
                    i = n % 2
                    dve.wait_ge(s_x[n], 16)
                    for b in range(QUAD):
                        ins = nc.vector.bn_stats(stats[i][:, b, :], x[:, 4 * n + b, :])
                    link(ins)
                    late(dve, s_norm, n, 2)
                    for b in range(QUAD):
                        ins = nc.vector.bn_aggr(mv[i][:, b, :], stats[i][:, b, :])
                    ins.then_inc(s_mv, 1)

                def normalise(n):
                    i = n % 2
                    dve.wait_ge(s_r, 2 * n + 2)
                    for b in range(QUAD):
                        ins = nc.vector.tensor_scalar(rows[:, 4 * n + b, :], x[:, 4 * n + b, :], mv[i][:, b, 0:1],
                                                      rstd[i][:, b:b + 1], ALU.subtract, ALU.mult)
                    link(ins)
                    r = rows[:, 4 * n:4 * n + 4, :]
                    nc.vector.tensor_tensor(r, r, gamma[:].to_broadcast([P, QUAD, D]), ALU.mult).then_inc(s_norm, 1)
                for n in range(NQUAD + 1):
                    if n < NQUAD:
                        moments(n)
                    if n:
                        normalise(n - 1)
            dve.wait_ge(s_logit, NQUAD)
            link(nc.vector.tensor_tensor(prob[:], pLogit[:, 0:B * E].rearrange("p (b e) -> p b e", e=E), be(br[:]), ALU.add))
            link(nc.vector.tensor_reduce(peak[:], prob[:], AX.X, ALU.max))
            nc.vector.tensor_tensor(prob[:], prob[:], be(peak[:].unsqueeze(2)), ALU.subtract).then_inc(s_less, 1)
            dve.wait_ge(s_exp, 1)
            link(nc.vector.tensor_reduce(total[:], prob[:], AX.X, ALU.add))
            link(nc.vector.reciprocal(total[:], total[:]))
            link(nc.vector.tensor_tensor(prob[:], prob[:], be(total[:].unsqueeze(2)), ALU.mult))
            for b in range(B):
                ins = nc.vector.max(top8[:, b, :], prob[:, b, :])
            link(ins)
            for b in range(B):
                ins = nc.vector.max_index(idx8[:, b, :], top8[:, b, :], prob[:, b, :])
            link(ins)
            link(nc.vector.tensor_copy(index[:], idx8[:, :, 0:top]))
            for t in range(top):
                ins = nc.vector.tensor_tensor(hot[t][:], be(iota[:]), be(index[:, :, t:t + 1]), ALU.is_equal)
            link(ins)
            if top == 2:
                nc.vector.tensor_tensor(both[:], hot[0][:], hot[1][:], ALU.add).then_inc(s_hot, 1)
            else:
                nc.vector.tensor_copy(both[:], hot[0][:]).then_inc(s_hot, 1)
            nc.vector.tensor_copy(gate[:], top8[:, :, 0:top])
            dve.wait_ge(s_rank, 1)
            link(nc.vector.tensor_copy(seen[:], pCount[:, 0:B * E].rearrange("p (b e) -> p e b", e=E)))
            flat = lambda t: t[:].rearrange("p e b -> p (e b)")
            nc.vector.tensor_reduce(count[:], seen[:], AX.X, ALU.add)
            link(nc.vector.tensor_tensor_scan(flat(before), flat(one), flat(seen), 0.0, ALU.mult, ALU.add))
            nc.vector.tensor_tensor(start[:], before[:, :, B - 1], count[:], ALU.subtract)
            link(nc.vector.tensor_tensor(seen[:], before[:], seen[:], ALU.subtract))
            link(nc.vector.tensor_tensor(seen[:], seen[:], start[:].unsqueeze(2).to_broadcast([P, E, B]), ALU.subtract))
            link(nc.vector.tensor_tensor(ranks[:], pBelow[:, 0:B * E].rearrange("p (b e) -> p b e", e=E),
                                         seen[:].rearrange("p e b -> p b e"), ALU.add))

            def of_expert(to, values, t):
                link(nc.vector.tensor_tensor(values, values, hot[t][:], ALU.mult))
                link(nc.vector.tensor_reduce(to, values, AX.X, ALU.add))
            if planned:
                link(nc.vector.tensor_tensor(more[:], count[:].unsqueeze(2).to_broadcast([P, E, NI]),
                                             steps[:].to_broadcast([P, E, NI]), ALU.is_gt))
                link(nc.vector.tensor_reduce(need[:], more[:], AX.X, ALU.add))
                link(nc.vector.tensor_tensor_scan(end[:], one_e[:], need[:], 0.0, ALU.mult, ALU.add))
                nc.vector.tensor_tensor(start[:], end[:], need[:], ALU.subtract)
                link(nc.vector.tensor_tensor(past[:], tile_no[:].unsqueeze(2).to_broadcast([P, NT, E]),
                                             end[:].unsqueeze(1).to_broadcast([P, NT, E]), ALU.is_ge))
                nc.vector.tensor_reduce(tile_of[:], past[:], AX.X, ALU.add)
                link(nc.vector.tensor_scalar(start[:], start[:], float(W), None, ALU.mult))
                link(nc.vector.tensor_tensor(ranks[:], ranks[:], start[:].unsqueeze(1).to_broadcast([P, B, E]), ALU.add))
                for t in range(top):
                    link(nc.vector.tensor_tensor(hot[t][:], ranks[:], hot[t][:], ALU.mult))
                    link(nc.vector.tensor_reduce(place[:, :, t:t + 1], hot[t][:], AX.X, ALU.add))
                nc.vector.tensor_scalar(tile_expert[:], tile_of[:], float(E - 1), None, ALU.min)
                nc.vector.tensor_copy(fetch[:], place[:]).then_inc(s_k, 1)
                nc.vector.tensor_copy(send[:], place[:]).then_inc(s_slot, 1)
                steps_done[0] += 1
                dve.wait_ge(s_slot, 1)
                dve.sem_inc(s_slot, 1)
            else:
                link(nc.vector.tensor_tensor(ranks[:], ranks[:], hot[0][:], ALU.mult))
                link(nc.vector.tensor_reduce(kept[:], ranks[:], AX.X, ALU.add))
                link(nc.vector.scalar_tensor_tensor(out=place[:], in0=index[:], scalar=float(cap), in1=kept[:],
                                                    op0=ALU.mult, op1=ALU.add))
                link(nc.vector.tensor_scalar(kept[:], kept[:], float(cap), None, ALU.is_lt))
                nc.vector.tensor_tensor(gate[:], gate[:], kept[:], ALU.mult)
                nc.vector.tensor_scalar(fetch[:], place[:], float(E * cap - 1), None, ALU.min)
                link(nc.vector.tensor_scalar(kept[:], kept[:], -1.0e6, 1.0e6, ALU.mult, ALU.add))
                nc.vector.tensor_tensor(send[:], place[:], kept[:], ALU.add).then_inc(s_slot, 1)
                dve.wait_ge(s_slot, 1)
                dve.sem_inc(s_slot, 1)

            dve.wait_ge(s_b1h, 2 if normed else 1)
            nc.vector.tensor_tensor(b1l[:], b1[:], b1h[:], ALU.subtract).then_inc(s_b1l, 1)
            if normed:
                link(nc.vector.scalar_tensor_tensor(out=b1cl[:], in0=b1c[:], scalar=0.0, in1=b1ch[:], op0=ALU.max,
                                                    op1=ALU.subtract))
            for n in range(NS):
                dve.wait_ge(s_wh, n + 1)
                nc.vector.tensor_tensor(piece(n)[2], stage[n % NST][:], piece(n)[1], ALU.subtract).then_inc(s_wl, 1)
            dve.wait_ge(s_wl, NS)
            dve.wait_ge(s_b1p, 32)
            dve.sem_inc(s_ready, 1)
            if normed:
                dve.wait_ge(s_c, 1)
                for t in range(2):
                    ins = nc.vector.tensor_tensor(crow[:, 4 * t:4 * t + 4, :],
                                                  pC[t][0:1, :].rearrange("p (e d) -> p e d", d=D),
                                                  b2r[:, 4 * t:4 * t + 4, :], ALU.add)
                link(ins)
                link(nc.vector.tensor_reduce(ctot[:, 0, :], crow[:].rearrange("p e d -> p d e"), AX.X, ALU.add))
                link(nc.vector.tensor_tensor(crow[:], b2r[:], crow[:], ALU.subtract))
                link(nc.vector.tensor_tensor(crow[:], crow[:], ctot[:].to_broadcast([1, E, D]), ALU.add))
                dve.sem_inc(s_ready, 1)
                dve.wait_ge(s_c, 2)
                for t in range(2):
                    ins = nc.vector.tensor_copy(const[:, 512 * t:512 * t + 512], pC[t][:])
                link(ins)
                dve.sem_inc(s_ready, 1)

            def tile(j, i):
                dve.wait_ge(s_xh, j + 1)
                nc.vector.tensor_tensor(xl[i][:], pT[:, 0:W], xh[i][:], ALU.subtract).then_inc(s_xl, 1)

            def hidden(j, i):
                dve.wait_ge(s_hh, j + 1)
                for t in range(NH):
                    c = slice(t * 512, (t + 1) * 512)
                    ins = nc.vector.scalar_tensor_tensor(out=hl[i][:, c], in0=pH[i][t][:], scalar=0.0, in1=hh[i][:, c],
                                                         op0=ALU.max, op1=ALU.subtract)
                ins.then_inc(s_hl, 1)

            def result(j, i, e, nth):
                dve.wait_ge(s_Y, j + 1)
                if not (isinstance(nth, int) and nth == 0):
                    dve.wait_ge(s_o[i], 16 * nth)
                for a in range(NW):
                    ins = nc.vector.tensor_tensor(yo[i][:, a, :], pY[i][:, a * D:(a + 1) * D], const[:, bass.ds(e * D, D)],
                                                  ALU.add)
                ins.then_inc(s_y, 1)

            def experts_of(j, n):
                if not planned:
                    return [j + t for t in range(n)]
                return nc.values_load_multi_w_load_instructions(tile_expert[0:1, bass.ds(j, n)],
                                                                engines=(mybir.EngineType.DVE,),
                                                                min_val=0, max_val=E - 1)[1]
            tile(0, 0)
            tile(1, 1)
            hidden(0, 0)
            e = experts_of(0, 6)
            for j in range(6):
                tile(j + 2, j % 2)
                hidden(j + 1, (j + 1) % 2)
                result(j, j % 2, e[j], j // 2)
            with dve.Fori(0, (NT - 8) // 8) as i:
                e = experts_of(8 * i + 6, 8)
                for h in range(8):
                    tile(8 * i + (h + 8), h % 2)
                    hidden(8 * i + (h + 7), (h + 1) % 2)
                    result(8 * i + (h + 6), h % 2, e[h], 4 * i + (h + 6) // 2)
            hidden(NT - 1, (NT - 1) % 2)
            e = experts_of(NT - 2, 2)
            for h in range(2):
                result(NT - 2 + h, h, e[h], (NT - 2) // 2)

            sums = [0]

            def then(ins):
                sums[0] += 1
                ins.then_inc(s_add, 1)
                dve.wait_ge(s_add, sums[0])

            def combine(n):
                i = n % 2
                q = x[:, 4 * n:4 * n + 4, :]
                dve.wait_ge(s_got[i], 16 * QUAD * top * (n // 2 + 1))
                for t in range(top):
                    for b in range(QUAD):
                        sofar = x[:, 4 * n + b, :] if t == 0 else got[i][:, b, 0, :]
                        to = got[i][:, b, 0, :] if t < top - 1 or normed else x[:, 4 * n + b, :]
                        ins = nc.vector.scalar_tensor_tensor(out=to, in0=got[i][:, b, t, :],
                                                             scalar=gate[:, 4 * n + b, t:t + 1], in1=sofar,
                                                             op0=ALU.mult, op1=ALU.add)
                    then(ins)
                if normed:
                    then(nc.vector.tensor_tensor(q, q, got[i][:, :, 0, :], ALU.add))
                for b in range(QUAD):
                    ins = nc.vector.bn_stats(stats[i][:, b, :], x[:, 4 * n + b, :])
                then(ins)
                for b in range(QUAD):
                    ins = nc.vector.bn_aggr(mv[i][:, b, :], stats[i][:, b, :])
                ins.then_inc(s_mv2, 1)

            def finish(n):
                i = n % 2
                dve.wait_ge(s_r2, 2 * n + 2)
                late(dve, s_st, n, 2, 16)
                for b in range(QUAD):
                    ins = nc.vector.tensor_scalar(out[i][:, b, :], x[:, 4 * n + b, :], mv[i][:, b, 0:1],
                                                  rstd[i][:, b:b + 1], ALU.subtract, ALU.mult)
                ins.then_inc(s_out, 1)
            for n in range(NQUAD + 1):
                if n < NQUAD:
                    late(dve, s_out, n, 2)
                    combine(n)
                if n:
                    finish(n - 1)
    release_semaphores(nc, sems)


def position_attention_pass(nc, tag, src, dst, k):
    scale = float(D) ** -0.5
    TG = 4
    NG = S // (4 * TG)
    sems = []
    with ExitStack() as ctx:
        def sb(name, shape, dt):
            return ctx.enter_context(nc.sbuf_tensor(f"{tag}_{name}", shape, dt))

        def sem(name):
            sems.append(nc.alloc_semaphore(f"{tag}_{name}"))
            return sems[-1]

        def two(name, shape, dt=F32):
            return [sb(f"{name}{i}", shape, dt) for i in range(2)]
        ident, identb, blocks = sb("ident", [P, P], F32), sb("identb", [P, P], BF16), sb("blocks", [P, TG * P], BF16)
        expo = sb("expo", [P, TG], F32)
        x, out = sb("x", [P, NG, TG, D], F32), sb("out", [P, NG, TG, D], F32)
        xT, p, pT = two("xT", [P, TG * P]), two("p", [P, TG * P]), two("pt", [P, TG * P])
        top, bias, total, recip = (two(n, [P, TG]) for n in ("top", "bias", "total", "recip"))
        y, stats, mv = two("y", [P, TG, D]), two("stats", [P, TG, 6]), two("mv", [P, TG, 2])
        veps, rstd = two("veps", [P, TG]), two("rstd", [P, TG])
        xTp, sc, pTp, yp = [[ctx.enter_context(nc.psum_tensor(f"{tag}_{n}{i}", [P, 512], F32)) for i in range(2)]
                            for n in ("xTp", "sc", "pTp", "yp")]
        s_c, s_T, s_Ts, s_S, s_b, s_e, s_P, s_Ps, s_Y, s_y, s_mv, s_r, s_o, s_st, s_k = (
            sem(n) for n in ("const", "turned", "turned_sb", "scores", "bias", "exp", "p_turned", "p_turned_sb",
                             "out_ps", "summed", "variance", "rstd", "normed", "stored", "step"))
        s_x = [sem(f"x_in{n}") for n in range(NG)]
        block = ctx.enter_context(nc.Block())

        def late(eng, s, n, back):
            if n >= back:
                eng.wait_ge(s, n - back + 1)

        def skewed(stages):
            for n in range(NG + max(lag for lag, _ in stages)):
                for lag, f in stages:
                    if 0 <= n - lag < NG:
                        f(n - lag, (n - lag) % 2)

        @block.sync
        def _(sp):
            for to, frm in ((ident[:], k["ident"]), (identb[:], k["ident4"][:, 0:P]), (blocks[:], k["blocks"]),
                            (expo[:], k["expo4"])):
                sp.dma_start(to, frm).then_inc(s_c, 16)
            for n in range(NG):
                for a in range(4):
                    sp.dma_start(x[32 * a:32 * a + 32, n], src[:, 4 * (4 * n + a):4 * (4 * n + a) + TG, :])\
                      .then_inc(s_x[n], 16)
            for n in range(NG):
                sp.wait_ge(s_o, n + 1)
                for a in range(4):
                    sp.dma_start(dst[:, 4 * (4 * n + a):4 * (4 * n + a) + TG, :], out[32 * a:32 * a + 32, n])\
                      .then_inc(s_st, 16)
            sp.wait_ge(s_st, 64 * NG)

        @block.tensor
        def _(pe):
            pe.wait_ge(s_c, 64)
            tile = lambda t: slice(t * P, (t + 1) * P)

            def turn(n, i):
                pe.wait_ge(s_x[n], 64)
                late(pe, s_Ts, n, 2)
                for t in range(TG):
                    mm = nc.tensor.transpose(xTp[i][:, tile(t)], x[:, n, t, :], ident[:])
                mm.then_inc(s_T, 1)

            def score(n, i):
                pe.wait_ge(s_Ts, n + 1)
                late(pe, s_e, n, 2)
                nc.tensor.matmul(sc[i][:], identb[:], blocks[:], start=True, stop=False, skip_group_check=True)
                for t in range(TG):
                    mm = nc.tensor.matmul(sc[i][:, tile(t)], xT[i][:, tile(t)], xT[i][:, tile(t)], start=False,
                                          stop=True, skip_group_check=True)
                mm.then_inc(s_S, 1)

            def turn_p(n, i):
                pe.wait_ge(s_e, n + 1)
                late(pe, s_Ps, n, 2)
                for t in range(TG):
                    mm = nc.tensor.transpose(pTp[i][:, tile(t)], p[i][:, tile(t)], ident[:])
                mm.then_inc(s_P, 1)

            def attend(n, i):
                pe.wait_ge(s_Ps, n + 1)
                late(pe, s_y, n, 2)
                for t in range(TG):
                    mm = nc.tensor.matmul(yp[i][:, tile(t)], pT[i][:, tile(t)], x[:, n, t, :], start=True, stop=True)
                mm.then_inc(s_Y, 1)
            skewed([(0, turn), (1, score), (2, turn_p), (3, attend)])

        @block.scalar
        def _(act):
            def turned(n, i):
                act.wait_ge(s_T, n + 1)
                late(act, s_S, n, 2)
                nc.scalar.copy(xT[i][:], xTp[i][:]).then_inc(s_Ts, 1)

            def exp(n, i):
                act.wait_ge(s_b, n + 1)
                late(act, s_P, n, 2)
                late(act, s_y, n, 2)
                for t in range(TG):
                    c = slice(t * P, (t + 1) * P)
                    ins = nc.scalar.activation(p[i][:, c], sc[i][:, c], ACT.Exp, scale=scale, bias=bias[i][:, t:t + 1],
                                               accum_out=total[i][:, t:t + 1])
                ins.then_inc(s_e, 1)

            def p_turned(n, i):
                act.wait_ge(s_P, n + 1)
                late(act, s_Y, n, 2)
                nc.scalar.copy(pT[i][:], pTp[i][:]).then_inc(s_Ps, 1)
            skewed([(0, turned), (1, exp), (2, p_turned)])

        @block.gpsimd
        def _(pool):
            pool.wait_ge(s_c, 64)
            for n in range(NG):
                i = n % 2
                pool.wait_ge(s_mv, n + 1)
                late(pool, s_o, n, 2)
                nc.gpsimd.tensor_scalar(veps[i][:], mv[i][:, :, 1], LN_EPS, None, ALU.add).then_inc(s_r, 1)
                pool.wait_ge(s_r, 2 * n + 1)
                nc.gpsimd.tensor_tensor(rstd[i][:], veps[i][:], expo[:], ALU.pow).then_inc(s_r, 1)

        @block.vector
        def _(dve):
            steps = [0]

            def link(ins):
                steps[0] += 1
                ins.then_inc(s_k, 1)
                dve.wait_ge(s_k, steps[0])

            def peak(n, i):
                dve.wait_ge(s_S, n + 1)
                late(dve, s_e, n, 2)
                link(nc.vector.tensor_reduce(top[i][:], sc[i][:].rearrange("p (t c) -> p t c", t=TG), AX.X, ALU.max))
                nc.vector.tensor_scalar(bias[i][:], top[i][:], -scale, None, ALU.mult).then_inc(s_b, 1)

            def add(n, i):
                dve.wait_ge(s_Y, n + 1)
                late(dve, s_o, n, 2)
                link(nc.vector.reciprocal(recip[i][:], total[i][:]))
                for t in range(TG):
                    ins = nc.vector.scalar_tensor_tensor(out=y[i][:, t, :], in0=yp[i][:, t * D:(t + 1) * D],
                                                         scalar=recip[i][:, t:t + 1], in1=x[:, n, t, :],
                                                         op0=ALU.mult, op1=ALU.add)
                ins.then_inc(s_y, 1)
                dve.wait_ge(s_y, n + 1)
                for t in range(TG):
                    ins = nc.vector.bn_stats(stats[i][:, t, :], y[i][:, t, :])
                link(ins)
                for t in range(TG):
                    ins = nc.vector.bn_aggr(mv[i][:, t, :], stats[i][:, t, :])
                ins.then_inc(s_mv, 1)

            def norm(n, i):
                dve.wait_ge(s_r, 2 * n + 2)
                for t in range(TG):
                    ins = nc.vector.tensor_scalar(out[:, n, t, :], y[i][:, t, :], mv[i][:, t, 0:1],
                                                  rstd[i][:, t:t + 1], ALU.subtract, ALU.mult)
                ins.then_inc(s_o, 1)
            skewed([(0, peak), (2, add), (3, norm)])
    release_semaphores(nc, sems)


def decoder_kernel(nc, out, **a):
    k = {n[2:]: v for n, v in a.items() if n.startswith("c_")}

    def group(tag):
        return {n[len(tag):]: v for n, v in a.items() if n.startswith(tag)}

    def rows(name, shape=(B, S, D)):
        return nc.dram_tensor(name, shape, F32, kind="Internal").ap()
    x1, x2, x3, x4, x5 = (rows(f"after{i}") for i in range(1, 6))
    slots0, results0 = rows("slots0", (TILES0 * P, D)), rows("results0", (TILES0 * P, D))
    slots1, results1 = rows("slots1", (E1 * CAP1, D)), rows("results1", (E1 * CAP1, D))
    cross = float(8) ** -0.5

    attention_pass(nc, "own", a["x"], x1, group("own_"), k | {"sel": k["sel_own"]}, scale=0.125)
    attention_pass(nc, "cross0", x1, x2, group("cross0_"), k | {"sel": k["sel_cross"]}, ctx_src=a["ctx"],
                   mask_src=a["mask"], scale=cross)
    mixture_pass(nc, "mix0", x2, x3, group("mix0_"), k, slots0, results0, E0, 2, TILES0, P, normed=True)
    position_attention_pass(nc, "position", x3, x4, k)
    attention_pass(nc, "cross1", x4, x5, group("cross1_"), k | {"sel": k["sel_cross"]}, ctx_src=a["ctx"], scale=cross)
    mixture_pass(nc, "mix1", x5, out, group("mix1_"), k, slots1, results1, E1, 1, E1, CAP1, cap=CAP1)



def constants():
    import numpy as np
    bf = mybir.dt.np(BF16)
    c = {"ident": np.eye(P, dtype=np.float32), "ident4": np.tile(np.eye(P, dtype=bf), (1, QUAD))}
    c["causal4"] = np.tile(np.triu(np.full((P, P), -1e30, np.float32), 1), (1, QUAD)).astype(bf)
    dh = 64
    theta = np.float32(10000.0) ** (np.arange(0, dh, 2, dtype=np.float32) / np.float32(dh))
    freqs = np.arange(S, dtype=np.float32)[:, None] * (np.float32(1.0) / theta)[None, :]
    emb = np.concatenate([freqs, freqs], axis=-1)
    sign = np.where(np.arange(dh) % 2 == 0, np.float32(-1), np.float32(1))
    c["cos"] = np.ascontiguousarray(np.tile(np.cos(emb).T.astype(np.float32), (2, QUAD)))
    c["sin"] = np.ascontiguousarray(np.tile((np.sin(emb) * sign).T.astype(np.float32), (2, QUAD)))
    own = np.zeros((P, 2, HU, P), np.float32)
    cross = np.zeros((P, 1, HU, P), np.float32)
    for u in range(UNITS):
        for part in range(NSPLIT):
            for j in range(HU):
                own[32 * u + HU * part + j, u % 2, j, :] = 1
                cross[32 * u + HU * part + j, 0, j, :] = 1
    c["sel_own"], c["sel_cross"] = own.astype(bf), cross.astype(bf)
    low = np.zeros((P, 2), np.float32)
    for u in range(UNITS):
        low[32 * u + 16:32 * u + 24, 0] = 1
        low[32 * u + 8:32 * u + 16, 1] = 1
    c["low_rows"] = low
    c["expo"] = np.full((P, 2), -0.5, np.float32)
    c["expo4"] = np.full((P, QUAD), -0.5, np.float32)
    c["below"] = np.triu(np.ones((P, P), np.float32), 1).astype(bf)
    c["ones"] = np.ones((P, P), bf)
    c["onesf"] = np.ones((1, P), np.float32)
    c["iota"] = np.tile(np.arange(16, dtype=np.float32), (P, 1))
    c["steps"] = np.tile(np.arange(B, dtype=np.float32) * P, (P, 1))
    c["tile_no"] = np.tile(np.arange(TILES0, dtype=np.float32), (P, 1))
    at = np.arange(P) // B
    c["blocks"] = np.tile(np.where(at[:, None] == at[None, :], np.float32(0), np.float32(-1e30)).astype(bf), (1, 4))
    return c


def rows_own(t):
    import numpy as np
    out = np.zeros((P, 8) + t.shape[1:], t.dtype)
    for h in range(H):
        g, j = divmod(h, HU)
        out[64 * (g % 2):64 * (g % 2) + 64, 4 * (g // 2) + j] = t[64 * h:64 * h + 64]
    return out


def rows_cross(t):
    import numpy as np
    out = np.zeros((P, 4) + t.shape[1:], t.dtype)
    for h in range(H):
        g, j = divmod(h, HU)
        for r in range(3):
            out[32 * g + 8 * r:32 * g + 8 * r + 8, j] = t[8 * h:8 * h + 8]
    return out


def swap_pairs(t):
    import numpy as np
    return np.ascontiguousarray(t.reshape((-1, 2) + t.shape[1:])[:, ::-1].reshape(t.shape))


def attention_layout(own, wq, bq, wk, bk, wv, bv, wo, bo):
    import numpy as np
    rows = rows_own if own else rows_cross
    cols = lambda t: np.ascontiguousarray(rows(t).transpose(2, 1, 0).reshape(P, -1))
    no = wo.shape[1] // P
    r = {"q": cols(wq), "k": cols(wk), "v": np.ascontiguousarray(wv.T),
         "o": np.ascontiguousarray(wo.T.reshape(no, P, D).transpose(1, 0, 2).reshape(P, no * D)),
         "vbias": np.ascontiguousarray(bv.reshape(no, P).T), "obias": bo}
    b = [rows(t) for t in ((bq, swap_pairs(bq), bk, swap_pairs(bk)) if own else (bq, bk))]
    r["bias"] = np.ascontiguousarray(np.stack(b, axis=1))
    if own:
        r["qs"], r["ks"] = cols(swap_pairs(wq)), cols(swap_pairs(wk))
    return r


def mixture_layout(w1, b1, w2, b2):
    import numpy as np
    e = w1.shape[0]
    return {"w1": np.ascontiguousarray(w1.transpose(1, 0, 2).reshape(P, e * F)),
            "w2": np.ascontiguousarray(w2.reshape(e, F // P, P, D).transpose(2, 0, 1, 3).reshape(P, -1)),
            "b1": np.ascontiguousarray(b1.reshape(P, -1)), "b2": np.ascontiguousarray(b2.reshape(1, -1)),
            "b1c": np.ascontiguousarray(b1.reshape(e, F // P, P).transpose(2, 0, 1).reshape(P, -1))}


def lay_out(inputs):
    import numpy as np
    f = {n: np.asarray(v) for n, v in inputs.items()}
    t = lambda v: np.ascontiguousarray(v.T)
    get = lambda tag, names: [f[f"{tag}_{n}"] for n in names]
    own = attention_layout(True, *get("L0_attn", ("wq", "bq", "wk", "bk", "wv", "bv", "wo", "bo")))
    cross0 = attention_layout(False, *[t(v) if v.ndim == 2 else v for v in
                                       get("L0_xattn", ("Wq", "bq", "Wk", "bk", "Wv", "bv", "Wo", "bo"))])
    cross1 = attention_layout(False, *get("L1_xattn", ("wq", "bq", "wk", "bk", "wv", "bv", "wo", "bo")))
    mix0 = mixture_layout(*get("L0_ffn", ("W1", "b1", "W2", "b2")))
    mix1 = mixture_layout(*get("L1_ffn", ("W1", "b1", "W2", "b2")))
    del mix1["b1c"]
    mix0 |= {"wr": f["L0_ffn_Wr"], "br": f["L0_ffn_br"], "gamma": f["L0_ffn_gamma"], "beta": f["L0_ffn_beta"]}
    mix1 |= {"wr": f["L1_ffn_Wg"], "br": f["L1_ffn_bg"]}
    arrays = {"x": f["x"], "ctx": f["ctx_1024"], "mask": f["mask_BxSxS2_bf0"]}
    for tag, group in (("own", own), ("cross0", cross0), ("cross1", cross1), ("mix0", mix0), ("mix1", mix1),
                       ("c", constants())):
        arrays |= {f"{tag}_{n}": np.ascontiguousarray(v) for n, v in group.items()}
    return arrays


def kernel(**inputs):
    import numpy as np
    import concourse.bacc as bacc
    from concourse.bass_utils import run_bass_kernel_spmd

    nc = bacc.Bacc("TRN2", target_bir_lowering=False, num_devices=1)
    arrays = lay_out(inputs)
    args = {n: nc.dram_tensor(f"in_{n}", v.shape, mybir.dt.from_np(v.dtype), kind="ExternalInput").ap()
            for n, v in arrays.items()}
    out = nc.dram_tensor("out_0", (B, S, D), F32, kind="ExternalOutput").ap()
    decoder_kernel(nc, out, **args)
    r = run_bass_kernel_spmd(nc, [{f"in_{n}": v for n, v in arrays.items()}], core_ids=[0])
    return r.results[0]["out_0"]
```
